# Optimizing a Trainium2 kernel written in Bass

```python
import numpy as np
import jax
import jax.numpy as jnp

def _softmax(x, axis=-1):
    return jax.nn.softmax(x, axis=axis)

def _gelu(x):
    return jax.nn.gelu(x, approximate=True)

def _silu(x):
    return jax.nn.silu(x)

def _sigmoid(x):
    return jax.nn.sigmoid(x)

def _layernorm(x, axis=-1, eps=1e-05):
    m = jnp.mean(x, axis=axis, keepdims=True)
    v = jnp.var(x, axis=axis, keepdims=True)
    return (x - m) / jnp.sqrt(v + eps)

def _scatter_add(tgt, idx, src, axis=0):
    return tgt.at[idx].add(src)

def _segment_sum(src, seg, n):
    return jax.ops.segment_sum(src, seg, n)
kernel_name = 'mk_prb_d2_jaxref_r8_62faa0'

def setup_inputs(seed: int=0):
    np.random.seed(seed)
    _w = jnp.asarray

    def _L0_attn_setup():
        import jax, jax.numpy as jnp
        import numpy as np
        INF = 1000000000.0
        D = 128
        key = jax.random.key(seed)
        k_enc, k_r = jax.random.split(key)
        encoding = jax.random.normal(k_enc, (8, 256, D), dtype=jnp.float32)
        R = jax.random.normal(k_r, (D, D), dtype=jnp.float32) / D
        return {'encoding': encoding, 'R': R}
    _L0_attn_in = _L0_attn_setup()

    def _L0_ffn_setup():
        import jax, jax.numpy as jnp
        import numpy as np
        H = 128
        M = 64
        E = 16
        TOP_K = 2
        SCALE = 2.5
        NORM_TOPK = True
        B, S = (1, 128)

        def _moe(x, gate_w, w_gate, w_up, w_down, ws_gate, ws_up, ws_down):
            T = x.shape[0]
            shared = jax.nn.silu(x @ ws_gate) * (x @ ws_up) @ ws_down
            scores = jax.nn.sigmoid(x.astype(jnp.float32) @ gate_w.T.astype(jnp.float32))
            topk_w, topk_idx = jax.lax.top_k(scores, TOP_K)
            if NORM_TOPK and TOP_K > 1:
                topk_w = topk_w / (topk_w.sum(-1, keepdims=True) + 1e-20)
            topk_w = topk_w * SCALE
            route = jnp.zeros((T, E), topk_w.dtype).at[jnp.arange(T)[:, None], topk_idx].set(topk_w)
            g = jnp.einsum('th,ehm->etm', x, w_gate)
            u = jnp.einsum('th,ehm->etm', x, w_up)
            eo = jnp.einsum('etm,emh->eth', jax.nn.silu(g) * u, w_down)
            routed = jnp.einsum('te,eth->th', route.astype(x.dtype), eo)
            return routed + shared
        key = jax.random.key(seed)
        ks = jax.random.split(key, 8)
        std = 0.02
        return {'hidden_states': jax.random.normal(ks[0], (B, S, H), jnp.float32), 'gate_w': jax.random.normal(ks[1], (E, H), jnp.float32) * std, 'w_gate': jax.random.normal(ks[2], (E, H, M), jnp.float32) * std, 'w_up': jax.random.normal(ks[3], (E, H, M), jnp.float32) * std, 'w_down': jax.random.normal(ks[4], (E, M, H), jnp.float32) * std, 'ws_gate': jax.random.normal(ks[5], (H, M), jnp.float32) * std, 'ws_up': jax.random.normal(ks[6], (H, M), jnp.float32) * std, 'ws_down': jax.random.normal(ks[7], (M, H), jnp.float32) * std}
    _L0_ffn_in = _L0_ffn_setup()

    def _L1_attn_setup():
        import jax, jax.numpy as jnp
        import numpy as np
        HIDDEN = 128
        HEADS = 16
        HEAD = HIDDEN // HEADS

        def _ternary_weight(key, shape):
            g = jax.random.normal(key, shape, dtype=jnp.float32)
            return jnp.where(jnp.abs(g) < 0.6, 0.0, jnp.sign(g)).astype(jnp.float32)

        def _tlin(x, w, s, b):
            return jnp.einsum('bsh,oh->bso', x, w) * s + b
        key = jax.random.key(seed)
        ks = jax.random.split(key, 10)
        x = jax.random.normal(ks[0], (2, 256, HIDDEN), dtype=jnp.float32)
        d = {'x': x}
        names = ['q', 'k', 'v', 'o']
        for i, n in enumerate(names):
            d[f'w_{n}'] = _ternary_weight(ks[1 + i], (HIDDEN, HIDDEN))
            d[f's_{n}'] = jnp.float32(0.02)
            d[f'b_{n}'] = jax.random.normal(ks[5 + i], (HIDDEN,), dtype=jnp.float32) * 0.02
        return d
    _L1_attn_in = _L1_attn_setup()

    def _L1_ffn_setup():
        import jax, jax.numpy as jnp
        import numpy as np
        B, S, D = (2, 128, 128)
        L, H = (64, 16)
        HD = L // H
        F, E, K = (256, 8, 2)
        THETA = 10000.0
        EPS = 1e-05

        def _rmsnorm(x, g):
            return x * g * jax.lax.rsqrt(jnp.mean(x * x, axis=-1, keepdims=True) + EPS)

        def _rope(t, pos):
            inv_freq = 1.0 / THETA ** (jnp.arange(0, HD, 2, dtype=jnp.float32) / HD)
            ang = pos[:, None].astype(jnp.float32) * inv_freq[None, :]
            cos, sin = (jnp.cos(ang), jnp.sin(ang))
            t1, t2 = (t[..., 0::2], t[..., 1::2])
            r1 = t1 * cos - t2 * sin
            r2 = t1 * sin + t2 * cos
            return jnp.stack([r1, r2], axis=-1).reshape(t.shape)

        def _forward(x, g1, g2, w_down, wq, wk, wv, w_up, router_w, w1, w2, w3):
            b, s, _ = x.shape
            pos = jnp.arange(s)
            h = _rmsnorm(x, g1)
            c = h @ w_down
            split = lambda t: t.reshape(b, s, H, HD).transpose(0, 2, 1, 3)
            q = _rope(split(c @ wq), pos)
            k = _rope(split(c @ wk), pos)
            v = split(c @ wv)
            scores = jnp.einsum('bhqd,bhkd->bhqk', q, k) / jnp.sqrt(jnp.float32(HD))
            causal = jnp.tril(jnp.ones((s, s), bool))
            scores = jnp.where(causal, scores, -jnp.inf)
            attn = jax.nn.softmax(scores, axis=-1)
            o = jnp.einsum('bhqk,bhkd->bhqd', attn, v).transpose(0, 2, 1, 3).reshape(b, s, L)
            x = x + o @ w_up
            res = x
            t = _rmsnorm(x, g2).reshape(-1, D)
            probs = jax.nn.softmax(t @ router_w, axis=-1)
            vals, idx = jax.lax.top_k(probs, K)
            w = vals / jnp.sum(vals, axis=-1, keepdims=True)
            gate = jnp.sum(jax.nn.one_hot(idx, E, dtype=t.dtype) * w[..., None], axis=1)
            hid = jax.nn.silu(jnp.einsum('td,edf->tef', t, w1)) * jnp.einsum('td,edf->tef', t, w3)
            y_e = jnp.einsum('tef,efd->ted', hid, w2)
            y = jnp.einsum('ted,te->td', y_e, gate)
            return res + y.reshape(b, s, D)
        key = jax.random.key(seed)
        ks = jax.random.split(key, 12)
        g = lambda k, shape, scale: jax.random.normal(k, shape, dtype=jnp.float32) * scale
        return {'x': g(ks[0], (B, S, D), 1.0), 'g1': jnp.ones((D,), jnp.float32), 'g2': jnp.ones((D,), jnp.float32), 'w_down': g(ks[1], (D, L), 0.02), 'wq': g(ks[2], (L, L), 0.02), 'wk': g(ks[3], (L, L), 0.02), 'wv': g(ks[4], (L, L), 0.02), 'w_up': g(ks[5], (L, D), 0.02), 'router_w': g(ks[6], (D, E), 0.02), 'w1': g(ks[7], (E, D, F), 0.02), 'w3': g(ks[8], (E, D, F), 0.02), 'w2': g(ks[9], (E, F, D), 0.02)}
    _L1_ffn_in = _L1_ffn_setup()
    _d = {'L0_attn_encoding': _L0_attn_in['encoding'], 'L0_attn_R': _L0_attn_in['R'], 'L0_ffn_gate_w': _L0_ffn_in['gate_w'], 'L0_ffn_w_gate': _L0_ffn_in['w_gate'], 'L0_ffn_w_up': _L0_ffn_in['w_up'], 'L0_ffn_w_down': _L0_ffn_in['w_down'], 'L0_ffn_ws_gate': _L0_ffn_in['ws_gate'], 'L0_ffn_ws_up': _L0_ffn_in['ws_up'], 'L0_ffn_ws_down': _L0_ffn_in['ws_down'], 'L1_attn_w_q': _L1_attn_in['w_q'], 'L1_attn_s_q': _L1_attn_in['s_q'], 'L1_attn_b_q': _L1_attn_in['b_q'], 'L1_attn_w_k': _L1_attn_in['w_k'], 'L1_attn_s_k': _L1_attn_in['s_k'], 'L1_attn_b_k': _L1_attn_in['b_k'], 'L1_attn_w_v': _L1_attn_in['w_v'], 'L1_attn_s_v': _L1_attn_in['s_v'], 'L1_attn_b_v': _L1_attn_in['b_v'], 'L1_attn_w_o': _L1_attn_in['w_o'], 'L1_attn_s_o': _L1_attn_in['s_o'], 'L1_attn_b_o': _L1_attn_in['b_o'], 'L1_ffn_g1': _L1_ffn_in['g1'], 'L1_ffn_g2': _L1_ffn_in['g2'], 'L1_ffn_w_down': _L1_ffn_in['w_down'], 'L1_ffn_wq': _L1_ffn_in['wq'], 'L1_ffn_wk': _L1_ffn_in['wk'], 'L1_ffn_wv': _L1_ffn_in['wv'], 'L1_ffn_w_up': _L1_ffn_in['w_up'], 'L1_ffn_router_w': _L1_ffn_in['router_w'], 'L1_ffn_w1': _L1_ffn_in['w1'], 'L1_ffn_w2': _L1_ffn_in['w2'], 'L1_ffn_w3': _L1_ffn_in['w3']}
    _x0 = _d['L0_attn_encoding']
    _d['L0_attn_encoding'] = jax.random.normal(jax.random.fold_in(jax.random.key(seed), 1), (4, 1024, 128), dtype=_x0.dtype)
    del _x0
    return _d

def reference(L0_attn_encoding, L0_attn_R, L0_ffn_gate_w, L0_ffn_w_gate, L0_ffn_w_up, L0_ffn_w_down, L0_ffn_ws_gate, L0_ffn_ws_up, L0_ffn_ws_down, L1_attn_w_q, L1_attn_s_q, L1_attn_b_q, L1_attn_w_k, L1_attn_s_k, L1_attn_b_k, L1_attn_w_v, L1_attn_s_v, L1_attn_b_v, L1_attn_w_o, L1_attn_s_o, L1_attn_b_o, L1_ffn_g1, L1_ffn_g2, L1_ffn_w_down, L1_ffn_wq, L1_ffn_wk, L1_ffn_wv, L1_ffn_w_up, L1_ffn_router_w, L1_ffn_w1, L1_ffn_w2, L1_ffn_w3):

    def _L0_attn_ref(encoding, R):
        import jax, jax.numpy as jnp
        import numpy as np
        INF = 1000000000.0
        D = 128
        b, n, d = encoding.shape
        encR = jnp.einsum('bnd,de->bne', encoding, R)
        scores = jnp.einsum('bnd,bmd->bnm', encR, encoding)
        mask = jnp.where(jnp.tril(jnp.ones((n, n), dtype=bool)), 0.0, -INF).astype(scores.dtype)
        A = jax.nn.softmax(scores + mask, axis=2)
        return jnp.einsum('bnm,bmd->bnd', A, encoding)

    def _L0_ffn_ref(hidden_states, gate_w, w_gate, w_up, w_down, ws_gate, ws_up, ws_down):
        import jax, jax.numpy as jnp
        import numpy as np
        H = 128
        M = 64
        E = 16
        TOP_K = 2
        SCALE = 2.5
        NORM_TOPK = True
        B, S = (1, 128)

        def _moe(x, gate_w, w_gate, w_up, w_down, ws_gate, ws_up, ws_down):
            T = x.shape[0]
            shared = jax.nn.silu(x @ ws_gate) * (x @ ws_up) @ ws_down
            scores = jax.nn.sigmoid(x.astype(jnp.float32) @ gate_w.T.astype(jnp.float32))
            topk_w, topk_idx = jax.lax.top_k(scores, TOP_K)
            if NORM_TOPK and TOP_K > 1:
                topk_w = topk_w / (topk_w.sum(-1, keepdims=True) + 1e-20)
            topk_w = topk_w * SCALE
            route = jnp.zeros((T, E), topk_w.dtype).at[jnp.arange(T)[:, None], topk_idx].set(topk_w)
            g = jnp.einsum('th,ehm->etm', x, w_gate)
            u = jnp.einsum('th,ehm->etm', x, w_up)
            eo = jnp.einsum('etm,emh->eth', jax.nn.silu(g) * u, w_down)
            routed = jnp.einsum('te,eth->th', route.astype(x.dtype), eo)
            return routed + shared
        b, s, h = hidden_states.shape
        x = hidden_states.reshape(-1, h)
        out = _moe(x, gate_w, w_gate, w_up, w_down, ws_gate, ws_up, ws_down)
        return out.reshape(b, s, h)

    def _L1_attn_ref(x, w_q, s_q, b_q, w_k, s_k, b_k, w_v, s_v, b_v, w_o, s_o, b_o):
        import jax, jax.numpy as jnp
        import numpy as np
        HIDDEN = 128
        HEADS = 16
        HEAD = HIDDEN // HEADS

        def _ternary_weight(key, shape):
            g = jax.random.normal(key, shape, dtype=jnp.float32)
            return jnp.where(jnp.abs(g) < 0.6, 0.0, jnp.sign(g)).astype(jnp.float32)

        def _tlin(x, w, s, b):
            return jnp.einsum('bsh,oh->bso', x, w) * s + b
        B, S, H = x.shape

        def split_heads(t):
            return t.reshape(B, S, HEADS, HEAD).transpose(0, 2, 1, 3)
        q = split_heads(_tlin(x, w_q, s_q, b_q))
        k = split_heads(_tlin(x, w_k, s_k, b_k))
        v = split_heads(_tlin(x, w_v, s_v, b_v))
        scores = jnp.einsum('bhqd,bhkd->bhqk', q, k) / jnp.sqrt(jnp.float32(HEAD))
        attn = jax.nn.softmax(scores, axis=-1)
        ctx = jnp.einsum('bhqk,bhkd->bhqd', attn, v)
        ctx = ctx.transpose(0, 2, 1, 3).reshape(B, S, H)
        return _tlin(ctx, w_o, s_o, b_o)

    def _L1_ffn_ref(x, g1, g2, w_down, wq, wk, wv, w_up, router_w, w1, w2, w3):
        import jax, jax.numpy as jnp
        import numpy as np
        B, S, D = (2, 128, 128)
        L, H = (64, 16)
        HD = L // H
        F, E, K = (256, 8, 2)
        THETA = 10000.0
        EPS = 1e-05

        def _rmsnorm(x, g):
            return x * g * jax.lax.rsqrt(jnp.mean(x * x, axis=-1, keepdims=True) + EPS)

        def _rope(t, pos):
            inv_freq = 1.0 / THETA ** (jnp.arange(0, HD, 2, dtype=jnp.float32) / HD)
            ang = pos[:, None].astype(jnp.float32) * inv_freq[None, :]
            cos, sin = (jnp.cos(ang), jnp.sin(ang))
            t1, t2 = (t[..., 0::2], t[..., 1::2])
            r1 = t1 * cos - t2 * sin
            r2 = t1 * sin + t2 * cos
            return jnp.stack([r1, r2], axis=-1).reshape(t.shape)

        def _forward(x, g1, g2, w_down, wq, wk, wv, w_up, router_w, w1, w2, w3):
            b, s, _ = x.shape
            pos = jnp.arange(s)
            h = _rmsnorm(x, g1)
            c = h @ w_down
            split = lambda t: t.reshape(b, s, H, HD).transpose(0, 2, 1, 3)
            q = _rope(split(c @ wq), pos)
            k = _rope(split(c @ wk), pos)
            v = split(c @ wv)
            scores = jnp.einsum('bhqd,bhkd->bhqk', q, k) / jnp.sqrt(jnp.float32(HD))
            causal = jnp.tril(jnp.ones((s, s), bool))
            scores = jnp.where(causal, scores, -jnp.inf)
            attn = jax.nn.softmax(scores, axis=-1)
            o = jnp.einsum('bhqk,bhkd->bhqd', attn, v).transpose(0, 2, 1, 3).reshape(b, s, L)
            x = x + o @ w_up
            res = x
            t = _rmsnorm(x, g2).reshape(-1, D)
            probs = jax.nn.softmax(t @ router_w, axis=-1)
            vals, idx = jax.lax.top_k(probs, K)
            w = vals / jnp.sum(vals, axis=-1, keepdims=True)
            gate = jnp.sum(jax.nn.one_hot(idx, E, dtype=t.dtype) * w[..., None], axis=1)
            hid = jax.nn.silu(jnp.einsum('td,edf->tef', t, w1)) * jnp.einsum('td,edf->tef', t, w3)
            y_e = jnp.einsum('tef,efd->ted', hid, w2)
            y = jnp.einsum('ted,te->td', y_e, gate)
            return res + y.reshape(b, s, D)
        return _forward(x, g1, g2, w_down, wq, wk, wv, w_up, router_w, w1, w2, w3)
    x = L0_attn_encoding
    xn = _layernorm(x, axis=-1)
    x = x + _L0_attn_ref(xn, L0_attn_R) + _L0_ffn_ref(xn, L0_ffn_gate_w, L0_ffn_w_gate, L0_ffn_w_up, L0_ffn_w_down, L0_ffn_ws_gate, L0_ffn_ws_up, L0_ffn_ws_down)
    xn = _layernorm(x, axis=-1)
    x = x + _L1_attn_ref(xn, L1_attn_w_q, L1_attn_s_q, L1_attn_b_q, L1_attn_w_k, L1_attn_s_k, L1_attn_b_k, L1_attn_w_v, L1_attn_s_v, L1_attn_b_v, L1_attn_w_o, L1_attn_s_o, L1_attn_b_o) + _L1_ffn_ref(xn, L1_ffn_g1, L1_ffn_g2, L1_ffn_w_down, L1_ffn_wq, L1_ffn_wk, L1_ffn_wv, L1_ffn_w_up, L1_ffn_router_w, L1_ffn_w1, L1_ffn_w2, L1_ffn_w3)
    return x

_drawn_inputs = setup_inputs


def setup_inputs(seed=0):
    import zlib

    import numpy as np

    out = dict(_drawn_inputs(seed))
    spreads = {'L1_ffn_g1': (1.0, 0.6), 'L1_ffn_g2': (1.0, 0.6)}
    factors = {'L0_ffn_gate_w': 8.0,
     'L0_ffn_w_gate': 7.871,
     'L0_ffn_w_up': 7.852,
     'L0_ffn_w_down': 7.807,
     'L0_ffn_ws_gate': 8.0,
     'L0_ffn_ws_up': 8.0,
     'L0_ffn_ws_down': 8.0,
     'L1_attn_w_q': 8.0,
     'L1_attn_b_q': 64.0,
     'L1_attn_w_k': 8.0,
     'L1_attn_b_k': 64.0,
     'L1_attn_w_v': 8.0,
     'L1_attn_b_v': 24.811,
     'L1_attn_w_o': 8.0,
     'L1_attn_b_o': 29.312,
     'L1_ffn_w_down': 8.0,
     'L1_ffn_wq': 8.0,
     'L1_ffn_wk': 8.0,
     'L1_ffn_wv': 8.0,
     'L1_ffn_w_up': 8.0,
     'L1_ffn_router_w': 8.0,
     'L1_ffn_w1': 8.0,
     'L1_ffn_w2': 8.0,
     'L1_ffn_w3': 8.0}
    for name, (base, spread) in spreads.items():
        noise = np.random.default_rng([zlib.crc32(name.encode()), seed]).standard_normal(out[name].shape)
        drawn = base * np.exp(spread * noise) if base else spread * noise
        out[name] = jnp.asarray(drawn.astype(out[name].dtype))
    for name, factor in factors.items():
        out[name] = (out[name] * factor).astype(out[name].dtype)
    return out
```

```python
from contextlib import ExitStack

import numpy as np

import concourse.bass as bass
from concourse import mybir

F32 = mybir.dt.float32
BF16 = mybir.dt.bfloat16
ALU = mybir.AluOpType
ACT = mybir.ActivationFunctionType
AX_X = mybir.AxisListType.X

P = 128
B, S, D = 4, 1024, 128
T = S // P
HALF = 512
HEADS = 16
PARTS = 3
HD = 8
HF = HD + 1
ROWS = PARTS * PARTS * HF
GH = 4
GROUPS = HEADS // GH
GR = GH * PARTS * HF
CW = P // GH
OC = GH * HF
MR = GH * PARTS
E0, M0 = 16, 64
E1, M1 = 8, 256
L = 64
C0 = (E0 + 1) * M0 // P + 1
C1 = E1 * M1 // P
CHUNKS = C0 + C1
STEPS = 2 * CHUNKS
EPS = 1e-5
ROUTE_SCALE = 2.5
ROUTE_EPS = 1e-20
NEG = -1e30
THETA = 10000.0


def constants():
    i = np.arange(P)
    mask_q = np.where(i[None, :] <= i[:, None], 0.0, NEG)
    mask_k = mask_q.T
    sel0 = np.zeros((P, (E0 + 1) * M0))
    sel1 = np.zeros((P, E1 * P))
    for a in range(PARTS):
        for e in range(E0 + 1):
            sel0[CW * a + e, e * M0:(e + 1) * M0] = 1.0
        for e in range(E1):
            sel1[CW * a + e, e * P:(e + 1) * P] = 1.0
    pick_q = np.zeros((P, GH, PARTS, PARTS, HF))
    pick_k = np.zeros((P, GH, PARTS, PARTS, HF))
    for j in range(GH):
        for part in range(PARTS):
            for d in range(HF):
                row = (j * PARTS + part) * HF + d
                pick_q[row, j, part, :, d] = 1.0
                pick_k[row, j, :, part, d] = 1.0
    cb = np.concatenate([np.eye(P), mask_q, mask_k, pick_q.reshape(P, -1), pick_k.reshape(P, -1), sel0, sel1], axis=1)
    pick_o = np.zeros((P, GH, HF))
    for j in range(GH):
        pick_o[CW * j + np.arange(HF), j, np.arange(HF)] = 1.0
    pos = (np.arange(T)[None, :] * P + i[:, None]).astype(np.float32)
    inv = (np.float32(1.0) / np.float32(THETA) ** (np.arange(0, 4, 2, dtype=np.float32) / np.float32(4))).astype(np.float32)
    ang = (pos[:, :, None] * inv[None, None, :]).astype(np.float32)
    rev0 = np.tile(E0 - np.arange(E0), (P, 1))
    rev1 = np.tile(E1 - np.arange(E1), (P, 1))
    cf = np.concatenate([np.eye(P), pick_o.reshape(P, -1), np.cos(ang).reshape(P, -1), np.sin(ang).reshape(P, -1), rev0, rev1], axis=1)
    return cb, np.ascontiguousarray(cf.astype(np.float32))


class Steps:

    def __init__(self, eng, sem, base):
        self.eng, self.sem, self.base, self.n = eng, sem, base, 0

    def done(self, ins):
        ins.then_inc(self.sem, 1)
        self.n += 1

    def wait(self):
        self.eng.wait_ge(self.sem, self.base + self.n)


def build(nc, h):
    with ExitStack() as ctx:
        def sb(name, cols, dt=F32):
            return ctx.enter_context(nc.sbuf_tensor(name, [P, cols], dt))

        def sem(name):
            return ctx.enter_context(nc.semaphore(name))

        cb_cols, cf_cols = h["const_b"].shape[1], h["const_f"].shape[1]
        const_b = sb("const_b", cb_cols, BF16)
        const_f = sb("const_f", cf_cols)
        ident_b, mask_q, mask_k = (const_b[:, k * P:(k + 1) * P] for k in range(3))
        pick_q = const_b[:, 3 * P:3 * P + GH * ROWS]
        pick_k = const_b[:, 3 * P + GH * ROWS:3 * P + 2 * GH * ROWS]
        sel0 = const_b[:, 3 * P + 2 * GH * ROWS:3 * P + 2 * GH * ROWS + (E0 + 1) * M0]
        sel1 = const_b[:, 3 * P + 2 * GH * ROWS + (E0 + 1) * M0:]
        ident_f = const_f[:, 0:P]
        pick_o = const_f[:, P:P + OC]
        cos = const_f[:, P + OC:P + OC + 2 * T].rearrange("p (t f) -> p t f", f=2)
        sin = const_f[:, P + OC + 2 * T:P + OC + 4 * T].rearrange("p (t f) -> p t f", f=2)
        rev0 = const_f[:, P + OC + 4 * T:P + OC + 4 * T + E0]
        rev1 = const_f[:, P + OC + 4 * T + E0:]
        R_w = sb("R_w", D)
        gate0 = sb("gate0", E0)
        wg0 = sb("wg0", (E0 + 1) * M0)
        wu0 = sb("wu0", (E0 + 1) * M0)
        wd0 = sb("wd0", C0 * D)
        wqkv = sb("wqkv", 3 * D)
        wo = sb("wo", D)
        scale4 = sb("scale4", 4)
        bias4 = sb("bias4", 4 * D)
        g1 = sb("g1", 1)
        g2 = sb("g2", D)
        w_down = sb("w_down", L)
        wqkv1 = sb("wqkv1", 3 * L)
        w_up = sb("w_up", D)
        router = sb("router", E1)
        wg1 = sb("wg1", E1 * M1)
        wu1 = sb("wu1", E1 * M1)
        wd1 = sb("wd1", C1 * D)
        x_b = sb("x_b", S)
        xn = sb("xn", S)
        xnT = sb("xnT", S)
        x1 = sb("x1", S)
        res = sb("res", S)
        qkv = sb("qkv", 3 * S)
        buf = sb("buf", T * S)
        q_parts = sb("q_parts", T * HEADS * PARTS * HF, BF16)
        k_parts = sb("k_parts", T * HEADS * PARTS * HF, BF16)
        qT = sb("qT", HEADS * S, BF16)
        kT = sb("kT", HEADS * S, BF16)
        v_ones = sb("v_ones", T * GH * CW)
        o_sb = sb("o_sb", S)
        stats = sb("stats", T * 6)
        mv = sb("mv", T * 3)
        var = sb("var", T)
        rstd = sb("rstd", T)
        small = sb("small", 6 * T * E0)
        tops = sb("tops", 8 * T)
        nmax = sb("nmax", 2 * T * GH)
        m_rest = sb("m_rest", T * GH)
        m_parts = sb("m_parts", T * MR, BF16)
        rsum_g = sb("rsum_g", T * GH)
        nmax0 = sb("nmax0", T)
        sum0 = sb("sum0", T)
        rsum = sb("rsum", T)
        routes = sb("routes", T * PARTS * CW, BF16)

        slot = lambda n: buf[:, n * S:(n + 1) * S]
        p0 = [slot(0), slot(1)]
        pT0 = slot(2)
        encR = slot(3)
        sg = [slot(4)[:, 0:HALF], slot(4)[:, HALF:]]
        gu = [slot(5)[:, 0:HALF], slot(5)[:, HALF:]]
        hid = [slot(6)[:, 0:HALF], slot(6)[:, HALF:]]
        yT = slot(7)
        routeT = slot(3)[:, 0:HALF].bitcast(BF16)
        rest = slot(0)
        spin_a, spin_b = slot(1), slot(2)
        q_groups = buf[:, 4 * S:6 * S].bitcast(BF16)
        k_groups = buf[:, 6 * S:8 * S].bitcast(BF16)
        q_tok, k_tok, v_tok = (qkv[:, n * S:(n + 1) * S] for n in range(3))
        heads_out, heads_outT = q_tok, k_tok
        mT = heads_outT[:, 0:HALF].bitcast(BF16)
        qp = q_parts[:].rearrange("p (n a d) -> p n a d", a=PARTS, d=HF)
        kp = k_parts[:].rearrange("p (n a d) -> p n a d", a=PARTS, d=HF)
        v_st = v_ones[:].rearrange("p (k j c) -> p k j c", j=GH, c=CW)
        mp = m_parts[:].rearrange("p (t a j) -> p t a j", a=PARTS, j=GH)
        rt = routes[:].rearrange("p (t a e) -> p t a e", a=PARTS, e=CW)

        ps = [ctx.enter_context(nc.psum_tensor(f"ps{n}", [P, S], F32)) for n in range(4)]

        names = """weights_in x_in out_stored setup_done var_ready std_ready tok_ready tokT_psum tokT_ready
        encr_psum encr_ready s0_psum max0_ready p0_ready pt_psum pt_ready o0_psum o0_used
        logit_psum shift1_ready e_ready route_ready rt_psum rt_ready gu_psum sg_ready gu_ready hid_ready down_done
        y_ready ytok_psum x1_ready qkv_psum qkv_used ct_psum ct_ready parts_ready qg_psum qg_ready kg_psum kg_ready
        qT_psum qT_ready kT_psum kT_ready
        s_psum max_done m_steps m_split mt_psum mt_ready m_stored m_rows st_psum st_psum_causal p_ready p_ready_causal pv_done o_evac ot_psum
        norm_done v_staged proj_psum dve_steps rsum_done""".split()
        s = {n: sem(n) for n in names}
        block = ctx.enter_context(nc.Block())

        N_WEIGHTS = 21
        LOADED = 16 * N_WEIGHTS
        CREDIT = 2
        DVE_STEPS = 148
        M_STEPS = 5

        PIECES = [[(j, t, half, lo, min(lo + HALF, (t + 1) * P if causal else S))
                   for j in range(GH) for t in range(T) for half, lo in enumerate(range(0, (t + 1) * P if causal else S, HALF))]
                  for causal in (False, True)]
        UNITS = [[(kc, j, max(kc * P, half * HALF) if causal else half * HALF, (half + 1) * HALF)
                  for kc in range(T) for j in range(GH) for half in range(2) if not (causal and kc * P >= (half + 1) * HALF)]
                 for causal in (False, True)]
        NP, NU = [len(p) for p in PIECES], [len(u) for u in UNITS]
        PIECES_END = [54, 36]
        UNIT_BANKS, PIECE_BANKS = (0, 1, 2), (3, 6, 7)
        GATHER_BANK = PIECE_BANKS[0]

        def bank(n):
            return ps[n // 2][:, n % 2 * HALF:(n % 2 + 1) * HALF]

        def unit_bank(i):
            return bank(UNIT_BANKS[i % 3])

        def piece_bank(i):
            return bank(PIECE_BANKS[(i + 1) % 3])

        ST_PSUM, P_READY = ("st_psum", "st_psum_causal"), ("p_ready", "p_ready_causal")

        def pieces_before(b, kind, g):
            return b * GROUPS * sum(NP) + kind * GROUPS * NP[0] + g * NP[kind]

        @block.sync
        def _(sp):
            loads = [(const_b[:], h["const_b"]), (const_f[:], h["const_f"]), (R_w[:], h["R"]), (gate0[:], h["gate0"]),
                     (wg0[:], h["wg0"]), (wu0[:], h["wu0"]), (wd0[:, 0:(C0 - 1) * D], h["wd0a"]), (wd0[0:M0, (C0 - 1) * D:], h["wd0b"]),
                     (wqkv[:], h["wqkv"]), (wo[:], h["wo"]), (scale4[:], h["scale4"].partition_broadcast(P)),
                     (bias4[:], h["bias4"].partition_broadcast(P)), (g1[:], h["g1"]), (g2[:], h["g2"].partition_broadcast(P)),
                     (w_down[:], h["w_down"]), (wqkv1[0:L, :], h["wqkv1"]), (w_up[0:L, :], h["w_up"]), (router[:], h["router"]),
                     (wg1[:], h["wg1"]), (wu1[:], h["wu1"]), (wd1[:], h["wd1"])]
            x_view = h["x"].rearrange("b (t p) d -> b p t d", p=P)
            out_view = h["out"].rearrange("b (t p) d -> b p t d", p=P)
            sp.dma_start(x_b[:].rearrange("p (t d) -> p t d", d=D), x_view[0]).then_inc(s["x_in"], 16)
            assert len(loads) == N_WEIGHTS
            for dst, src in loads:
                sp.dma_start(dst, src).then_inc(s["weights_in"], 16)
            def store(b):
                sp.wait_ge(s["x1_ready"], 2 * b + 2)
                sp.dma_start(out_view[bass.ds(b, 1)].rearrange("b p t d -> (b p) t d"),
                             res[:].rearrange("p (t d) -> p t d", d=D)).then_inc(s["out_stored"], 16)

            def max_rows(b):
                for kind in range(2):
                    a = 2 * b + kind
                    with sp.Fori(0, GROUPS) as g:
                        sp.wait_ge(s["mt_ready"], a * GROUPS + g + 1)
                        sp.dma_start(h["m_rows"].rearrange("a j s -> (a j) s"), mT[0:MR, :]).then_inc(s["m_stored"], 16)
                        sp.wait_ge(s["m_stored"], 16 * (a * GROUPS + g + 1))
                        for part in range(PARTS):
                            row = part * PARTS * HF + HD
                            sp.dma_start(qT[row:row + 1, bass.ds(g * GH * S, GH * S)],
                                         h["m_rows"][part:part + 1].rearrange("a j s -> a (j s)")).then_inc(s["m_rows"], 16)

            with sp.Fori(0, B - 1) as b:
                sp.wait_ge(s["o0_used"], b * T + T)
                sp.dma_start(x_b[:].rearrange("p (t d) -> p t d", d=D),
                             x_view[bass.ds(b + 1, 1)].rearrange("b p t d -> (b p) t d")).then_inc(s["x_in"], 16)
                max_rows(b)
                store(b)
            max_rows(B - 1)
            store(B - 1)
            sp.wait_ge(s["out_stored"], 16 * B + 16)

        @block.gpsimd
        def _(pool):
            with pool.Fori(0, B) as b:
                for kind in range(2):
                    a = 2 * b + kind
                    with pool.Fori(0, GROUPS) as g:
                        pool.wait_ge(s["parts_ready"], a + 1)
                        pool.wait_ge(s["pv_done"], CREDIT + (a * GROUPS + g) * T)
                        pool.tensor_copy(v_st[:, :, :, 0:HD], v_tok.rearrange("p (t n) -> p t n", t=T)
                                         [:, :, bass.ds(g * GH * HD, GH * HD)].rearrange("p t (j c) -> p t j c", c=HD)).then_inc(s["v_staged"], 1)

        @block.vector
        def _(dve):
            dve.memset(v_ones[:], 0.0).then_inc(s["max_done"], CREDIT)
            dve.memset(routes[:], 0.0).then_inc(s["pv_done"], CREDIT)
            dve.memset(kp[:, :, 1:, HD:HF], 0.0).then_inc(s["norm_done"], CREDIT)
            dve.memset(kp[:, :, 0, HD:HF], 1.0).then_inc(s["kT_ready"], CREDIT)
            dve.memset(tops[:, 0:T], 0.0).then_inc(s["out_stored"], 16)
            dve.memset(tops[:, T:], 0.0).then_inc(s["qT_ready"], CREDIT)
            dve.memset(small[:], 0.0).then_inc(s["setup_done"], 1)
            dve.wait_ge(s["max_done"], CREDIT)
            dve.wait_ge(s["pv_done"], CREDIT)
            dve.memset(rt[:, :, 0, E0:E0 + 1], 1.0).then_inc(s["setup_done"], 1)
            dve.memset(v_st[:, :, :, HD:HF], 1.0).then_inc(s["setup_done"], 1)
            dve.wait_ge(s["weights_in"], LOADED)
            dve.tensor_scalar(w_down[:], w_down[:], g1[:, 0:1], None, ALU.mult).then_inc(s["setup_done"], 1)

            def tiles(ap):
                return ap.rearrange("p (t c) -> p t c", t=T)

            with dve.Fori(0, B) as b:
                st = Steps(dve, s["dve_steps"], b * DVE_STEPS)

                def statistics(src):
                    for t in range(T):
                        st.done(dve.bn_stats(stats[:, 6 * t:6 * t + 6], src[:, t * D:(t + 1) * D]))
                    st.wait()
                    even, odd = field[:, :, 1], field[:, :, 4]
                    st.done(dve.tensor_tensor(means, even, odd, ALU.add))
                    st.done(dve.tensor_tensor(apart, even, odd, ALU.subtract))
                    st.done(dve.tensor_tensor(variances, field[:, :, 2], field[:, :, 5], ALU.add))
                    st.wait()
                    st.done(dve.tensor_scalar(means, means, 0.5, None, ALU.mult))
                    st.done(dve.scalar_tensor_tensor(apart, apart, 0.25, apart, ALU.mult, ALU.mult))
                    st.wait()
                    st.done(dve.scalar_tensor_tensor(variances, variances, 1.0 / D, apart, ALU.mult, ALU.add))
                    st.wait()

                field = stats[:].rearrange("p (t k) -> p t k", k=6)
                means, variances, apart = (mv[:, n * T:(n + 1) * T] for n in range(3))

                def inverse_deviation(n):
                    dve.wait_ge(s["std_ready"], 4 * b + n + 1)
                    st.done(dve.reciprocal(rstd[:], var[:]))
                    st.wait()

                def layernorm(src, n):
                    statistics(src)
                    dve.tensor_scalar(var[:], variances, EPS, None, ALU.add).then_inc(s["var_ready"], 1)
                    inverse_deviation(n)
                    for t in range(T):
                        ins = dve.tensor_scalar(xn[:, t * D:(t + 1) * D], src[:, t * D:(t + 1) * D], means[:, t:t + 1],
                                                rstd[:, t:t + 1], ALU.subtract, ALU.mult)
                    ins.then_inc(s["tok_ready"], 1)

                def top2(score, experts, rev, scale, eps):
                    n = T * experts
                    view = lambda k: small[:, k * T * E0:k * T * E0 + n].rearrange("p (t e) -> p t e", e=experts)
                    eq, key, hot1, left = view(2), view(3), view(4), view(5)
                    col = lambda k: tops[:, k * T:(k + 1) * T]
                    wide = lambda c: c.unsqueeze(2).to_broadcast([P, T, experts])
                    order = rev.unsqueeze(1).to_broadcast([P, T, experts])

                    def best(src, value, hot):
                        st.done(dve.tensor_reduce(value, src, AX_X, ALU.max))
                        st.wait()
                        st.done(dve.tensor_tensor(eq, src, wide(value), ALU.is_equal))
                        st.wait()
                        st.done(dve.tensor_tensor(key, eq, order, ALU.mult))
                        st.wait()
                        st.done(dve.tensor_reduce(col(4), key, AX_X, ALU.max))
                        st.wait()
                        st.done(dve.tensor_tensor(hot, key, wide(col(4)), ALU.is_equal))
                        st.wait()

                    best(score, col(2), hot1)
                    st.done(dve.scalar_tensor_tensor(left, hot1, -4.0, score, ALU.mult, ALU.add))
                    st.wait()
                    best(left, col(3), eq)
                    st.done(dve.tensor_tensor(hot1, hot1, eq, ALU.add))
                    st.done(dve.scalar_tensor_tensor(col(5), col(2), eps, col(3), ALU.add, ALU.add))
                    st.wait()
                    st.done(dve.tensor_tensor(key, hot1, score, ALU.mult))
                    st.done(dve.reciprocal(col(6), col(5)))
                    st.wait()
                    st.done(dve.scalar_tensor_tensor(left, key, scale, wide(col(6)), ALU.mult, ALU.mult))
                    st.wait()
                    for part in range(PARTS):
                        dst = rt[:, :, part, 0:experts]
                        ins = dve.tensor_copy(dst, left)
                        if part == PARTS - 1:
                            ins.then_inc(s["route_ready"], 1)
                            break
                        st.done(ins)
                        st.wait()
                        st.done(dve.tensor_tensor(left, left, dst, ALU.subtract))
                        st.wait()

                def mixture(base, chunks, hid_rows):
                    for n in range(2 * chunks):
                        k = STEPS * b + base + n
                        m = hid_rows(n % chunks)
                        dve.wait_ge(s["sg_ready"], k + 1)
                        dve.tensor_tensor(gu[n % 2][0:m, :], sg[n % 2][0:m, :], ps[n % 2][0:m, HALF:], ALU.mult).then_inc(s["gu_ready"], 1)
                        if base + n >= 2:
                            dve.wait_ge(s["down_done"], k - 1)
                        dve.wait_ge(s["gu_ready"], k + 1)
                        dve.tensor_tensor(hid[n % 2][0:m, :], gu[n % 2][0:m, :], ps[3][0:m, (n % 2) * HALF:(n % 2 + 1) * HALF],
                                          ALU.mult).then_inc(s["hid_ready"], 1)

                def split(src_of, parts):
                    src, hd = src_of
                    r = rest[:, 0:HEADS * T * hd].rearrange("p (t n d) -> p t n d", t=T, d=hd)
                    to = lambda part: parts[:, :, part, 0:hd].rearrange("p (t n) d -> p t n d", t=T)
                    st.done(dve.tensor_copy(to(0), src))
                    st.wait()
                    st.done(dve.tensor_tensor(r, src, to(0), ALU.subtract))
                    st.wait()
                    st.done(dve.tensor_copy(to(1), r))
                    st.wait()
                    st.done(dve.tensor_tensor(r, r, to(1), ALU.subtract))
                    st.wait()
                    ins = dve.tensor_copy(to(2), r)
                    return ins

                def attention(kind, hd):
                    causal = kind == 1
                    a = 2 * b + kind
                    for g in range(GROUPS):
                        dve.wait_ge(s["kg_psum"], a * GROUPS + g + 1)
                        dve.tensor_copy(k_groups[0:GR, g * S:(g + 1) * S], ps[g][0:GR, HALF:].bitcast(BF16)).then_inc(s["kg_ready"], 1)
                    with dve.Fori(0, HEADS // 2) as hp:
                        for u in range(2):
                            n = a * HEADS + 2 * hp + u
                            dve.wait_ge(s["kT_psum"], n + 1)
                            dve.tensor_scalar(kT[0:ROWS, bass.ds((2 * hp + u) * S, S)], ps[2 * u + 1][0:ROWS, :], 1.0, None,
                                              ALU.mult).then_inc(s["kT_ready"], 1)
                    maxima(kind, 0)
                    maxima(kind, 1)
                    with dve.Fori(1, GROUPS - 1) as g:
                        outputs(a * GROUPS + g - 1, g - 1, hd)
                        maxima(kind, g + 1)
                    outputs(a * GROUPS + GROUPS - 2, GROUPS - 2, hd)
                    outputs(a * GROUPS + GROUPS - 1, GROUPS - 1, hd)
                    dve.wait_ge(s["norm_done"], CREDIT + (a + 1) * GROUPS)

                def maxima(kind, g):
                    G = (2 * b + kind) * GROUPS + g
                    first = pieces_before(b, kind, g)
                    nm = nmax[:].rearrange("p (h t j) -> p h t j", h=2, j=GH)
                    for i, (j, t, half, lo, hi) in enumerate(PIECES[kind]):
                        dve.wait_ge(s["s_psum"], first + i + 1)
                        dve.tensor_reduce(nm[:, half, t, j:j + 1], piece_bank(i)[:, 0:hi - lo],
                                          AX_X, ALU.max, negate=True).then_inc(s["max_done"], 1)
                    ms = Steps(dve, s["m_steps"], G * M_STEPS)
                    dve.wait_ge(s["max_done"], CREDIT + first + NP[kind])
                    m, r = nm[:, 0], m_rest[:].rearrange("p (t j) -> p t j", j=GH)
                    two = T // 2 if kind == 1 else 0
                    ms.done(dve.tensor_tensor(m[:, two:], m[:, two:], nm[:, 1, two:], ALU.min))
                    ms.wait()
                    ms.done(dve.tensor_copy(mp[:, :, 0], m))
                    ms.wait()
                    ms.done(dve.tensor_tensor(r, m, mp[:, :, 0], ALU.subtract))
                    ms.wait()
                    ms.done(dve.tensor_copy(mp[:, :, 1], r))
                    ms.wait()
                    ms.done(dve.tensor_tensor(r, r, mp[:, :, 1], ALU.subtract))
                    ms.wait()
                    assert ms.n == M_STEPS
                    dve.tensor_copy(mp[:, :, 2], r).then_inc(s["m_split"], 1)
                    dve.wait_ge(s["mt_psum"], G + 1)
                    dve.tensor_copy(mT[0:MR, :], piece_bank(NP[kind])[0:MR, :].bitcast(BF16)).then_inc(s["mt_ready"], 1)

                def outputs(G, g, hd):
                    dve.wait_ge(s["pv_done"], CREDIT + (G + 1) * T)
                    dve.tensor_copy(o_sb[:], ps[2][:]).then_inc(s["o_evac"], 1)
                    dve.wait_ge(s["ot_psum"], G + 1)
                    o = bank(GATHER_BANK)[:, 0:T * OC].rearrange("p (t j c) -> p t j c", j=GH, c=HF)
                    inv = rsum_g[:].rearrange("p (t j) -> p t j", j=GH)
                    dve.reciprocal(inv, o[:, :, :, HD]).then_inc(s["rsum_done"], 1)
                    dve.wait_ge(s["rsum_done"], G + 1)
                    dst = tiles(heads_out[:, 0:T * HEADS * hd])[:, :, bass.ds(g * GH * hd, GH * hd)].rearrange("p t (j d) -> p t j d", d=hd)
                    dve.tensor_tensor(dst, o[:, :, :, 0:hd], inv.unsqueeze(3).to_broadcast([P, T, GH, hd]), ALU.mult).then_inc(s["norm_done"], 1)

                dve.wait_ge(s["x_in"], 16 * b + 16)
                layernorm(x_b, 0)
                for t in range(T):
                    dve.wait_ge(s["s0_psum"], b * T + t + 1)
                    dve.tensor_reduce(nmax0[:, t:t + 1], ps[t % 2][:, 0:(t + 1) * P], AX_X, ALU.max, negate=True).then_inc(s["max0_ready"], 1)
                    dve.wait_ge(s["pt_psum"], b * T + t + 1)
                    if t >= 1:
                        dve.wait_ge(s["o0_psum"], b * T + t)
                    dve.tensor_copy(pT0[:, 0:(t + 1) * P], ps[2][:, 0:(t + 1) * P]).then_inc(s["pt_ready"], 1)
                    dve.wait_ge(s["p0_ready"], b * T + t + 1)
                    st.done(dve.reciprocal(rsum[:, t:t + 1], sum0[:, t:t + 1]))
                    st.wait()
                    dve.wait_ge(s["o0_psum"], b * T + t + 1)
                    dve.scalar_tensor_tensor(x1[:, t * D:(t + 1) * D], ps[3][:, (t % 2) * HALF:(t % 2) * HALF + D], rsum[:, t:t + 1],
                                             x_b[:, t * D:(t + 1) * D], ALU.mult, ALU.add).then_inc(s["o0_used"], 1)
                e0, score = small[:, 0:T * E0], small[:, T * E0:2 * T * E0]
                dve.wait_ge(s["e_ready"], 2 * b + 1)
                st.done(dve.tensor_scalar(e0, e0, 1.0, None, ALU.add))
                st.wait()
                st.done(dve.reciprocal(score, e0))
                st.wait()
                top2(score.rearrange("p (t e) -> p t e", e=E0), E0, rev0, ROUTE_SCALE, ROUTE_EPS)
                mixture(0, C0, lambda c: P if c < C0 - 1 else M0)
                dve.wait_ge(s["ytok_psum"], 2 * b + 1)
                dve.wait_ge(s["o0_used"], b * T + T)
                dve.tensor_tensor(x1[:], x1[:], ps[0][:], ALU.add).then_inc(s["x1_ready"], 1)
                dve.wait_ge(s["x1_ready"], 2 * b + 1)
                layernorm(x1, 1)
                st.done(dve.memset(qp[:, :, :, HD:HF], 0.0))
                for t in range(T):
                    dve.wait_ge(s["qkv_psum"], 2 * T * b + t + 1)
                    for n, dst in enumerate((q_tok, k_tok, v_tok)):
                        ins = dve.scalar_tensor_tensor(dst[:, t * D:(t + 1) * D], ps[t % 2][:, n * D:(n + 1) * D], scale4[:, n:n + 1],
                                                       bias4[:, n * D:(n + 1) * D], ALU.mult, ALU.add)
                    ins.then_inc(s["qkv_used"], 1)
                dve.wait_ge(s["qkv_used"], 2 * T * b + T)
                heads4 = lambda ap: ap.rearrange("p (t n d) -> p t n d", t=T, d=HD)
                st.done(split((heads4(q_tok), HD), qp))
                st.wait()
                split((heads4(k_tok), HD), kp).then_inc(s["parts_ready"], 1)
                attention(0, HD)
                dve.tensor_scalar(heads_outT[:, 0:1], heads_out[:, 0:1], 1.0, None, ALU.mult).then_inc(s["tok_ready"], 1)
                dve.wait_ge(s["proj_psum"], 2 * b + 1)
                st.done(dve.scalar_tensor_tensor(x1[:], ps[1][:], scale4[:, 3:4], x1[:], ALU.mult, ALU.add))
                st.wait()
                st.done(dve.tensor_tensor(tiles(x1[:]), tiles(x1[:]), bias4[:, 3 * D:4 * D].unsqueeze(1).to_broadcast([P, T, D]), ALU.add))
                def rms(src, n):
                    statistics(src)
                    st.done(dve.tensor_tensor(var[:], means, means, ALU.mult))
                    st.wait()
                    dve.scalar_tensor_tensor(var[:], var[:], EPS, variances, ALU.add, ALU.add).then_inc(s["var_ready"], 1)
                    inverse_deviation(n)

                rms(xn, 2)
                st.done(dve.memset(qp[:, :, :, 4:HF], 0.0))
                st.done(dve.memset(kp[:, :, :, 4:HD], 0.0))
                st.done(dve.memset(v_tok, 0.0))
                st.wait()
                for t in range(T):
                    dve.wait_ge(s["qkv_psum"], 2 * T * b + T + t + 1)
                    dve.tensor_scalar(q_tok[:, t * 2 * L:(t + 1) * 2 * L], ps[t % 2][:, 0:2 * L], rstd[:, t:t + 1], None, ALU.mult)
                    dve.tensor_scalar(heads4(v_tok)[:, t, :, 0:4], ps[t % 2][:, 2 * L:3 * L].rearrange("p (n d) -> p n d", d=4),
                                      rstd[:, t:t + 1], None, ALU.mult).then_inc(s["qkv_used"], 1)
                dve.wait_ge(s["qkv_used"], 2 * T * b + 2 * T)
                pairs = q_tok.rearrange("p (t n f two) -> p t n f two", t=T, n=2 * HEADS, two=2)
                turned = k_tok.rearrange("p (t n f two) -> p t n f two", t=T, n=2 * HEADS, two=2)
                left4 = spin_a[:, 0:S // 2].rearrange("p (t n f) -> p t n f", t=T, f=2)
                right4 = spin_b[:, 0:S // 2].rearrange("p (t n f) -> p t n f", t=T, f=2)
                over = lambda c: c.unsqueeze(2).to_broadcast([P, T, 2 * HEADS, 2])
                for out_half, (first, second, op) in enumerate(((cos, sin, ALU.subtract), (sin, cos, ALU.add))):
                    st.done(dve.tensor_tensor(left4, pairs[:, :, :, :, 0], over(first), ALU.mult))
                    st.done(dve.tensor_tensor(right4, pairs[:, :, :, :, 1], over(second), ALU.mult))
                    st.wait()
                    st.done(dve.tensor_tensor(turned[:, :, :, :, out_half], left4, right4, op))
                    st.wait()
                turned4 = k_tok.rearrange("p (t n d) -> p t n d", t=T, d=4)
                st.done(split((turned4[:, :, 0:HEADS, :], 4), qp))
                st.wait()
                split((turned4[:, :, HEADS:, :], 4), kp).then_inc(s["parts_ready"], 1)
                attention(1, 4)
                dve.tensor_scalar(heads_outT[:, 0:1], heads_out[:, 0:1], 1.0, None, ALU.mult).then_inc(s["tok_ready"], 1)
                dve.wait_ge(s["proj_psum"], 2 * b + 2)
                dve.wait_ge(s["out_stored"], 16 * b + 16)
                st.done(dve.tensor_tensor(res[:], xn[:], ps[1][:], ALU.add))
                st.wait()
                st.done(dve.tensor_tensor(x1[:], x1[:], res[:], ALU.add))
                rms(res, 3)
                for t in range(T):
                    ins = dve.scalar_tensor_tensor(q_tok[:, t * D:(t + 1) * D], res[:, t * D:(t + 1) * D], rstd[:, t:t + 1], g2[:],
                                                   ALU.mult, ALU.mult)
                ins.then_inc(s["tok_ready"], 1)
                z = small[:, 0:T * E1].rearrange("p (t e) -> p t e", e=E1)
                prob = small[:, T * E0:T * E0 + T * E1].rearrange("p (t e) -> p t e", e=E1)
                wide1 = lambda c: c.unsqueeze(2).to_broadcast([P, T, E1])
                logits = ps[3][:, 0:T * E1].rearrange("p (t e) -> p t e", e=E1)
                dve.wait_ge(s["logit_psum"], 2 * b + 2)
                st.done(dve.tensor_reduce(tops[:, 0:T], logits, AX_X, ALU.max))
                st.wait()
                dve.tensor_tensor(z, logits, wide1(tops[:, 0:T]), ALU.subtract).then_inc(s["shift1_ready"], 1)
                dve.wait_ge(s["e_ready"], 2 * b + 2)
                st.done(dve.tensor_reduce(tops[:, T:2 * T], z, AX_X, ALU.add))
                st.wait()
                st.done(dve.reciprocal(tops[:, 0:T], tops[:, T:2 * T]))
                st.wait()
                st.done(dve.tensor_tensor(prob, z, wide1(tops[:, 0:T]), ALU.mult))
                st.wait()
                top2(prob, E1, rev1, 1.0, 0.0)
                mixture(2 * C0, C1, lambda c: P)
                dve.wait_ge(s["ytok_psum"], 2 * b + 2)
                dve.tensor_tensor(res[:], x1[:], ps[0][:], ALU.add).then_inc(s["x1_ready"], 1)
                assert st.n == DVE_STEPS, st.n

        @block.scalar
        def _(act):
            act.wait_ge(s["weights_in"], LOADED)
            with act.Fori(0, B) as b:
                def root(n):
                    act.wait_ge(s["var_ready"], 4 * b + n + 1)
                    act.activation(var[:], var[:], ACT.Sqrt).then_inc(s["std_ready"], 1)

                def evacuate(n, dst, rows=P):
                    act.wait_ge(s["tokT_psum"], 5 * b + n + 1)
                    act.activation(dst[0:rows, :], ps[0][0:rows, :], ACT.Copy).then_inc(s["tokT_ready"], 1)

                def mixture(base, chunks, hid_rows):
                    for n in range(2 * chunks):
                        m = hid_rows(n % chunks)
                        act.wait_ge(s["gu_psum"], STEPS * b + base + n + 1)
                        act.activation(sg[n % 2][0:m, :], ps[n % 2][0:m, 0:HALF], ACT.Silu).then_inc(s["sg_ready"], 1)

                def leave(n):
                    act.wait_ge(s["down_done"], STEPS * b + (2 * C0, STEPS)[n])
                    act.activation(yT, ps[2][:], ACT.Copy).then_inc(s["y_ready"], 1)

                def routes_out(n):
                    act.wait_ge(s["rt_psum"], 2 * b + n + 1)
                    act.activation(routeT[0:PARTS * CW, :], ps[3][0:PARTS * CW, HALF:].bitcast(BF16), ACT.Copy).then_inc(s["rt_ready"], 1)

                def attention(kind, scale):
                    causal = kind == 1
                    a = 2 * b + kind
                    for g in range(GROUPS):
                        act.wait_ge(s["qg_psum"], a * GROUPS + g + 1)
                        act.activation(q_groups[0:GR, g * S:(g + 1) * S], ps[g][0:GR, 0:HALF].bitcast(BF16), ACT.Copy).then_inc(s["qg_ready"], 1)
                    with act.Fori(0, HEADS // 2) as hp:
                        for u in range(2):
                            act.wait_ge(s["qT_psum"], a * HEADS + 2 * hp + u + 1)
                            act.activation(qT[0:ROWS, bass.ds((2 * hp + u) * S, S)], ps[2 * u][0:ROWS, :],
                                           ACT.Copy).then_inc(s["qT_ready"], 1)
                    with act.Fori(0, GROUPS) as g:
                        G = a * GROUPS + g
                        first = (b * GROUPS + g) * NU[kind]
                        for i, (kc, j, lo, hi) in enumerate(UNITS[kind]):
                            act.wait_ge(s[ST_PSUM[kind]], first + i + 1)
                            if j == 0:
                                act.wait_ge(s["pv_done"], CREDIT + G * T + kc - 1)
                            act.activation(slot(kc % 2 * GH + j)[:, lo:hi], unit_bank(i)[:, 0:hi - lo], ACT.Exp,
                                           scale=scale).then_inc(s[P_READY[kind]], 1)

                root(0)
                evacuate(0, xnT)
                act.wait_ge(s["encr_psum"], b + 1)
                act.activation(encR, ps[1][:], ACT.Copy).then_inc(s["encr_ready"], 1)
                for t in range(T):
                    act.wait_ge(s["max0_ready"], b * T + t + 1)
                    if t >= 2:
                        act.wait_ge(s["pt_psum"], b * T + t - 1)
                    act.activation(p0[t % 2][:, 0:(t + 1) * P], ps[t % 2][:, 0:(t + 1) * P], ACT.Exp, bias=nmax0[:, t:t + 1],
                                   accum_out=sum0[:, t:t + 1]).then_inc(s["p0_ready"], 1)
                act.wait_ge(s["logit_psum"], 2 * b + 1)
                act.activation(small[:, 0:T * E0], ps[3][:, 0:T * E0], ACT.Exp, scale=-1.0).then_inc(s["e_ready"], 1)
                routes_out(0)
                mixture(0, C0, lambda c: P if c < C0 - 1 else M0)
                leave(0)
                root(1)
                evacuate(1, xnT)
                attention(0, float(1.0 / np.sqrt(np.float32(8))))
                evacuate(2, heads_outT)
                root(2)
                act.wait_ge(s["ct_psum"], b + 1)
                act.activation(heads_outT[0:L, :], ps[0][0:L, :], ACT.Copy).then_inc(s["ct_ready"], 1)
                attention(1, 0.5)
                evacuate(3, heads_outT, L)
                root(3)
                evacuate(4, xnT)
                act.wait_ge(s["shift1_ready"], b + 1)
                act.activation(small[:, 0:T * E1], small[:, 0:T * E1], ACT.Exp).then_inc(s["e_ready"], 1)
                routes_out(1)
                mixture(2 * C0, C1, lambda c: P)
                leave(1)

        @block.tensor
        def _(pe):
            pe.wait_ge(s["weights_in"], LOADED)
            pe.wait_ge(s["setup_done"], 4)
            with pe.Fori(0, B) as b:
                def turn(n, src, width=D):
                    pe.wait_ge(s["tok_ready"], 5 * b + n + 1)
                    for t in range(T):
                        dst, tile = ps[0][0:width, t * P:(t + 1) * P], src[:, t * width:(t + 1) * width]
                        ins = pe.transpose(dst, tile, ident_f) if width == D else pe.matmul(dst, tile, ident_f, start=True, stop=True)
                    ins.then_inc(s["tokT_psum"], 1)

                def mixture(which, base, chunks, hid_rows, wg, wu, wd, spread, xT):
                    def down(n):
                        half, c = n // chunks, n % chunks
                        m = hid_rows(c)
                        pe.wait_ge(s["hid_ready"], STEPS * b + base + n + 1)
                        pe.matmul(ps[2][:, half * HALF:(half + 1) * HALF], wd[0:m, c * D:(c + 1) * D], hid[n % 2][0:m, :],
                                  start=c == 0, stop=c == chunks - 1).then_inc(s["down_done"], 1)

                    for n in range(2 * chunks):
                        half, c = n // chunks, n % chunks
                        m = hid_rows(c)
                        tok = slice(half * HALF, (half + 1) * HALF)
                        if n >= 2:
                            pe.wait_ge(s["hid_ready"], STEPS * b + base + n - 1)
                        pe.matmul(ps[n % 2][0:m, 0:HALF], wg[:, c * P:c * P + m], xT[:, tok], start=True, stop=True)
                        pe.matmul(ps[n % 2][0:m, HALF:], wu[:, c * P:c * P + m], xT[:, tok], start=True, stop=True)
                        pe.matmul(ps[3][0:m, (n % 2) * HALF:(n % 2 + 1) * HALF], spread(c, m), routeT[0:PARTS * CW, tok],
                                  start=True, stop=True).then_inc(s["gu_psum"], 1)
                        if n >= 1:
                            down(n - 1)
                    down(2 * chunks - 1)
                    pe.wait_ge(s["y_ready"], 2 * b + which + 1)
                    for t in range(T):
                        ins = pe.transpose(ps[0][:, t * P:(t + 1) * P], yT[:, t * P:(t + 1) * P], ident_f)
                    ins.then_inc(s["ytok_psum"], 1)

                def routes_in(n):
                    pe.wait_ge(s["route_ready"], 2 * b + n + 1)
                    dst = ps[3][:, HALF:].bitcast(BF16)
                    for t in range(T):
                        ins = pe.transpose(dst[0:PARTS * CW, t * P:(t + 1) * P], routes[:, t * PARTS * CW:(t + 1) * PARTS * CW], ident_b)
                    ins.then_inc(s["rt_psum"], 1)
                    pe.wait_ge(s["rt_ready"], 2 * b + n + 1)

                def turn_parts(parts, g, dst):
                    for t in range(T):
                        at = (t * HEADS + g * GH) * PARTS * HF
                        ins = pe.transpose(dst[0:GR, t * P:(t + 1) * P], parts[:, at:at + GR], ident_b)
                    return ins

                def stack(dst, pick, j, groups, g):
                    for half in range(2):
                        ins = pe.matmul(dst[0:ROWS, half * HALF:(half + 1) * HALF], pick[0:GR, j * ROWS:(j + 1) * ROWS],
                                        groups[0:GR, bass.ds(g * S + half * HALF, HALF)], start=True, stop=True)
                    return ins

                def attention(kind):
                    causal = kind == 1
                    a = 2 * b + kind
                    pe.wait_ge(s["parts_ready"], a + 1)
                    for g in range(GROUPS):
                        turn_parts(q_parts, g, ps[g][:, 0:HALF].bitcast(BF16)).then_inc(s["qg_psum"], 1)
                        turn_parts(k_parts, g, ps[g][:, HALF:].bitcast(BF16)).then_inc(s["kg_psum"], 1)
                    with pe.Fori(0, GROUPS) as g:
                        pe.wait_ge(s["qg_ready"], (a + 1) * GROUPS)
                        pe.wait_ge(s["kg_ready"], (a + 1) * GROUPS)
                        for j in range(GH):
                            hh, u = GH * g + j, j % 2
                            pe.wait_ge(s["qT_ready"], a * HEADS + hh - 1 + CREDIT)
                            stack(ps[2 * u], pick_q, j, q_groups, g).then_inc(s["qT_psum"], 1)
                            pe.wait_ge(s["kT_ready"], a * HEADS + hh - 1 + CREDIT)
                            stack(ps[2 * u + 1], pick_k, j, k_groups, g).then_inc(s["kT_psum"], 1)
                    pe.wait_ge(s["qT_ready"], CREDIT + (a + 1) * HEADS)
                    pe.wait_ge(s["kT_ready"], CREDIT + (a + 1) * HEADS)

                    def head(stacked, g, j):
                        return stacked[0:ROWS, bass.ds((g * GH + j) * S, S)]

                    def piece(g, i):
                        j, t, half, lo, hi = PIECES[kind][i]
                        n = hi - lo
                        if i >= 3:
                            pe.wait_ge(s["max_done"], CREDIT + pieces_before(b, kind, g) + i - 2)
                        ins = pe.matmul(piece_bank(i)[:, 0:n], head(qT, g, j)[:, t * P:(t + 1) * P], head(kT, g, j)[:, lo:hi],
                                        start=True, stop=True)
                        if causal and hi == (t + 1) * P:
                            ins = pe.matmul(piece_bank(i)[:, n - P:n], ident_b, mask_q, start=False, stop=True, skip_group_check=True)
                        ins.then_inc(s["s_psum"], 1)

                    def turn_maxima(g):
                        pe.wait_ge(s["m_split"], a * GROUPS + g + 1)
                        for t in range(T):
                            ins = pe.transpose(piece_bank(NP[kind])[0:MR, :].bitcast(BF16)[:, t * P:(t + 1) * P], m_parts[:, t * MR:(t + 1) * MR], ident_b)
                        ins.then_inc(s["mt_psum"], 1)

                    def scores(g, i):
                        kc, j, lo, hi = UNITS[kind][i]
                        if i >= 3:
                            pe.wait_ge(s[P_READY[kind]], (b * GROUPS + g) * NU[kind] + i - 2)
                        ins = pe.matmul(unit_bank(i)[:, 0:hi - lo], head(kT, g, j)[:, kc * P:(kc + 1) * P], head(qT, g, j)[:, lo:hi],
                                        start=True, stop=True)
                        if causal and lo == kc * P:
                            ins = pe.matmul(unit_bank(i)[:, 0:P], ident_b, mask_k, start=False, stop=True, skip_group_check=True)
                        ins.then_inc(s[ST_PSUM[kind]], 1)

                    def values(g, kc, half):
                        lo, hi = max(kc * P if causal else 0, half * HALF), (half + 1) * HALF
                        if lo >= hi:
                            return
                        if kc == 0 and half == 0:
                            pe.wait_ge(s["v_staged"], a * GROUPS + g + 1)
                        done = sum(unit[0] <= kc for unit in UNITS[kind])
                        pe.wait_ge(s[P_READY[kind]], (b * GROUPS + g) * NU[kind] + done)
                        for j in range(GH):
                            ins = pe.matmul(ps[2][CW * j:CW * (j + 1), lo:hi], v_st[:, kc, j, :], slot(kc % 2 * GH + j)[:, lo:hi],
                                            start=kc == 0, stop=kc == T - 1, skip_group_check=True)
                        if half == 1:
                            ins.then_inc(s["pv_done"], 1)

                    def gather(g):
                        pe.wait_ge(s["o_evac"], a * GROUPS + g + 1)
                        for t in range(T):
                            ins = pe.matmul(bank(GATHER_BANK)[:, OC * t:OC * (t + 1)], o_sb[:, t * P:(t + 1) * P], pick_o, start=True, stop=True)
                        ins.then_inc(s["ot_psum"], 1)

                    def group(g, previous, following):
                        G = a * GROUPS + g
                        pe.wait_ge(s["m_rows"], 16 * PARTS * (G + 1))
                        work = [hi - lo for _, _, lo, hi in UNITS[kind]]
                        first, end = 2, PIECES_END[kind]
                        out = 0
                        for i, (kc, j, lo, hi) in enumerate(UNITS[kind]):
                            scores(g, i)
                            if kc >= 1 and hi == S and j % 2 == 1:
                                values(g, kc - 1, j // 2)
                            if i == first and previous:
                                gather(g - 1)
                            if i >= first and following:
                                due = min(NP[kind], -(-NP[kind] * sum(work[first:i + 1]) // sum(work[first:end + 1])))
                                while out < due:
                                    if out == 0:
                                        pe.wait_ge(s["mt_ready"], G + 1)
                                    if out == 2 and previous:
                                        pe.wait_ge(s["norm_done"], CREDIT + G)
                                    piece(g + 1, out)
                                    out += 1
                            if i == end + 3 and following:
                                turn_maxima(g + 1)
                        values(g, T - 1, 0)
                        values(g, T - 1, 1)

                    for i in range(NP[kind]):
                        piece(0, i)
                    turn_maxima(0)
                    group(0, False, True)
                    with pe.Fori(1, GROUPS - 1) as g:
                        group(g, True, True)
                    group(GROUPS - 1, True, False)
                    gather(GROUPS - 1)

                turn(0, xn)
                pe.wait_ge(s["tokT_ready"], 5 * b + 1)
                for half in range(2):
                    ins = pe.matmul(ps[1][:, half * HALF:(half + 1) * HALF], R_w[:], xnT[:, half * HALF:(half + 1) * HALF], start=True, stop=True)
                ins.then_inc(s["encr_psum"], 1)
                pe.wait_ge(s["encr_ready"], b + 1)

                def scores0(t):
                    if t >= 2:
                        pe.wait_ge(s["p0_ready"], b * T + t - 1)
                    keys = (t + 1) * P
                    for lo in range(0, keys, HALF):
                        hi = min(keys, lo + HALF)
                        pe.matmul(ps[t % 2][:, lo:hi], encR[:, t * P:(t + 1) * P], xnT[:, lo:hi], start=True, stop=True)
                    pe.matmul(ps[t % 2][:, t * P:keys], ident_b, mask_q, start=False, stop=True, skip_group_check=True).then_inc(s["s0_psum"], 1)

                scores0(0)
                for t in range(T):
                    if t + 1 < T:
                        scores0(t + 1)
                    pe.wait_ge(s["p0_ready"], b * T + t + 1)
                    if t >= 1:
                        pe.wait_ge(s["pt_ready"], b * T + t)
                    for j in range(t + 1):
                        ins = pe.transpose(ps[2][:, j * P:(j + 1) * P], p0[t % 2][:, j * P:(j + 1) * P], ident_f)
                    ins.then_inc(s["pt_psum"], 1)
                    pe.wait_ge(s["pt_ready"], b * T + t + 1)
                    if t >= 2:
                        pe.wait_ge(s["o0_used"], b * T + t - 1)
                    for j in range(t + 1):
                        ins = pe.matmul(ps[3][:, (t % 2) * HALF:(t % 2) * HALF + D], pT0[:, j * P:(j + 1) * P], xn[:, j * D:(j + 1) * D],
                                        start=j == 0, stop=j == t)
                    ins.then_inc(s["o0_psum"], 1)
                pe.wait_ge(s["o0_used"], b * T + T)
                for t in range(T):
                    ins = pe.matmul(ps[3][:, t * E0:(t + 1) * E0], xnT[:, t * P:(t + 1) * P], gate0[:], start=True, stop=True)
                ins.then_inc(s["logit_psum"], 1)
                routes_in(0)
                mixture(0, 0, C0, lambda c: P if c < C0 - 1 else M0, wg0, wu0, wd0,
                        lambda c, m: sel0[0:PARTS * CW, c * P:c * P + m], xnT)
                turn(1, xn)
                pe.wait_ge(s["tokT_ready"], 5 * b + 2)
                for t in range(T):
                    if t >= 2:
                        pe.wait_ge(s["qkv_used"], 2 * T * b + t - 1)
                    pe.matmul(ps[t % 2][:, 0:3 * D], xnT[:, t * P:(t + 1) * P], wqkv[:], start=True, stop=True).then_inc(s["qkv_psum"], 1)
                attention(0)
                turn(2, heads_out)
                pe.wait_ge(s["tokT_ready"], 5 * b + 3)
                for t in range(T):
                    ins = pe.matmul(ps[1][:, t * D:(t + 1) * D], heads_outT[:, t * P:(t + 1) * P], wo[:], start=True, stop=True)
                ins.then_inc(s["proj_psum"], 1)
                for half in range(2):
                    ins = pe.matmul(ps[0][0:L, half * HALF:(half + 1) * HALF], w_down[:], xnT[:, half * HALF:(half + 1) * HALF], start=True, stop=True)
                ins.then_inc(s["ct_psum"], 1)
                pe.wait_ge(s["ct_ready"], b + 1)
                pe.wait_ge(s["std_ready"], 4 * b + 3)
                for t in range(T):
                    if t >= 2:
                        pe.wait_ge(s["qkv_used"], 2 * T * b + T + t - 1)
                    pe.matmul(ps[t % 2][:, 0:3 * L], heads_outT[0:L, t * P:(t + 1) * P], wqkv1[0:L, :], start=True, stop=True).then_inc(s["qkv_psum"], 1)
                attention(1)
                turn(3, heads_out, L)
                pe.wait_ge(s["tokT_ready"], 5 * b + 4)
                for t in range(T):
                    ins = pe.matmul(ps[1][:, t * D:(t + 1) * D], heads_outT[0:L, t * P:(t + 1) * P], w_up[0:L, :], start=True, stop=True)
                ins.then_inc(s["proj_psum"], 1)
                turn(4, q_tok)
                pe.wait_ge(s["tokT_ready"], 5 * b + 5)
                for t in range(T):
                    ins = pe.matmul(ps[3][:, t * E1:(t + 1) * E1], xnT[:, t * P:(t + 1) * P], router[:], start=True, stop=True)
                ins.then_inc(s["logit_psum"], 1)
                routes_in(1)
                mixture(1, 2 * C0, C1, lambda c: P, wg1, wu1, wd1, lambda c, m: sel1[0:PARTS * CW, (c // 2) * P:(c // 2) * P + m], xnT)


def kernel(**inputs):
    import ml_dtypes
    import concourse.bacc as bacc
    from concourse.bass_utils import run_bass_kernel_spmd as run

    i = {k: np.asarray(v) for k, v in inputs.items()}
    cb, cf = constants()
    side = lambda w: w.transpose(1, 0, 2).reshape(w.shape[1], -1)
    rows = lambda w: w.reshape(-1, P, D).transpose(1, 0, 2).reshape(P, -1)
    a = {
        "const_b": cb.astype(ml_dtypes.bfloat16), "const_f": cf,
        "x": i["L0_attn_encoding"], "R": i["L0_attn_R"], "gate0": i["L0_ffn_gate_w"].T,
        "wg0": np.concatenate([side(i["L0_ffn_w_gate"]), i["L0_ffn_ws_gate"]], axis=1),
        "wu0": np.concatenate([side(i["L0_ffn_w_up"]), i["L0_ffn_ws_up"]], axis=1),
        "wd0a": rows(i["L0_ffn_w_down"].reshape(-1, D)), "wd0b": i["L0_ffn_ws_down"],
        "wqkv": np.concatenate([i[f"L1_attn_w_{n}"].T for n in "qkv"], axis=1), "wo": i["L1_attn_w_o"].T,
        "scale4": np.stack([i[f"L1_attn_s_{n}"].reshape(()) for n in "qkvo"]),
        "bias4": np.concatenate([i[f"L1_attn_b_{n}"] for n in "qkvo"]),
        "g1": i["L1_ffn_g1"].reshape(D, 1), "g2": i["L1_ffn_g2"],
        "w_down": i["L1_ffn_w_down"], "wqkv1": np.concatenate([i[f"L1_ffn_w{n}"] for n in "qkv"], axis=1),
        "w_up": i["L1_ffn_w_up"], "router": i["L1_ffn_router_w"],
        "wg1": side(i["L1_ffn_w1"]), "wu1": side(i["L1_ffn_w3"]), "wd1": rows(i["L1_ffn_w2"].reshape(-1, D)),
    }
    nc = bacc.Bacc("TRN2", target_bir_lowering=False, num_devices=1)
    arrays, h = {}, {}
    for name, v in a.items():
        v = np.ascontiguousarray(v)
        arrays[f"in_{name}"] = v
        h[name] = nc.dram_tensor(f"in_{name}", v.shape, mybir.dt.from_np(v.dtype), kind="ExternalInput").ap()
    h["m_rows"] = nc.dram_tensor("m_rows", (PARTS, GH, S), BF16, kind="Internal").ap()
    h["out"] = nc.dram_tensor("out_0", (B, S, D), F32, kind="ExternalOutput").ap()
    build(nc, h)
    r = run(nc, [arrays], core_ids=[0])
    return r.results[0]["out_0"]
```

```python
from contextlib import ExitStack

import numpy as np

import concourse.bass as bass
from concourse import mybir

F32 = mybir.dt.float32
BF16 = mybir.dt.bfloat16
ALU = mybir.AluOpType
ACT = mybir.ActivationFunctionType
AX_X = mybir.AxisListType.X

P = 128
B, S, D = 4, 1024, 128
T = S // P
HALF = 512
HEADS = 16
PARTS = 3
HD = 8
HF = HD + 1
HDC = 4
HFC = HDC + 1
ROWS = PARTS * PARTS * HF
ROWSC = PARTS * PARTS * HFC
GH = 4
GROUPS = HEADS // GH
GR = GH * PARTS * HF
GRC = GH * PARTS * HFC
CW = P // GH
OC = GH * HF
MR = GH * PARTS
E0, M0 = 16, 64
E1, M1 = 8, 256
L = 64
C0 = (E0 + 1) * M0 // P + 1
C1 = E1 * M1 // P
CHUNKS = C0 + C1
STEPS = 2 * CHUNKS
EPS = 1e-5
ROUTE_SCALE = 2.5
ROUTE_EPS = 1e-20
NEG = -1e30
THETA = 10000.0


def constants():
    i = np.arange(P)
    mask_q = np.where(i[None, :] <= i[:, None], 0.0, NEG)
    mask_k = mask_q.T
    sel0 = np.zeros((P, (E0 + 1) * M0))
    sel1 = np.zeros((P, E1 * P))
    for a in range(PARTS):
        for e in range(E0 + 1):
            sel0[CW * a + e, e * M0:(e + 1) * M0] = 1.0
        for e in range(E1):
            sel1[CW * a + e, e * P:(e + 1) * P] = 1.0
    picks = []
    for features in (HF, HFC):
        stacked, pick_q, pick_k = np.arange(PARTS * PARTS * features).reshape(PARTS, PARTS, features), *np.zeros((2, P, GH, P))
        for j in range(GH):
            for part in range(PARTS):
                for d in range(features):
                    row = (j * PARTS + part) * features + d
                    pick_q[row, j, stacked[part, :, d]] = 1.0
                    pick_k[row, j, stacked[:, part, d]] = 1.0
        picks += [pick_q.reshape(P, -1), pick_k.reshape(P, -1)]
    cb = np.concatenate([np.eye(P), mask_q, mask_k, *picks, sel0, sel1], axis=1)
    pick_o = np.zeros((P, GH, HF))
    for j in range(GH):
        pick_o[CW * j + np.arange(HF), j, np.arange(HF)] = 1.0
    pos = (np.arange(T)[None, :] * P + i[:, None]).astype(np.float32)
    inv = (np.float32(1.0) / np.float32(THETA) ** (np.arange(0, 4, 2, dtype=np.float32) / np.float32(4))).astype(np.float32)
    ang = (pos[:, :, None] * inv[None, None, :]).astype(np.float32)
    rev0 = np.tile(E0 - np.arange(E0), (P, 1))
    rev1 = np.tile(E1 - np.arange(E1), (P, 1))
    cf = np.concatenate([np.eye(P), pick_o.reshape(P, -1), np.cos(ang).reshape(P, -1), np.sin(ang).reshape(P, -1), rev0, rev1], axis=1)
    return cb, np.ascontiguousarray(cf.astype(np.float32))


class Steps:

    def __init__(self, eng, sem, base):
        self.eng, self.sem, self.base, self.n = eng, sem, base, 0

    def done(self, ins):
        ins.then_inc(self.sem, 1)
        self.n += 1

    def wait(self):
        self.eng.wait_ge(self.sem, self.base + self.n)


def build(nc, h):
    with ExitStack() as ctx:
        def sb(name, cols, dt=F32):
            return ctx.enter_context(nc.sbuf_tensor(name, [P, cols], dt))

        def sem(name):
            return ctx.enter_context(nc.semaphore(name))

        cb_cols, cf_cols = h["const_b"].shape[1], h["const_f"].shape[1]
        const_b = sb("const_b", cb_cols, BF16)
        const_f = sb("const_f", cf_cols)
        ident_b, mask_q, mask_k = (const_b[:, k * P:(k + 1) * P] for k in range(3))
        picks, at = [], 3 * P
        for _ in range(4):
            picks.append(const_b[:, at:at + GH * P])
            at += GH * P
        pick_q, pick_k, pick_qc, pick_kc = picks
        sel0 = const_b[:, at:at + (E0 + 1) * M0]
        sel1 = const_b[:, at + (E0 + 1) * M0:]
        ident_f = const_f[:, 0:P]
        pick_o = const_f[:, P:P + OC]
        cos = const_f[:, P + OC:P + OC + 2 * T].rearrange("p (t f) -> p t f", f=2)
        sin = const_f[:, P + OC + 2 * T:P + OC + 4 * T].rearrange("p (t f) -> p t f", f=2)
        rev0 = const_f[:, P + OC + 4 * T:P + OC + 4 * T + E0]
        rev1 = const_f[:, P + OC + 4 * T + E0:]
        R_w = sb("R_w", D)
        gate0 = sb("gate0", E0)
        wg0 = sb("wg0", (E0 + 1) * M0)
        wu0 = sb("wu0", (E0 + 1) * M0)
        wd0 = sb("wd0", C0 * D)
        wqkv = sb("wqkv", 3 * D)
        wo = sb("wo", D)
        scale4 = sb("scale4", 4)
        bias4 = sb("bias4", 4 * D)
        g1 = sb("g1", 1)
        g2 = sb("g2", D)
        w_down = sb("w_down", L)
        wqkv1 = sb("wqkv1", 3 * L)
        w_up = sb("w_up", D)
        router = sb("router", E1)
        wg1 = sb("wg1", E1 * M1)
        wu1 = sb("wu1", E1 * M1)
        wd1 = sb("wd1", C1 * D)
        x_b = sb("x_b", S)
        xn = sb("xn", S)
        xnT = sb("xnT", S)
        x1 = sb("x1", S)
        res = sb("res", S)
        qkv = sb("qkv", 3 * S)
        buf = sb("buf", T * S)
        q_parts = sb("q_parts", T * HEADS * PARTS * HF, BF16)
        k_parts = sb("k_parts", T * HEADS * PARTS * HF, BF16)
        qT = sb("qT", HEADS * S, BF16)
        kT = sb("kT", HEADS * S, BF16)
        v_ones = sb("v_ones", T * GH * CW)
        o_sb = sb("o_sb", S)
        stats = sb("stats", T * 6)
        mv = sb("mv", T * 3)
        var = sb("var", T)
        rstd = sb("rstd", T)
        tops = sb("tops", 8 * T)
        nmax = sb("nmax", 2 * T * GH)
        m_rest = sb("m_rest", T * GH)
        m_parts = sb("m_parts", T * MR, BF16)
        rsum_g = sb("rsum_g", T * GH)
        nmax0 = sb("nmax0", T)
        sum0 = sb("sum0", T)
        rsum = sb("rsum", T)
        routes = sb("routes", T * PARTS * CW, BF16)

        slot = lambda n: buf[:, n * S:(n + 1) * S]
        p0 = [slot(0), slot(1)]
        pT0 = slot(2)
        encR = slot(3)
        sg = [slot(4)[:, 0:HALF], slot(4)[:, HALF:]]
        gu = [slot(5)[:, 0:HALF], slot(5)[:, HALF:]]
        hid = [slot(6)[:, 0:HALF], slot(6)[:, HALF:]]
        yT = slot(7)
        routeT = slot(3)[:, 0:HALF].bitcast(BF16)
        rest = slot(0)
        small = slot(1)[:, 0:6 * T * E0]
        spin_a, spin_b = slot(1), slot(2)
        cT, qk_c, turned = slot(3), slot(4), slot(5)
        q_turn = slot(6)[0:GR, 0:HALF].bitcast(BF16)
        k_turn = slot(6)[0:GR, HALF:].bitcast(BF16)
        q_tok, k_tok, v_tok = (qkv[:, n * S:(n + 1) * S] for n in range(3))
        heads_out, heads_outT = q_tok, k_tok
        heads_c = v_tok[:, 0:T * L]
        heads_cT = v_tok[0:L, :]
        mT = k_tok[:, 0:HALF].bitcast(BF16)
        v_c = k_tok[:, HALF:]
        q_parts_c, k_parts_c = x_b[:].bitcast(BF16), xnT[:].bitcast(BF16)
        PC = T * GROUPS * GRC
        qpc = q_parts_c[:, 0:PC].rearrange("p (n a d) -> p n a d", a=PARTS, d=HFC)
        kpc = k_parts_c[:, 0:PC].rearrange("p (n a d) -> p n a d", a=PARTS, d=HFC)
        q_turn_c, k_turn_c = q_parts[0:GR, 0:S], q_parts[0:GR, S:2 * S]
        qp = q_parts[:].rearrange("p (n a d) -> p n a d", a=PARTS, d=HF)
        kp = k_parts[:].rearrange("p (n a d) -> p n a d", a=PARTS, d=HF)
        v_st = v_ones[:].rearrange("p (k j c) -> p k j c", j=GH, c=CW)
        mp = m_parts[:].rearrange("p (t j a) -> p t j a", a=PARTS, j=GH)
        rt = routes[:].rearrange("p (t a e) -> p t a e", a=PARTS, e=CW)

        ps = [ctx.enter_context(nc.psum_tensor(f"ps{n}", [P, S], F32)) for n in range(4)]

        names = """weights_in x_in out_stored setup_done var_ready std_ready tok_ready tokT_psum tokT_ready
        encr_psum encr_ready s0_psum max0_ready p0_ready pt_psum pt_ready o0_psum o0_used
        logit_psum shift1_ready e_ready route_ready rt_psum rt_ready gu_psum sg_ready gu_ready hid_ready down_done
        y_ready ytok_psum x1_ready qkv_psum qkv_used ct_psum ct_ready qkv_c_psum parts_ready parts_c_ready
        stack_psum stack_ready qc_psum qc_ready kc_psum kc_ready
        s_psum max_done m_steps m_split mt_psum mt_ready m_rows st_psum st_psum_causal p_ready p_ready_causal pv_done o_evac ot_psum
        norm_done v_staged proj_psum dve_steps rsum_done""".split()
        s = {n: sem(n) for n in names}
        block = ctx.enter_context(nc.Block())

        N_WEIGHTS = 21
        LOADED = 16 * N_WEIGHTS
        CREDIT = 2
        DVE_STEPS = 166
        M_STEPS = 5
        QKV_C_BANKS = (2, 3, 6, 7)

        PIECES = [[(j, t, half, lo, min(lo + HALF, (t + 1) * P if causal else S))
                   for j in range(GH) for t in range(T) for half, lo in enumerate(range(0, (t + 1) * P if causal else S, HALF))]
                  for causal in (False, True)]
        UNITS = [[(kc, j, max(kc * P, half * HALF) if causal else half * HALF, (half + 1) * HALF)
                  for kc in range(T) for j in range(GH) for half in range(2) if not (causal and kc * P >= (half + 1) * HALF)]
                 for causal in (False, True)]
        NP, NU = [len(p) for p in PIECES], [len(u) for u in UNITS]
        UNIT_BANKS, PIECE_BANKS = (0, 1, 2), (6, 7)
        LAST_BANKS = UNIT_BANKS + PIECE_BANKS
        SIDE_BANK = 3
        PRELUDE, EARLY = 10, 12

        def bank(n):
            return ps[n // 2][:, n % 2 * HALF:(n % 2 + 1) * HALF]

        def banks_of_units(kind, last):
            return LAST_BANKS if kind == 1 and last else UNIT_BANKS

        def piece_bank(kind, i):
            if kind == 1 or i < EARLY:
                return bank(PIECE_BANKS[i % 2]), 2
            return bank(((SIDE_BANK,) + PIECE_BANKS)[i % 3]), 3

        def side_bank(g, side):
            return bank(PIECE_BANKS[0] if (g, side) == (0, "k") else SIDE_BANK)

        TURNS = 2 * GH + 1

        def plan(kind, g):
            todo = [[] for _ in range(NU[kind] + 1)]

            def spread(items, lo, hi):
                for k, item in enumerate(items):
                    todo[lo + k * (hi - lo) // len(items)].append(item)

            first, last = (kind, g) == (0, 0), (kind, g) == (1, GROUPS - 1)
            after = kind if g < GROUPS - 1 else 1
            pieces = [] if last else [("piece", i) for i in range(NP[after])]
            end = [("values", 0), ("values", 1), ("outputs", 0), ("outputs", 1)] if not first else []
            if (kind, g) == (0, GROUPS - 1):
                ahead = [("stack", 0, m, side) for m in range(TURNS) for side in "qk"]
                todo[0] = end + ahead[:8]
                spread(ahead[8:], 2, 14)
                spread([("stack", 1, m, side) for m in range(TURNS) for side in "qk"], 15, 60)
                spread(pieces, 15, 57)
                todo[59].append(("maxima", 0))
            else:
                todo[0] = end[:1] + pieces[:2] + end[1:2] + pieces[2:6] + end[2:3] + pieces[6:8] + end[3:] + pieces[8:PRELUDE]
                hi = (55, 41)[kind]
                if kind == 1 and g < 2:
                    spread([("stack", g + 2, m, side) for m in range(TURNS) for side in "qk"], 4, 44)
                spread(pieces[PRELUDE:], 2, hi)
                if pieces:
                    todo[hi + 1].append(("maxima", 0))
            return todo

        ST_PSUM, P_READY = ("st_psum", "st_psum_causal"), ("p_ready", "p_ready_causal")

        def pieces_before(b, kind, g):
            return b * GROUPS * sum(NP) + kind * GROUPS * NP[0] + g * NP[kind]

        @block.sync
        def _(sp):
            loads = [(const_b[:], h["const_b"]), (const_f[:], h["const_f"]), (R_w[:], h["R"]), (gate0[:], h["gate0"]),
                     (wg0[:], h["wg0"]), (wu0[:], h["wu0"]), (wd0[:, 0:(C0 - 1) * D], h["wd0a"]), (wd0[0:M0, (C0 - 1) * D:], h["wd0b"]),
                     (wqkv[:], h["wqkv"]), (wo[:], h["wo"]), (scale4[:], h["scale4"].partition_broadcast(P)),
                     (bias4[:], h["bias4"].partition_broadcast(P)), (g1[:], h["g1"]), (g2[:], h["g2"].partition_broadcast(P)),
                     (w_down[:], h["w_down"]), (wqkv1[0:L, :], h["wqkv1"]), (w_up[0:L, :], h["w_up"]), (router[:], h["router"]),
                     (wg1[:], h["wg1"]), (wu1[:], h["wu1"]), (wd1[:], h["wd1"])]
            x_view = h["x"].rearrange("b (t p) d -> b p t d", p=P)
            out_view = h["out"].rearrange("b (t p) d -> b p t d", p=P)
            sp.dma_start(x_b[:].rearrange("p (t d) -> p t d", d=D), x_view[0]).then_inc(s["x_in"], 16)
            assert len(loads) == N_WEIGHTS
            for dst, src in loads:
                sp.dma_start(dst, src).then_inc(s["weights_in"], 16)
            def store(b):
                sp.wait_ge(s["x1_ready"], 2 * b + 2)
                sp.dma_start(out_view[bass.ds(b, 1)].rearrange("b p t d -> (b p) t d"),
                             res[:].rearrange("p (t d) -> p t d", d=D)).then_inc(s["out_stored"], 16)

            def max_rows(b):
                for kind, features in enumerate((HF, HFC)):
                    a = 2 * b + kind
                    with sp.Fori(0, GROUPS) as g:
                        sp.wait_ge(s["mt_ready"], a * GROUPS + g + 1)
                        for j in range(GH):
                            rows = slice(features - 1, features + 2 * PARTS * features, PARTS * features)
                            sp.dma_start(qT[rows, bass.ds((g * GH + j) * S, S)], mT[j * PARTS:(j + 1) * PARTS, :]).then_inc(s["m_rows"], 16)

            with sp.Fori(0, B - 1) as b:
                max_rows(b)
                sp.wait_ge(s["qc_psum"], (b + 1) * GROUPS * TURNS)
                sp.dma_start(x_b[:].rearrange("p (t d) -> p t d", d=D),
                             x_view[bass.ds(b + 1, 1)].rearrange("b p t d -> (b p) t d")).then_inc(s["x_in"], 16)
                store(b)
            max_rows(B - 1)
            store(B - 1)
            sp.wait_ge(s["out_stored"], 16 * B + 16)

        @block.gpsimd
        def _(pool):
            with pool.Fori(0, B) as b:
                for kind, (ready, values, hd) in enumerate((("parts_ready", v_tok, HD), ("parts_c_ready", v_c, HDC))):
                    a = 2 * b + kind
                    with pool.Fori(0, GROUPS) as g:
                        pool.wait_ge(s[ready], b + 1)
                        pool.wait_ge(s["pv_done"], CREDIT + (a * GROUPS + g) * T)
                        pool.tensor_copy(v_st[:, :, :, 0:hd], values.rearrange("p (t n) -> p t n", t=T)
                                         [:, :, bass.ds(g * GH * hd, GH * hd)].rearrange("p t (j c) -> p t j c", c=hd)).then_inc(s["v_staged"], 1)

        @block.vector
        def _(dve):
            dve.memset(v_ones[:], 0.0).then_inc(s["max_done"], CREDIT)
            dve.memset(routes[:], 0.0).then_inc(s["pv_done"], CREDIT)
            dve.memset(kp[:, :, 1:, HD:HF], 0.0).then_inc(s["norm_done"], CREDIT)
            dve.memset(kp[:, :, 0, HD:HF], 1.0).then_inc(s["kc_ready"], CREDIT)
            dve.memset(tops[:, 0:T], 0.0).then_inc(s["out_stored"], 16)
            dve.memset(tops[:, T:], 0.0).then_inc(s["stack_ready"], CREDIT)
            dve.wait_ge(s["max_done"], CREDIT)
            dve.wait_ge(s["pv_done"], CREDIT)
            dve.memset(rt[:, :, 0, E0:E0 + 1], 1.0).then_inc(s["setup_done"], 1)
            dve.memset(v_st[:, :, :, HD:HF], 1.0).then_inc(s["setup_done"], 1)
            dve.wait_ge(s["weights_in"], LOADED)
            dve.tensor_scalar(w_down[:], w_down[:], g1[:, 0:1], None, ALU.mult).then_inc(s["setup_done"], 1)

            def tiles(ap):
                return ap.rearrange("p (t c) -> p t c", t=T)

            with dve.Fori(0, B) as b:
                st = Steps(dve, s["dve_steps"], b * DVE_STEPS)

                def statistics(src):
                    for t in range(T):
                        st.done(dve.bn_stats(stats[:, 6 * t:6 * t + 6], src[:, t * D:(t + 1) * D]))
                    st.wait()
                    even, odd = field[:, :, 1], field[:, :, 4]
                    st.done(dve.tensor_tensor(means, even, odd, ALU.add))
                    st.done(dve.tensor_tensor(apart, even, odd, ALU.subtract))
                    st.done(dve.tensor_tensor(variances, field[:, :, 2], field[:, :, 5], ALU.add))
                    st.wait()
                    st.done(dve.tensor_scalar(means, means, 0.5, None, ALU.mult))
                    st.done(dve.scalar_tensor_tensor(apart, apart, 0.25, apart, ALU.mult, ALU.mult))
                    st.wait()
                    st.done(dve.scalar_tensor_tensor(variances, variances, 1.0 / D, apart, ALU.mult, ALU.add))
                    st.wait()

                field = stats[:].rearrange("p (t k) -> p t k", k=6)
                means, variances, apart = (mv[:, n * T:(n + 1) * T] for n in range(3))

                def inverse_deviation(n):
                    dve.wait_ge(s["std_ready"], 4 * b + n + 1)
                    st.done(dve.reciprocal(rstd[:], var[:]))
                    st.wait()

                def layernorm(src, n):
                    statistics(src)
                    dve.tensor_scalar(var[:], variances, EPS, None, ALU.add).then_inc(s["var_ready"], 1)
                    inverse_deviation(n)
                    for t in range(T):
                        ins = dve.tensor_scalar(xn[:, t * D:(t + 1) * D], src[:, t * D:(t + 1) * D], means[:, t:t + 1],
                                                rstd[:, t:t + 1], ALU.subtract, ALU.mult)
                    ins.then_inc(s["tok_ready"], 1)

                def top2(score, experts, rev, scale, eps):
                    n = T * experts
                    view = lambda k: small[:, k * T * E0:k * T * E0 + n].rearrange("p (t e) -> p t e", e=experts)
                    eq, key, hot1, left = view(2), view(3), view(4), view(5)
                    col = lambda k: tops[:, k * T:(k + 1) * T]
                    wide = lambda c: c.unsqueeze(2).to_broadcast([P, T, experts])
                    order = rev.unsqueeze(1).to_broadcast([P, T, experts])

                    def best(src, value, hot):
                        st.done(dve.tensor_reduce(value, src, AX_X, ALU.max))
                        st.wait()
                        st.done(dve.tensor_tensor(eq, src, wide(value), ALU.is_equal))
                        st.wait()
                        st.done(dve.tensor_tensor(key, eq, order, ALU.mult))
                        st.wait()
                        st.done(dve.tensor_reduce(col(4), key, AX_X, ALU.max))
                        st.wait()
                        st.done(dve.tensor_tensor(hot, key, wide(col(4)), ALU.is_equal))
                        st.wait()

                    best(score, col(2), hot1)
                    st.done(dve.scalar_tensor_tensor(left, hot1, -4.0, score, ALU.mult, ALU.add))
                    st.wait()
                    best(left, col(3), eq)
                    st.done(dve.tensor_tensor(hot1, hot1, eq, ALU.add))
                    st.done(dve.scalar_tensor_tensor(col(5), col(2), eps, col(3), ALU.add, ALU.add))
                    st.wait()
                    st.done(dve.tensor_tensor(key, hot1, score, ALU.mult))
                    st.done(dve.reciprocal(col(6), col(5)))
                    st.wait()
                    st.done(dve.scalar_tensor_tensor(left, key, scale, wide(col(6)), ALU.mult, ALU.mult))
                    st.wait()
                    for part in range(PARTS):
                        dst = rt[:, :, part, 0:experts]
                        ins = dve.tensor_copy(dst, left)
                        if part == PARTS - 1:
                            ins.then_inc(s["route_ready"], 1)
                            break
                        st.done(ins)
                        st.wait()
                        st.done(dve.tensor_tensor(left, left, dst, ALU.subtract))
                        st.wait()

                def mixture(base, chunks, hid_rows):
                    for n in range(2 * chunks):
                        k = STEPS * b + base + n
                        m = hid_rows(n % chunks)
                        dve.wait_ge(s["sg_ready"], k + 1)
                        dve.tensor_tensor(gu[n % 2][0:m, :], sg[n % 2][0:m, :], ps[n % 2][0:m, HALF:], ALU.mult).then_inc(s["gu_ready"], 1)
                        if base + n >= 2:
                            dve.wait_ge(s["down_done"], k - 1)
                        dve.wait_ge(s["gu_ready"], k + 1)
                        dve.tensor_tensor(hid[n % 2][0:m, :], gu[n % 2][0:m, :], ps[3][0:m, (n % 2) * HALF:(n % 2 + 1) * HALF],
                                          ALU.mult).then_inc(s["hid_ready"], 1)

                def split(src_of, parts):
                    src, hd = src_of
                    r = rest[:, 0:HEADS * T * hd].rearrange("p (t n d) -> p t n d", t=T, d=hd)
                    to = lambda part: parts[:, :, part, 0:hd].rearrange("p (t n) d -> p t n d", t=T)
                    st.done(dve.tensor_copy(to(0), src))
                    st.wait()
                    st.done(dve.tensor_tensor(r, src, to(0), ALU.subtract))
                    st.wait()
                    st.done(dve.tensor_copy(to(1), r))
                    st.wait()
                    st.done(dve.tensor_tensor(r, r, to(1), ALU.subtract))
                    st.wait()
                    ins = dve.tensor_copy(to(2), r)
                    return ins

                def piece(kind, g, i):
                    j, t, half, lo, hi = PIECES[kind][i]
                    dve.wait_ge(s["s_psum"], pieces_before(b, kind, g) + i + 1)
                    dve.tensor_reduce(nm[:, half, t, j:j + 1], piece_bank(kind, i)[0][:, 0:hi - lo],
                                      AX_X, ALU.max, negate=True).then_inc(s["max_done"], 1)

                nm = nmax[:].rearrange("p (h t j) -> p h t j", h=2, j=GH)

                def maxima(kind, g):
                    G = (2 * b + kind) * GROUPS + g
                    ms = Steps(dve, s["m_steps"], G * M_STEPS)
                    dve.wait_ge(s["max_done"], CREDIT + pieces_before(b, kind, g) + NP[kind])
                    m, r = nm[:, 0], m_rest[:].rearrange("p (t j) -> p t j", j=GH)
                    two = T // 2 if kind == 1 else 0
                    ms.done(dve.tensor_tensor(m[:, two:], m[:, two:], nm[:, 1, two:], ALU.min))
                    ms.wait()
                    ms.done(dve.tensor_copy(mp[:, :, :, 0], m))
                    ms.wait()
                    ms.done(dve.tensor_tensor(r, m, mp[:, :, :, 0], ALU.subtract))
                    ms.wait()
                    ms.done(dve.tensor_copy(mp[:, :, :, 1], r))
                    ms.wait()
                    ms.done(dve.tensor_tensor(r, r, mp[:, :, :, 1], ALU.subtract))
                    ms.wait()
                    assert ms.n == M_STEPS
                    dve.tensor_copy(mp[:, :, :, 2], r).then_inc(s["m_split"], 1)
                    dve.wait_ge(s["mt_psum"], G + 1)
                    dve.tensor_copy(mT[0:MR, :], piece_bank(kind, NP[kind])[0][0:MR, :].bitcast(BF16)).then_inc(s["mt_ready"], 1)

                def stack_keys(g, m):
                    dve.wait_ge(s["kc_psum"], (b * GROUPS + g) * TURNS + m + 1)
                    if m == 0:
                        dst, src = k_turn_c, side_bank(g, "k")[0:GR, :].bitcast(BF16)
                    else:
                        at = g * GH * S + (m - 1) * HALF
                        dst, src = kT[:, at:at + HALF], side_bank(g, "k")
                    dve.tensor_scalar(dst, src, 1.0, None, ALU.mult).then_inc(s["kc_ready"], 1)

                def beside(kind, g, step):
                    G = (2 * b + kind) * GROUPS + g
                    after, later = (kind, g + 1) if step < GROUPS - 1 else (1, 0)
                    for what, *how in sum(plan(kind, step), []):
                        if what == "piece":
                            piece(after, later, how[0])
                        elif what == "maxima":
                            maxima(after, later)
                        elif what == "stack" and how[2] == "k":
                            stack_keys(how[0], how[1])
                        elif what == "outputs" and how[0] == 1:
                            outputs(G - 1, *((g - 1, kind) if step > 0 else (GROUPS - 1, 0)))

                def attentions():
                    for i in range(NP[0]):
                        piece(0, 0, i)
                    maxima(0, 0)
                    beside(0, 0, 0)
                    with dve.Fori(1, GROUPS - 1) as g:
                        beside(0, g, 1)
                    beside(0, GROUPS - 1, GROUPS - 1)
                    for g in range(GROUPS):
                        beside(1, g, g)
                    outputs((2 * b + 2) * GROUPS - 1, GROUPS - 1, 1)

                def outputs(G, g, kind):
                    hd, dst = ((HD, heads_out), (HDC, heads_c))[kind]
                    dve.wait_ge(s["ot_psum"], G + 1)
                    o = bank(SIDE_BANK)[:, 0:T * OC].rearrange("p (t j c) -> p t j c", j=GH, c=HF)
                    inv = rsum_g[:].rearrange("p (t j) -> p t j", j=GH)
                    dve.reciprocal(inv, o[:, :, :, HD]).then_inc(s["rsum_done"], 1)
                    dve.wait_ge(s["rsum_done"], G + 1)
                    dst = tiles(dst)[:, :, bass.ds(g * GH * hd, GH * hd)].rearrange("p t (j d) -> p t j d", d=hd)
                    dve.tensor_tensor(dst, o[:, :, :, 0:hd], inv.unsqueeze(3).to_broadcast([P, T, GH, hd]), ALU.mult).then_inc(s["norm_done"], 1)

                dve.wait_ge(s["x_in"], 16 * b + 16)
                layernorm(x_b, 0)
                for t in range(T):
                    dve.wait_ge(s["s0_psum"], b * T + t + 1)
                    dve.tensor_reduce(nmax0[:, t:t + 1], ps[t % 2][:, 0:(t + 1) * P], AX_X, ALU.max, negate=True).then_inc(s["max0_ready"], 1)
                    dve.wait_ge(s["pt_psum"], b * T + t + 1)
                    if t >= 1:
                        dve.wait_ge(s["o0_psum"], b * T + t)
                    dve.tensor_copy(pT0[:, 0:(t + 1) * P], ps[2][:, 0:(t + 1) * P]).then_inc(s["pt_ready"], 1)
                    dve.wait_ge(s["p0_ready"], b * T + t + 1)
                    st.done(dve.reciprocal(rsum[:, t:t + 1], sum0[:, t:t + 1]))
                    st.wait()
                    dve.wait_ge(s["o0_psum"], b * T + t + 1)
                    dve.scalar_tensor_tensor(x1[:, t * D:(t + 1) * D], ps[3][:, (t % 2) * HALF:(t % 2) * HALF + D], rsum[:, t:t + 1],
                                             x_b[:, t * D:(t + 1) * D], ALU.mult, ALU.add).then_inc(s["o0_used"], 1)
                e0, score = small[:, 0:T * E0], small[:, T * E0:2 * T * E0]
                dve.wait_ge(s["e_ready"], 2 * b + 1)
                st.done(dve.tensor_scalar(e0, e0, 1.0, None, ALU.add))
                st.wait()
                st.done(dve.reciprocal(score, e0))
                st.wait()
                top2(score.rearrange("p (t e) -> p t e", e=E0), E0, rev0, ROUTE_SCALE, ROUTE_EPS)
                mixture(0, C0, lambda c: P if c < C0 - 1 else M0)
                dve.wait_ge(s["ytok_psum"], 2 * b + 1)
                dve.wait_ge(s["o0_used"], b * T + T)
                dve.tensor_tensor(x1[:], x1[:], ps[0][:], ALU.add).then_inc(s["x1_ready"], 1)
                dve.wait_ge(s["x1_ready"], 2 * b + 1)
                layernorm(x1, 1)
                st.done(dve.memset(qp[:, :, :, HD:HF], 0.0))
                for t in range(T):
                    dve.wait_ge(s["qkv_psum"], T * b + t + 1)
                    for n, dst in enumerate((q_tok, k_tok, v_tok)):
                        ins = dve.scalar_tensor_tensor(dst[:, t * D:(t + 1) * D], bank(t % 2)[:, n * D:(n + 1) * D], scale4[:, n:n + 1],
                                                       bias4[:, n * D:(n + 1) * D], ALU.mult, ALU.add)
                    ins.then_inc(s["qkv_used"], 1)
                dve.wait_ge(s["qkv_used"], T * b + T)
                heads4 = lambda ap: ap.rearrange("p (t n d) -> p t n d", t=T, d=HD)
                st.done(split((heads4(q_tok), HD), qp))
                st.wait()
                split((heads4(k_tok), HD), kp).then_inc(s["parts_ready"], 1)

                def rms(src, n):
                    statistics(src)
                    st.done(dve.tensor_tensor(var[:], means, means, ALU.mult))
                    st.wait()
                    dve.scalar_tensor_tensor(var[:], var[:], EPS, variances, ALU.add, ALU.add).then_inc(s["var_ready"], 1)
                    inverse_deviation(n)

                rms(xn, 2)
                dve.wait_ge(s["qkv_c_psum"], b + 1)
                st.done(dve.memset(qpc[:, :, :, HDC:HFC], 0.0))
                st.done(dve.memset(q_parts_c[:, PC:PC + GR - GRC], 0.0))
                st.done(dve.memset(k_parts_c[:, PC:PC + GR - GRC], 0.0))
                st.done(dve.memset(kpc[:, :, 0, HDC:HFC], 1.0))
                st.done(dve.memset(kpc[:, :, 1:, HDC:HFC], 0.0))
                for t in range(T):
                    src = bank(QKV_C_BANKS[t // 2])[:, t % 2 * 3 * L:(t % 2 + 1) * 3 * L]
                    st.done(dve.tensor_scalar(qk_c[:, t * 2 * L:(t + 1) * 2 * L], src[:, 0:2 * L], rstd[:, t:t + 1], None, ALU.mult))
                    st.done(dve.tensor_scalar(v_c[:, t * L:(t + 1) * L], src[:, 2 * L:3 * L], rstd[:, t:t + 1], None, ALU.mult))
                st.wait()
                pairs = qk_c.rearrange("p (t n f two) -> p t n f two", t=T, n=2 * HEADS, two=2)
                turned_pairs = turned.rearrange("p (t n f two) -> p t n f two", t=T, n=2 * HEADS, two=2)
                left4 = spin_a[:, 0:S // 2].rearrange("p (t n f) -> p t n f", t=T, f=2)
                right4 = spin_b[:, 0:S // 2].rearrange("p (t n f) -> p t n f", t=T, f=2)
                over = lambda c: c.unsqueeze(2).to_broadcast([P, T, 2 * HEADS, 2])
                for out_half, (first, second, op) in enumerate(((cos, sin, ALU.subtract), (sin, cos, ALU.add))):
                    st.done(dve.tensor_tensor(left4, pairs[:, :, :, :, 0], over(first), ALU.mult))
                    st.done(dve.tensor_tensor(right4, pairs[:, :, :, :, 1], over(second), ALU.mult))
                    st.wait()
                    st.done(dve.tensor_tensor(turned_pairs[:, :, :, :, out_half], left4, right4, op))
                    st.wait()
                turned4 = turned.rearrange("p (t n d) -> p t n d", t=T, d=HDC)
                st.done(split((turned4[:, :, 0:HEADS, :], HDC), qpc))
                st.wait()
                split((turned4[:, :, HEADS:, :], HDC), kpc).then_inc(s["parts_c_ready"], 1)
                attentions()
                dve.wait_ge(s["proj_psum"], 2 * b + 1)
                st.done(dve.scalar_tensor_tensor(x1[:], ps[2][:], scale4[:, 3:4], x1[:], ALU.mult, ALU.add))
                st.wait()
                st.done(dve.tensor_tensor(tiles(x1[:]), tiles(x1[:]), bias4[:, 3 * D:4 * D].unsqueeze(1).to_broadcast([P, T, D]), ALU.add))
                st.wait()
                dve.wait_ge(s["proj_psum"], 2 * b + 2)
                dve.wait_ge(s["out_stored"], 16 * b + 16)
                st.done(dve.tensor_tensor(res[:], xn[:], ps[3][:], ALU.add))
                st.wait()
                st.done(dve.tensor_tensor(x1[:], x1[:], res[:], ALU.add))
                rms(res, 3)
                for t in range(T):
                    ins = dve.scalar_tensor_tensor(q_tok[:, t * D:(t + 1) * D], res[:, t * D:(t + 1) * D], rstd[:, t:t + 1], g2[:],
                                                   ALU.mult, ALU.mult)
                ins.then_inc(s["tok_ready"], 1)
                z = small[:, 0:T * E1].rearrange("p (t e) -> p t e", e=E1)
                prob = small[:, T * E0:T * E0 + T * E1].rearrange("p (t e) -> p t e", e=E1)
                wide1 = lambda c: c.unsqueeze(2).to_broadcast([P, T, E1])
                logits = ps[3][:, 0:T * E1].rearrange("p (t e) -> p t e", e=E1)
                dve.wait_ge(s["logit_psum"], 2 * b + 2)
                st.done(dve.tensor_reduce(tops[:, 0:T], logits, AX_X, ALU.max))
                st.wait()
                dve.tensor_tensor(z, logits, wide1(tops[:, 0:T]), ALU.subtract).then_inc(s["shift1_ready"], 1)
                dve.wait_ge(s["e_ready"], 2 * b + 2)
                st.done(dve.tensor_reduce(tops[:, T:2 * T], z, AX_X, ALU.add))
                st.wait()
                st.done(dve.reciprocal(tops[:, 0:T], tops[:, T:2 * T]))
                st.wait()
                st.done(dve.tensor_tensor(prob, z, wide1(tops[:, 0:T]), ALU.mult))
                st.wait()
                top2(prob, E1, rev1, 1.0, 0.0)
                mixture(2 * C0, C1, lambda c: P)
                dve.wait_ge(s["ytok_psum"], 2 * b + 2)
                dve.tensor_tensor(res[:], x1[:], ps[0][:], ALU.add).then_inc(s["x1_ready"], 1)
                assert st.n == DVE_STEPS, st.n

        @block.scalar
        def _(act):
            act.wait_ge(s["weights_in"], LOADED)
            with act.Fori(0, B) as b:
                def root(n):
                    act.wait_ge(s["var_ready"], 4 * b + n + 1)
                    act.activation(var[:], var[:], ACT.Sqrt).then_inc(s["std_ready"], 1)

                def evacuate(n, dst, rows=P):
                    act.wait_ge(s["tokT_psum"], 5 * b + n + 1)
                    act.activation(dst[0:rows, :], ps[0][0:rows, :], ACT.Copy).then_inc(s["tokT_ready"], 1)

                def mixture(base, chunks, hid_rows):
                    for n in range(2 * chunks):
                        m = hid_rows(n % chunks)
                        act.wait_ge(s["gu_psum"], STEPS * b + base + n + 1)
                        act.activation(sg[n % 2][0:m, :], ps[n % 2][0:m, 0:HALF], ACT.Silu).then_inc(s["sg_ready"], 1)

                def leave(n):
                    act.wait_ge(s["down_done"], STEPS * b + (2 * C0, STEPS)[n])
                    act.activation(yT, ps[2][:], ACT.Copy).then_inc(s["y_ready"], 1)

                def routes_out(n):
                    act.wait_ge(s["rt_psum"], 2 * b + n + 1)
                    act.activation(routeT[0:PARTS * CW, :], ps[3][0:PARTS * CW, HALF:].bitcast(BF16), ACT.Copy).then_inc(s["rt_ready"], 1)

                def stacks(g):
                    for n in range(2 + 2 * GH):
                        act.wait_ge(s["stack_psum"], (b * GROUPS + g) * (2 + 2 * GH) + n + 1)
                        src = ps[n % 2 * 2]
                        if n < 2:
                            act.activation((q_turn, k_turn)[n], src[0:GR, 0:HALF].bitcast(BF16), ACT.Copy).then_inc(s["stack_ready"], 1)
                        else:
                            act.activation((qT, kT)[n % 2][:, bass.ds((g * GH + n // 2 - 1) * S, S)], src[:],
                                           ACT.Copy).then_inc(s["stack_ready"], 1)

                def stack_queries(g, m):
                    act.wait_ge(s["qc_psum"], (b * GROUPS + g) * TURNS + m + 1)
                    if m == 0:
                        dst, src = q_turn_c, bank(SIDE_BANK)[0:GR, :].bitcast(BF16)
                    else:
                        at = g * GH * S + (m - 1) * HALF
                        dst, src = qT[:, at:at + HALF], bank(SIDE_BANK)
                    act.activation(dst, src, ACT.Copy).then_inc(s["qc_ready"], 1)

                def outputs(G):
                    act.wait_ge(s["pv_done"], CREDIT + (G + 1) * T)
                    act.activation(o_sb[:], ps[2][:], ACT.Copy).then_inc(s["o_evac"], 1)

                def group(kind, g, step):
                    G = (2 * b + kind) * GROUPS + g
                    first = (b * GROUPS + g) * NU[kind]
                    todo = plan(kind, step)
                    banks = banks_of_units(kind, step == GROUPS - 1)
                    for i, (kc, j, lo, hi) in enumerate(UNITS[kind]):
                        for what, *how in todo[i]:
                            if what == "stack" and how[2] == "q":
                                stack_queries(how[0], how[1])
                            elif what == "outputs" and how[0] == 0:
                                outputs(G - 1)
                        act.wait_ge(s[ST_PSUM[kind]], first + i + 1)
                        if j == 0:
                            act.wait_ge(s["pv_done"], CREDIT + G * T + kc - 1)
                        act.activation(slot(kc % 2 * GH + j)[:, lo:hi], bank(banks[i % len(banks)])[:, 0:hi - lo], ACT.Exp,
                                       scale=SCALES[kind]).then_inc(s[P_READY[kind]], 1)

                SCALES = float(1.0 / np.sqrt(np.float32(HD))), float(1.0 / np.sqrt(np.float32(HDC)))

                def attentions():
                    group(0, 0, 0)
                    with act.Fori(1, GROUPS - 1) as g:
                        group(0, g, 1)
                    group(0, GROUPS - 1, GROUPS - 1)
                    for g in range(GROUPS):
                        group(1, g, g)
                    outputs((2 * b + 2) * GROUPS - 1)

                root(0)
                evacuate(0, xnT)
                act.wait_ge(s["encr_psum"], b + 1)
                act.activation(encR, ps[1][:], ACT.Copy).then_inc(s["encr_ready"], 1)
                for t in range(T):
                    act.wait_ge(s["max0_ready"], b * T + t + 1)
                    if t >= 2:
                        act.wait_ge(s["pt_psum"], b * T + t - 1)
                    act.activation(p0[t % 2][:, 0:(t + 1) * P], ps[t % 2][:, 0:(t + 1) * P], ACT.Exp, bias=nmax0[:, t:t + 1],
                                   accum_out=sum0[:, t:t + 1]).then_inc(s["p0_ready"], 1)
                act.wait_ge(s["logit_psum"], 2 * b + 1)
                act.activation(small[:, 0:T * E0], ps[3][:, 0:T * E0], ACT.Exp, scale=-1.0).then_inc(s["e_ready"], 1)
                routes_out(0)
                mixture(0, C0, lambda c: P if c < C0 - 1 else M0)
                leave(0)
                root(1)
                evacuate(1, xnT)
                act.wait_ge(s["ct_psum"], b + 1)
                act.activation(cT[0:L, :], ps[2][0:L, :], ACT.Copy).then_inc(s["ct_ready"], 1)
                stacks(0)
                root(2)
                with act.Fori(1, GROUPS) as g:
                    stacks(g)
                attentions()
                evacuate(2, heads_outT)
                evacuate(3, heads_cT, L)
                root(3)
                evacuate(4, xnT)
                act.wait_ge(s["shift1_ready"], b + 1)
                act.activation(small[:, 0:T * E1], small[:, 0:T * E1], ACT.Exp).then_inc(s["e_ready"], 1)
                routes_out(1)
                mixture(2 * C0, C1, lambda c: P)
                leave(1)

        @block.tensor
        def _(pe):
            pe.wait_ge(s["weights_in"], LOADED)
            pe.wait_ge(s["setup_done"], 3)
            with pe.Fori(0, B) as b:
                def turn(n, src, width=D):
                    for t in range(T):
                        dst, tile = ps[0][0:width, t * P:(t + 1) * P], src[:, t * width:(t + 1) * width]
                        ins = pe.transpose(dst, tile, ident_f) if width == D else pe.matmul(dst, tile, ident_f, start=True, stop=True)
                    ins.then_inc(s["tokT_psum"], 1)

                def mixture(which, base, chunks, hid_rows, wg, wu, wd, spread, xT):
                    def down(n):
                        half, c = n // chunks, n % chunks
                        m = hid_rows(c)
                        pe.wait_ge(s["hid_ready"], STEPS * b + base + n + 1)
                        pe.matmul(ps[2][:, half * HALF:(half + 1) * HALF], wd[0:m, c * D:(c + 1) * D], hid[n % 2][0:m, :],
                                  start=c == 0, stop=c == chunks - 1).then_inc(s["down_done"], 1)

                    for n in range(2 * chunks):
                        half, c = n // chunks, n % chunks
                        m = hid_rows(c)
                        tok = slice(half * HALF, (half + 1) * HALF)
                        if n >= 2:
                            pe.wait_ge(s["hid_ready"], STEPS * b + base + n - 1)
                        pe.matmul(ps[n % 2][0:m, 0:HALF], wg[:, c * P:c * P + m], xT[:, tok], start=True, stop=True)
                        pe.matmul(ps[n % 2][0:m, HALF:], wu[:, c * P:c * P + m], xT[:, tok], start=True, stop=True)
                        pe.matmul(ps[3][0:m, (n % 2) * HALF:(n % 2 + 1) * HALF], spread(c, m), routeT[0:PARTS * CW, tok],
                                  start=True, stop=True).then_inc(s["gu_psum"], 1)
                        if n >= 1:
                            down(n - 1)
                    down(2 * chunks - 1)
                    pe.wait_ge(s["y_ready"], 2 * b + which + 1)
                    for t in range(T):
                        ins = pe.transpose(ps[0][:, t * P:(t + 1) * P], yT[:, t * P:(t + 1) * P], ident_f)
                    ins.then_inc(s["ytok_psum"], 1)

                def routes_in(n):
                    pe.wait_ge(s["route_ready"], 2 * b + n + 1)
                    dst = ps[3][:, HALF:].bitcast(BF16)
                    for t in range(T):
                        ins = pe.transpose(dst[0:PARTS * CW, t * P:(t + 1) * P], routes[:, t * PARTS * CW:(t + 1) * PARTS * CW], ident_b)
                    ins.then_inc(s["rt_psum"], 1)
                    pe.wait_ge(s["rt_ready"], 2 * b + n + 1)

                def turn_parts(parts, g, rows, dst):
                    for t in range(T):
                        at = (t * GROUPS + g) * rows
                        ins = pe.transpose(dst[0:GR, t * P:(t + 1) * P], parts[:, at:at + GR], ident_b)
                    return ins

                def stacks(g, n):
                    pe.wait_ge(s["stack_ready"], (b * GROUPS + g) * (2 + 2 * GH) + n - 1 + CREDIT)
                    dst = ps[n % 2 * 2]
                    if n < 2:
                        ins = turn_parts((q_parts, k_parts)[n], g, GR, dst[:, 0:HALF].bitcast(BF16))
                    else:
                        j = n // 2 - 1
                        for half in range(2):
                            ins = pe.matmul(dst[:, half * HALF:(half + 1) * HALF], (pick_q, pick_k)[n % 2][0:GR, j * P:(j + 1) * P],
                                            (q_turn, k_turn)[n % 2][:, half * HALF:(half + 1) * HALF], start=True, stop=True)
                    ins.then_inc(s["stack_psum"], 1)

                def stacks_c(g, m, side):
                    count = (b * GROUPS + g) * TURNS + m
                    if side == "q":
                        if m >= 1 or g >= 1:
                            pe.wait_ge(s["qc_ready"], count)
                        if g >= 1:
                            pe.wait_ge(s["kc_ready"], count + CREDIT)
                        parts, pick, turned_parts, done = q_parts_c, pick_qc, q_turn_c, "qc_psum"
                    else:
                        if g >= 1:
                            pe.wait_ge(s["qc_ready"], count + 1)
                        else:
                            pe.wait_ge(s["kc_ready"], count + CREDIT)
                        parts, pick, turned_parts, done = k_parts_c, pick_kc, k_turn_c, "kc_psum"
                    if m == 0:
                        ins = turn_parts(parts, g, GRC, side_bank(g, side).bitcast(BF16))
                    else:
                        j, half = (m - 1) // 2, (m - 1) % 2
                        ins = pe.matmul(side_bank(g, side), pick[0:GR, j * P:(j + 1) * P],
                                        turned_parts[:, half * HALF:(half + 1) * HALF], start=True, stop=True)
                    ins.then_inc(s[done], 1)

                def head(stacked, g, j):
                    return stacked[:, bass.ds((g * GH + j) * S, S)]

                def piece(kind, g, i):
                    j, t, half, lo, hi = PIECES[kind][i]
                    n = hi - lo
                    dst, gone = piece_bank(kind, i)
                    if i >= gone and not (kind == 0 and i == EARLY):
                        pe.wait_ge(s["max_done"], CREDIT + pieces_before(b, kind, g) + i - gone + 1)
                    ins = pe.matmul(dst[:, 0:n], head(qT, g, j)[:, t * P:(t + 1) * P], head(kT, g, j)[:, lo:hi], start=True, stop=True)
                    if kind == 1 and hi == (t + 1) * P:
                        ins = pe.matmul(dst[:, n - P:n], ident_b, mask_q, start=False, stop=True, skip_group_check=True)
                    ins.then_inc(s["s_psum"], 1)

                def maxima(kind, g):
                    pe.wait_ge(s["m_split"], (2 * b + kind) * GROUPS + g + 1)
                    dst = piece_bank(kind, NP[kind])[0][0:MR, :].bitcast(BF16)
                    for t in range(T):
                        ins = pe.transpose(dst[:, t * P:(t + 1) * P], m_parts[:, t * MR:(t + 1) * MR], ident_b)
                    ins.then_inc(s["mt_psum"], 1)

                def scores(kind, g, i, banks):
                    kc, j, lo, hi = UNITS[kind][i]
                    dst = bank(banks[i % len(banks)])
                    if i >= len(banks):
                        pe.wait_ge(s[P_READY[kind]], (b * GROUPS + g) * NU[kind] + i - len(banks) + 1)
                    ins = pe.matmul(dst[:, 0:hi - lo], head(kT, g, j)[:, kc * P:(kc + 1) * P], head(qT, g, j)[:, lo:hi], start=True, stop=True)
                    if kind == 1 and lo == kc * P:
                        ins = pe.matmul(dst[:, 0:P], ident_b, mask_k, start=False, stop=True, skip_group_check=True)
                    ins.then_inc(s[ST_PSUM[kind]], 1)

                def values(kind, g, kc, half):
                    lo, hi = max(kc * P if kind == 1 else 0, half * HALF), (half + 1) * HALF
                    if lo >= hi:
                        return
                    if kc == 0 and half == 0:
                        pe.wait_ge(s["v_staged"], (2 * b + kind) * GROUPS + g + 1)
                    done = sum(unit[0] <= kc for unit in UNITS[kind])
                    pe.wait_ge(s[P_READY[kind]], (b * GROUPS + g) * NU[kind] + done)
                    for j in range(GH):
                        ins = pe.matmul(ps[2][CW * j:CW * (j + 1), lo:hi], v_st[:, kc, j, :], slot(kc % 2 * GH + j)[:, lo:hi],
                                        start=kc == 0, stop=kc == T - 1, skip_group_check=True)
                    if half == 1:
                        ins.then_inc(s["pv_done"], 1)

                def outputs(G, half):
                    if half == 0:
                        pe.wait_ge(s["norm_done"], CREDIT + G)
                        pe.wait_ge(s["o_evac"], G + 1)
                    for t in range(half * T // 2, (half + 1) * T // 2):
                        ins = pe.matmul(bank(SIDE_BANK)[:, OC * t:OC * (t + 1)], o_sb[:, t * P:(t + 1) * P], pick_o, start=True, stop=True)
                    if half == 1:
                        ins.then_inc(s["ot_psum"], 1)

                def group(kind, g, step):
                    G = (2 * b + kind) * GROUPS + g
                    after, later = (kind, g + 1) if step < GROUPS - 1 else (1, 0)
                    before = (kind, g - 1) if step > 0 else (0, GROUPS - 1)
                    todo = plan(kind, step)
                    banks = banks_of_units(kind, step == GROUPS - 1)
                    for i in range(NU[kind] + 1):
                        if i == 1:
                            pe.wait_ge(s["m_rows"], 16 * GH * (G + 1))
                        if i >= 1:
                            kc, j, lo, hi = UNITS[kind][i - 1]
                            scores(kind, g, i - 1, banks)
                            if kc >= 1 and hi == S and j % 2 == 1:
                                values(kind, g, kc - 1, j // 2)
                        for what, *how in todo[i]:
                            if what == "values":
                                values(*before, T - 1, how[0])
                            elif what == "outputs":
                                outputs(G - 1, how[0])
                            elif what == "stack":
                                if how[:] == [0, 0, "k"]:
                                    pe.wait_ge(s["mt_ready"], G + 1)
                                if how[1:] == [0, "q"]:
                                    pe.wait_ge(s["norm_done"], CREDIT + G)
                                stacks_c(*how)
                            elif what == "piece":
                                if how[0] == 0:
                                    pe.wait_ge(s["mt_ready"], G + 1)
                                if how[0] == 0 and after == 1:
                                    pe.wait_ge(s["qc_ready"], (b * GROUPS + later + 1) * TURNS)
                                    pe.wait_ge(s["kc_ready"], (b * GROUPS + later + 1) * TURNS + CREDIT)
                                if how[0] == EARLY and after == 0 and step > 0:
                                    pe.wait_ge(s["norm_done"], CREDIT + G)
                                piece(after, later, how[0])
                            else:
                                maxima(after, later)

                def attentions():
                    pe.wait_ge(s["parts_ready"], b + 1)
                    each = 2 + 2 * GH
                    for n in range(each):
                        stacks(0, n)
                    pe.wait_ge(s["stack_ready"], CREDIT + b * GROUPS * each + each)
                    pe.wait_ge(s["parts_c_ready"], b + 1)
                    out = each
                    for i in range(NP[0]):
                        piece(0, 0, i)
                        while out - each < (GROUPS - 1) * each * (i + 1) // NP[0]:
                            stacks(out // each, out % each)
                            out += 1
                    maxima(0, 0)
                    pe.wait_ge(s["stack_ready"], CREDIT + (b + 1) * GROUPS * each)
                    group(0, 0, 0)
                    with pe.Fori(1, GROUPS - 1) as g:
                        group(0, g, 1)
                    group(0, GROUPS - 1, GROUPS - 1)
                    for g in range(GROUPS):
                        group(1, g, g)
                    values(1, GROUPS - 1, T - 1, 0)
                    values(1, GROUPS - 1, T - 1, 1)

                pe.wait_ge(s["tok_ready"], 3 * b + 1)
                turn(0, xn)
                pe.wait_ge(s["tokT_ready"], 5 * b + 1)
                for half in range(2):
                    ins = pe.matmul(ps[1][:, half * HALF:(half + 1) * HALF], R_w[:], xnT[:, half * HALF:(half + 1) * HALF], start=True, stop=True)
                ins.then_inc(s["encr_psum"], 1)
                pe.wait_ge(s["encr_ready"], b + 1)

                def scores0(t):
                    if t >= 2:
                        pe.wait_ge(s["p0_ready"], b * T + t - 1)
                    keys = (t + 1) * P
                    for lo in range(0, keys, HALF):
                        hi = min(keys, lo + HALF)
                        pe.matmul(ps[t % 2][:, lo:hi], encR[:, t * P:(t + 1) * P], xnT[:, lo:hi], start=True, stop=True)
                    pe.matmul(ps[t % 2][:, t * P:keys], ident_b, mask_q, start=False, stop=True, skip_group_check=True).then_inc(s["s0_psum"], 1)

                scores0(0)
                for t in range(T):
                    if t + 1 < T:
                        scores0(t + 1)
                    pe.wait_ge(s["p0_ready"], b * T + t + 1)
                    if t >= 1:
                        pe.wait_ge(s["pt_ready"], b * T + t)
                    for j in range(t + 1):
                        ins = pe.transpose(ps[2][:, j * P:(j + 1) * P], p0[t % 2][:, j * P:(j + 1) * P], ident_f)
                    ins.then_inc(s["pt_psum"], 1)
                    pe.wait_ge(s["pt_ready"], b * T + t + 1)
                    if t >= 2:
                        pe.wait_ge(s["o0_used"], b * T + t - 1)
                    for j in range(t + 1):
                        ins = pe.matmul(ps[3][:, (t % 2) * HALF:(t % 2) * HALF + D], pT0[:, j * P:(j + 1) * P], xn[:, j * D:(j + 1) * D],
                                        start=j == 0, stop=j == t)
                    ins.then_inc(s["o0_psum"], 1)
                pe.wait_ge(s["o0_used"], b * T + T)
                for t in range(T):
                    ins = pe.matmul(ps[3][:, t * E0:(t + 1) * E0], xnT[:, t * P:(t + 1) * P], gate0[:], start=True, stop=True)
                ins.then_inc(s["logit_psum"], 1)
                routes_in(0)
                mixture(0, 0, C0, lambda c: P if c < C0 - 1 else M0, wg0, wu0, wd0,
                        lambda c, m: sel0[0:PARTS * CW, c * P:c * P + m], xnT)
                pe.wait_ge(s["tok_ready"], 3 * b + 2)
                turn(1, xn)
                pe.wait_ge(s["tokT_ready"], 5 * b + 2)
                for half in range(2):
                    ins = pe.matmul(ps[2][0:L, half * HALF:(half + 1) * HALF], w_down[:], xnT[:, half * HALF:(half + 1) * HALF], start=True, stop=True)
                ins.then_inc(s["ct_psum"], 1)
                for t in range(T):
                    if t >= 2:
                        pe.wait_ge(s["qkv_used"], T * b + t - 1)
                    pe.matmul(bank(t % 2)[:, 0:3 * D], xnT[:, t * P:(t + 1) * P], wqkv[:], start=True, stop=True).then_inc(s["qkv_psum"], 1)
                pe.wait_ge(s["ct_ready"], b + 1)
                for t in range(T):
                    ins = pe.matmul(bank(QKV_C_BANKS[t // 2])[:, t % 2 * 3 * L:(t % 2 + 1) * 3 * L], cT[0:L, t * P:(t + 1) * P], wqkv1[0:L, :],
                                    start=True, stop=True)
                ins.then_inc(s["qkv_c_psum"], 1)
                attentions()
                turn(2, heads_out)
                outputs((2 * b + 2) * GROUPS - 1, 0)
                outputs((2 * b + 2) * GROUPS - 1, 1)
                pe.wait_ge(s["tokT_ready"], 5 * b + 3)
                for t in range(T):
                    ins = pe.matmul(ps[2][:, t * D:(t + 1) * D], heads_outT[:, t * P:(t + 1) * P], wo[:], start=True, stop=True)
                ins.then_inc(s["proj_psum"], 1)
                pe.wait_ge(s["norm_done"], CREDIT + (2 * b + 2) * GROUPS)
                turn(3, heads_c, L)
                pe.wait_ge(s["tokT_ready"], 5 * b + 4)
                for t in range(T):
                    ins = pe.matmul(ps[3][:, t * D:(t + 1) * D], heads_cT[:, t * P:(t + 1) * P], w_up[0:L, :], start=True, stop=True)
                ins.then_inc(s["proj_psum"], 1)
                pe.wait_ge(s["tok_ready"], 3 * b + 3)
                turn(4, q_tok)
                pe.wait_ge(s["tokT_ready"], 5 * b + 5)
                for t in range(T):
                    ins = pe.matmul(ps[3][:, t * E1:(t + 1) * E1], xnT[:, t * P:(t + 1) * P], router[:], start=True, stop=True)
                ins.then_inc(s["logit_psum"], 1)
                routes_in(1)
                mixture(1, 2 * C0, C1, lambda c: P, wg1, wu1, wd1, lambda c, m: sel1[0:PARTS * CW, (c // 2) * P:(c // 2) * P + m], xnT)


def kernel(**inputs):
    import ml_dtypes
    import concourse.bacc as bacc
    from concourse.bass_utils import run_bass_kernel_spmd as run

    i = {k: np.asarray(v) for k, v in inputs.items()}
    cb, cf = constants()
    side = lambda w: w.transpose(1, 0, 2).reshape(w.shape[1], -1)
    rows = lambda w: w.reshape(-1, P, D).transpose(1, 0, 2).reshape(P, -1)
    a = {
        "const_b": cb.astype(ml_dtypes.bfloat16), "const_f": cf,
        "x": i["L0_attn_encoding"], "R": i["L0_attn_R"], "gate0": i["L0_ffn_gate_w"].T,
        "wg0": np.concatenate([side(i["L0_ffn_w_gate"]), i["L0_ffn_ws_gate"]], axis=1),
        "wu0": np.concatenate([side(i["L0_ffn_w_up"]), i["L0_ffn_ws_up"]], axis=1),
        "wd0a": rows(i["L0_ffn_w_down"].reshape(-1, D)), "wd0b": i["L0_ffn_ws_down"],
        "wqkv": np.concatenate([i[f"L1_attn_w_{n}"].T for n in "qkv"], axis=1), "wo": i["L1_attn_w_o"].T,
        "scale4": np.stack([i[f"L1_attn_s_{n}"].reshape(()) for n in "qkvo"]),
        "bias4": np.concatenate([i[f"L1_attn_b_{n}"] for n in "qkvo"]),
        "g1": i["L1_ffn_g1"].reshape(D, 1), "g2": i["L1_ffn_g2"],
        "w_down": i["L1_ffn_w_down"], "wqkv1": np.concatenate([i[f"L1_ffn_w{n}"] for n in "qkv"], axis=1),
        "w_up": i["L1_ffn_w_up"], "router": i["L1_ffn_router_w"],
        "wg1": side(i["L1_ffn_w1"]), "wu1": side(i["L1_ffn_w3"]), "wd1": rows(i["L1_ffn_w2"].reshape(-1, D)),
    }
    nc = bacc.Bacc("TRN2", target_bir_lowering=False, num_devices=1)
    arrays, h = {}, {}
    for name, v in a.items():
        v = np.ascontiguousarray(v)
        arrays[f"in_{name}"] = v
        h[name] = nc.dram_tensor(f"in_{name}", v.shape, mybir.dt.from_np(v.dtype), kind="ExternalInput").ap()
    h["out"] = nc.dram_tensor("out_0", (B, S, D), F32, kind="ExternalOutput").ap()
    build(nc, h)
    r = run(nc, [arrays], core_ids=[0])
    return r.results[0]["out_0"]
```

```python
from contextlib import ExitStack

import numpy as np

import concourse.bass as bass
from concourse import mybir

F32 = mybir.dt.float32
BF16 = mybir.dt.bfloat16
ALU = mybir.AluOpType
ACT = mybir.ActivationFunctionType
AX_X = mybir.AxisListType.X

P = 128
B, S, D = 4, 1024, 128
T = S // P
HALF = 512
HEADS = 16
PARTS = 3
HD = 8
HF = HD + 1
HDC = 4
HFC = HDC + 1
ROWS = PARTS * PARTS * HF
ROWSC = PARTS * PARTS * HFC
GH = 4
GROUPS = HEADS // GH
GR = GH * PARTS * HF
GRC = GH * PARTS * HFC
CW = P // GH
OC = GH * HF
MR = GH * PARTS
E0, M0 = 16, 64
E1, M1 = 8, 256
L = 64
C0 = (E0 + 1) * M0 // P + 1
C1 = E1 * M1 // P
CHUNKS = C0 + C1
STEPS = 2 * CHUNKS
EPS = 1e-5
ROUTE_SCALE = 2.5
ROUTE_EPS = 1e-20
NEG = -1e30
THETA = 10000.0


def constants():
    i = np.arange(P)
    mask_q = np.where(i[None, :] <= i[:, None], 0.0, NEG)
    mask_k = mask_q.T
    sel0 = np.zeros((P, (E0 + 1) * M0))
    sel1 = np.zeros((P, E1 * P))
    for a in range(PARTS):
        for e in range(E0 + 1):
            sel0[CW * a + e, e * M0:(e + 1) * M0] = 1.0
        for e in range(E1):
            sel1[CW * a + e, e * P:(e + 1) * P] = 1.0
    picks = []
    for features in (HF, HFC):
        stacked, pick_q, pick_k = np.arange(PARTS * PARTS * features).reshape(PARTS, PARTS, features), *np.zeros((2, P, GH, P))
        for j in range(GH):
            for part in range(PARTS):
                for d in range(features):
                    row = (j * PARTS + part) * features + d
                    pick_q[row, j, stacked[part, :, d]] = 1.0
                    pick_k[row, j, stacked[:, part, d]] = 1.0
        picks += [pick_q.reshape(P, -1), pick_k.reshape(P, -1)]
    cb = np.concatenate([np.eye(P), mask_q, mask_k, *picks, sel0, sel1], axis=1)
    pick_o = np.zeros((P, GH, HF))
    for j in range(GH):
        pick_o[CW * j + np.arange(HF), j, np.arange(HF)] = 1.0
    pos = (np.arange(T)[None, :] * P + i[:, None]).astype(np.float32)
    inv = (np.float32(1.0) / np.float32(THETA) ** (np.arange(0, 4, 2, dtype=np.float32) / np.float32(4))).astype(np.float32)
    ang = (pos[:, :, None] * inv[None, None, :]).astype(np.float32)
    rev0 = np.tile(E0 - np.arange(E0), (P, 1))
    rev1 = np.tile(E1 - np.arange(E1), (P, 1))
    cf = np.concatenate([np.eye(P), pick_o.reshape(P, -1), np.cos(ang).reshape(P, -1), np.sin(ang).reshape(P, -1), rev0, rev1], axis=1)
    return cb, np.ascontiguousarray(cf.astype(np.float32))


class Steps:

    def __init__(self, eng, sem, base):
        self.eng, self.sem, self.base, self.n = eng, sem, base, 0

    def done(self, ins):
        ins.then_inc(self.sem, 1)
        self.n += 1

    def wait(self):
        self.eng.wait_ge(self.sem, self.base + self.n)


def build(nc, h):
    with ExitStack() as ctx:
        def sb(name, cols, dt=F32):
            return ctx.enter_context(nc.sbuf_tensor(name, [P, cols], dt))

        def sem(name):
            return ctx.enter_context(nc.semaphore(name))

        cb_cols, cf_cols = h["const_b"].shape[1], h["const_f"].shape[1]
        const_b = sb("const_b", cb_cols, BF16)
        const_f = sb("const_f", cf_cols)
        ident_b, mask_q, mask_k = (const_b[:, k * P:(k + 1) * P] for k in range(3))
        picks, at = [], 3 * P
        for _ in range(4):
            picks.append(const_b[:, at:at + GH * P])
            at += GH * P
        pick_q, pick_k, pick_qc, pick_kc = picks
        sel0 = const_b[:, at:at + (E0 + 1) * M0]
        sel1 = const_b[:, at + (E0 + 1) * M0:]
        ident_f = const_f[:, 0:P]
        pick_o = const_f[:, P:P + OC]
        cos = const_f[:, P + OC:P + OC + 2 * T].rearrange("p (t f) -> p t f", f=2)
        sin = const_f[:, P + OC + 2 * T:P + OC + 4 * T].rearrange("p (t f) -> p t f", f=2)
        rev0 = const_f[:, P + OC + 4 * T:P + OC + 4 * T + E0]
        rev1 = const_f[:, P + OC + 4 * T + E0:]
        R_w = sb("R_w", D)
        gate0 = sb("gate0", E0)
        wg0 = sb("wg0", (E0 + 1) * M0)
        wu0 = sb("wu0", (E0 + 1) * M0)
        wd0 = sb("wd0", C0 * D)
        wqkv = sb("wqkv", 3 * D)
        wo = sb("wo", D)
        scale4 = sb("scale4", 4)
        bias4 = sb("bias4", 4 * D)
        g1 = sb("g1", 1)
        g2 = sb("g2", D)
        w_down = sb("w_down", L)
        wqkv1 = sb("wqkv1", 3 * L)
        w_up = sb("w_up", D)
        router = sb("router", E1)
        wg1 = sb("wg1", E1 * M1)
        wu1 = sb("wu1", E1 * M1)
        wd1 = sb("wd1", C1 * D)
        x_b = sb("x_b", S)
        xn = sb("xn", S)
        xnT = sb("xnT", S)
        x1 = sb("x1", S)
        res = sb("res", S)
        qkv = sb("qkv", 3 * S)
        buf = sb("buf", T * S)
        q_parts = sb("q_parts", T * HEADS * PARTS * HF, BF16)
        k_parts = sb("k_parts", T * HEADS * PARTS * HF, BF16)
        qT = sb("qT", HEADS * S, BF16)
        kT = sb("kT", HEADS * S, BF16)
        v_ones = sb("v_ones", T * GH * CW)
        o_sb = sb("o_sb", S)
        stats = sb("stats", T * 6)
        mv = sb("mv", T * 3)
        var = sb("var", T)
        rstd = sb("rstd", T)
        rstd_c = sb("rstd_c", T)
        tops = sb("tops", 8 * T)
        nmax = sb("nmax", 2 * T * GH)
        m_rest = sb("m_rest", T * GH)
        m_parts = sb("m_parts", T * MR, BF16)
        rsum_g = sb("rsum_g", T * GH)
        nmax0 = sb("nmax0", T)
        sum0 = sb("sum0", T)
        rsum = sb("rsum", T)
        routes = sb("routes", T * PARTS * CW, BF16)

        slot = lambda n: buf[:, n * S:(n + 1) * S]
        p0 = [slot(0), slot(1)]
        pT0 = slot(2)
        encR = slot(3)
        sg = [slot(4)[:, 0:HALF], slot(4)[:, HALF:]]
        gu = [slot(5)[:, 0:HALF], slot(5)[:, HALF:]]
        hid = [slot(6)[:, 0:HALF], slot(6)[:, HALF:]]
        yT = slot(7)
        routeT = kT[:, 0:S]
        tT = qT[:, 0:2 * S].bitcast(F32)
        rest = slot(0)
        small = slot(1)[:, 0:6 * T * E0]
        spin_a, spin_b = slot(1), slot(2)
        cT, qk_c, turned = slot(3), slot(4), slot(5)
        q_turn = slot(6)[0:GR, 0:HALF].bitcast(BF16)
        k_turn = slot(6)[0:GR, HALF:].bitcast(BF16)
        q_tok, k_tok, v_tok = (qkv[:, n * S:(n + 1) * S] for n in range(3))
        heads_out, heads_outT = q_tok, k_tok
        heads_c = v_tok[:, 0:T * L]
        heads_cT = slot(5)[0:L, :]
        xn0 = qT[:, 2 * S:4 * S].bitcast(F32)
        x0 = kT[:, 2 * S:4 * S].bitcast(F32)
        k_rest = slot(7)
        mT = k_tok[:, 0:HALF].bitcast(BF16)
        v_c = k_tok[:, HALF:]
        q_parts_c, k_parts_c = x_b[:].bitcast(BF16), xnT[:].bitcast(BF16)
        PC = T * GROUPS * GRC
        qpc = q_parts_c[:, 0:PC].rearrange("p (n a d) -> p n a d", a=PARTS, d=HFC)
        kpc = k_parts_c[:, 0:PC].rearrange("p (n a d) -> p n a d", a=PARTS, d=HFC)
        q_turn_c, k_turn_c = q_parts[0:GR, 0:S], q_parts[0:GR, S:2 * S]
        qp = q_parts[:].rearrange("p (n a d) -> p n a d", a=PARTS, d=HF)
        kp = k_parts[:].rearrange("p (n a d) -> p n a d", a=PARTS, d=HF)
        heads4 = lambda ap: ap.rearrange("p (t n d) -> p t n d", t=T, d=HD)
        turned4 = turned.rearrange("p (t n d) -> p t n d", t=T, d=HDC)
        v_st = v_ones[:].rearrange("p (k j c) -> p k j c", j=GH, c=CW)
        mp = m_parts[:].rearrange("p (t j a) -> p t j a", a=PARTS, j=GH)
        rt = routes[:].rearrange("p (t a e) -> p t a e", a=PARTS, e=CW)

        def splits(kind):
            hd = (HD, HDC)[kind]
            sources = (heads4(q_tok), heads4(k_tok)) if kind == 0 else (turned4[:, :, 0:HEADS, :], turned4[:, :, HEADS:, :])
            left = [ap[:, 0:HEADS * T * hd].rearrange("p (t n d) -> p t n d", t=T, d=hd) for ap in (rest, k_rest)]
            parts = [lambda part, to=to: to[:, :, part, 0:hd].rearrange("p (t n) d -> p t n d", t=T)
                     for to in ((qp, kp), (qpc, kpc))[kind]]
            return list(zip(sources, left, parts))

        ps = [ctx.enter_context(nc.psum_tensor(f"ps{n}", [P, S], F32)) for n in range(4)]

        names = """first_in weights_in x_in out_stored setup_done var0_ready std0_ready var_ready std_ready
        x_norm_ready xT_psum xT_ready tok_ready tokT_psum tokT_ready
        encr_psum encr_ready s0_psum max0_ready p0_ready pt_psum pt_ready o0_psum o0_used
        logit_psum shift1_ready e_ready route_ready rt_psum rt_ready gu_psum spread_psum sg_ready gu_ready hid_ready down_done
        y_ready ytok_psum out_ready qkv_psum qkv_used ct_psum ct_ready qkv_c_psum turned_ready part_done left_done
        stack_psum stack_ready qc_psum qc_ready kc_psum kc_ready
        s_psum max_done m_steps m_split mt_psum mt_ready m_rows st_psum st_psum_causal p_ready p_ready_causal pv_done o_evac ot_psum
        norm_done v_staged proj_psum dve_steps front_steps rsum_done""".split()
        s = {n: sem(n) for n in names}
        block = ctx.enter_context(nc.Block())

        N_FIRST = 4
        N_WEIGHTS = 17
        CREDIT = 2
        DVE_STEPS = 91
        FRONT_STEPS = 45
        M_STEPS = 5
        TURN_X, ENCODE, TILES, LOGITS = 2, 3, 4, 4 + 3 * T
        FRONT = LOGITS + 1
        ROUTES = 5
        AHEAD = 10
        FRONT_PS = 3
        Y_BANK, SPREAD_BANK, LOGIT_BANK = 4, 5, 2

        def front_stages(step):
            count = FRONT + ROUTES - AHEAD
            return [AHEAD + k for k in range(count) if k * 2 * C1 // count == step]
        QKV_BANKS = (0, 1, 2, 3, 6, 7)
        QKV_C_BANKS = (2, 3, 6, 7)

        PIECES = [[(j, t, half, lo, min(lo + HALF, (t + 1) * P if causal else S))
                   for j in range(GH) for t in range(T) for half, lo in enumerate(range(0, (t + 1) * P if causal else S, HALF))]
                  for causal in (False, True)]
        UNITS = [[(kc, j, max(kc * P, half * HALF) if causal else half * HALF, (half + 1) * HALF)
                  for kc in range(T) for j in range(GH) for half in range(2) if not (causal and kc * P >= (half + 1) * HALF)]
                 for causal in (False, True)]
        NP, NU = [len(p) for p in PIECES], [len(u) for u in UNITS]
        UNIT_BANKS = (0, 1, 2), (0, 1)
        PIECE_BANKS, MORE_BANK = (6, 7), 2
        LAST_BANKS = (0, 1, 2) + PIECE_BANKS
        SIDE_BANK = 3
        PRELUDE, EARLY = 10, 12

        def bank(n):
            return ps[n // 2][:, n % 2 * HALF:(n % 2 + 1) * HALF]

        def banks_of_units(kind, last):
            return LAST_BANKS if kind == 1 and last else UNIT_BANKS[kind]

        def piece_bank(kind, g, i):
            if kind == 1 and g > 0:
                return bank((PIECE_BANKS + (MORE_BANK,))[i % 3]), 3
            if kind == 1 or i < EARLY:
                return bank(PIECE_BANKS[i % 2]), 2
            return bank(((SIDE_BANK,) + PIECE_BANKS)[i % 3]), 3

        def side_bank(g, side, m):
            return bank(((0, 2) if side == "q" else (1, PIECE_BANKS[0]))[m % 2] if g == 0 else SIDE_BANK)

        TURNS = 2 * GH + 1

        def plan(kind, g):
            todo = [[] for _ in range(NU[kind] + 1)]

            def spread(items, lo, hi):
                for k, item in enumerate(items):
                    todo[lo + k * (hi - lo) // len(items)].append(item)

            first, last = (kind, g) == (0, 0), (kind, g) == (1, GROUPS - 1)
            after = kind if g < GROUPS - 1 else 1
            pieces = [] if last else [("piece", i) for i in range(NP[after])]
            end = [("values", 0), ("values", 1), ("outputs", 0), ("outputs", 1)] if not first else []
            if (kind, g) == (0, GROUPS - 1):
                ahead = [("stack", 0, m, side) for m in range(TURNS) for side in "qk"]
                todo[0] = end[:2] + ahead[:6] + end[2:] + ahead[6:]
                spread([("stack", 1, m, side) for m in range(TURNS) for side in "qk"], 4, 60)
                spread(pieces, 2, 57)
                todo[59].append(("maxima", 0))
            else:
                todo[0] = end[:1] + pieces[:2] + end[1:2] + pieces[2:6] + end[2:3] + pieces[6:8] + end[3:] + pieces[8:PRELUDE]
                hi = (55, 41)[kind]
                if kind == 1 and g < 2:
                    spread([("stack", g + 2, m, side) for m in range(TURNS) for side in "qk"], 4, 44)
                spread(pieces[PRELUDE:], 2, hi)
                if pieces:
                    todo[hi + 1].append(("maxima", 0))
            return todo

        ST_PSUM, P_READY = ("st_psum", "st_psum_causal"), ("p_ready", "p_ready_causal")

        def pieces_before(b, kind, g):
            return b * GROUPS * sum(NP) + kind * GROUPS * NP[0] + g * NP[kind]

        @block.sync
        def _(sp):
            loads = [(const_b[:], h["const_b"]), (const_f[:], h["const_f"]), (R_w[:], h["R"]), (gate0[:], h["gate0"]),
                     (wg0[:], h["wg0"]), (wu0[:], h["wu0"]), (wd0[:, 0:(C0 - 1) * D], h["wd0a"]), (wd0[0:M0, (C0 - 1) * D:], h["wd0b"]),
                     (wqkv[:], h["wqkv"]), (wo[:], h["wo"]), (scale4[:], h["scale4"].partition_broadcast(P)),
                     (bias4[:], h["bias4"].partition_broadcast(P)), (g1[:], h["g1"]), (g2[:], h["g2"].partition_broadcast(P)),
                     (w_down[:], h["w_down"]), (wqkv1[0:L, :], h["wqkv1"]), (w_up[0:L, :], h["w_up"]), (router[:], h["router"]),
                     (wg1[:], h["wg1"]), (wu1[:], h["wu1"]), (wd1[:], h["wd1"])]
            x_view = h["x"].rearrange("b (t p) d -> b p t d", p=P)
            out_view = h["out"].rearrange("b (t p) d -> b p t d", p=P)
            sp.dma_start(x_b[:].rearrange("p (t d) -> p t d", d=D), x_view[0]).then_inc(s["x_in"], 16)
            assert len(loads) == N_FIRST + N_WEIGHTS
            for n, (dst, src) in enumerate(loads):
                sp.dma_start(dst, src).then_inc(s["first_in" if n < N_FIRST else "weights_in"], 16)
            def store(b):
                sp.wait_ge(s["out_ready"], CREDIT + b + 1)
                sp.dma_start(out_view[bass.ds(b, 1)].rearrange("b p t d -> (b p) t d"),
                             res[:].rearrange("p (t d) -> p t d", d=D)).then_inc(s["out_stored"], 16)

            def max_rows(b):
                for kind, features in enumerate((HF, HFC)):
                    a = 2 * b + kind
                    with sp.Fori(0, GROUPS) as g:
                        sp.wait_ge(s["mt_ready"], a * GROUPS + g + 1)
                        for j in range(GH):
                            rows = slice(features - 1, features + 2 * PARTS * features, PARTS * features)
                            sp.dma_start(qT[rows, bass.ds((g * GH + j) * S, S)], mT[j * PARTS:(j + 1) * PARTS, :]).then_inc(s["m_rows"], 16)

            with sp.Fori(0, B - 1) as b:
                max_rows(b)
                sp.wait_ge(s["qc_psum"], (b + 1) * GROUPS * TURNS)
                sp.dma_start(x_b[:].rearrange("p (t d) -> p t d", d=D),
                             x_view[bass.ds(b + 1, 1)].rearrange("b p t d -> (b p) t d")).then_inc(s["x_in"], 16)
                store(b)
            max_rows(B - 1)
            store(B - 1)
            sp.wait_ge(s["out_stored"], 16 * B + 16)

        @block.gpsimd
        def _(pool):
            with pool.Fori(0, B) as b:
                for kind, (ready, values, hd) in enumerate(((1, v_tok, HD), (2, v_c, HDC))):
                    a = 2 * b + kind
                    with pool.Fori(0, GROUPS) as g:
                        pool.wait_ge(s["left_done"], (2 * b + ready) * 2 * (PARTS - 1))
                        pool.wait_ge(s["pv_done"], CREDIT + (a * GROUPS + g) * T)
                        pool.tensor_copy(v_st[:, :, :, 0:hd], values.rearrange("p (t n) -> p t n", t=T)
                                         [:, :, bass.ds(g * GH * hd, GH * hd)].rearrange("p t (j c) -> p t j c", c=hd)).then_inc(s["v_staged"], 1)

        @block.vector
        def _(dve):
            dve.memset(v_ones[:], 0.0).then_inc(s["max_done"], CREDIT)
            dve.memset(routes[:], 0.0).then_inc(s["pv_done"], CREDIT)
            dve.memset(kp[:, :, 1:, HD:HF], 0.0).then_inc(s["norm_done"], CREDIT)
            dve.memset(kp[:, :, 0, HD:HF], 1.0).then_inc(s["kc_ready"], CREDIT)
            dve.memset(nmax0[:], 0.0).then_inc(s["out_ready"], CREDIT)
            dve.memset(tops[:, 0:T], 0.0).then_inc(s["out_stored"], 16)
            dve.memset(tops[:, T:], 0.0).then_inc(s["stack_ready"], CREDIT)
            dve.wait_ge(s["max_done"], CREDIT)
            dve.wait_ge(s["pv_done"], CREDIT)
            dve.memset(rt[:, :, 0, E0:E0 + 1], 1.0).then_inc(s["setup_done"], 1)
            dve.memset(v_st[:, :, :, HD:HF], 1.0).then_inc(s["setup_done"], 1)
            dve.wait_ge(s["first_in"], 16 * N_FIRST)

            def tiles(ap):
                return ap.rearrange("p (t c) -> p t c", t=T)

            def half_statistics(st, src, half):
                for t in range(half * T // 2, (half + 1) * T // 2):
                    st.done(dve.bn_stats(stats[:, 6 * t:6 * t + 6], src[:, t * D:(t + 1) * D]))

            def statistics(st, src):
                half_statistics(st, src, 0)
                half_statistics(st, src, 1)
                join_statistics(st)

            def join_statistics(st):
                st.wait()
                even, odd = field[:, :, 1], field[:, :, 4]
                st.done(dve.tensor_tensor(means, even, odd, ALU.add))
                st.done(dve.tensor_tensor(apart, even, odd, ALU.subtract))
                st.done(dve.tensor_tensor(variances, field[:, :, 2], field[:, :, 5], ALU.add))
                st.wait()
                st.done(dve.tensor_scalar(means, means, 0.5, None, ALU.mult))
                st.done(dve.scalar_tensor_tensor(apart, apart, 0.25, apart, ALU.mult, ALU.mult))
                st.wait()
                st.done(dve.scalar_tensor_tensor(variances, variances, 1.0 / D, apart, ALU.mult, ALU.add))
                st.wait()

            field = stats[:].rearrange("p (t k) -> p t k", k=6)
            means, variances, apart = (mv[:, n * T:(n + 1) * T] for n in range(3))

            def inverse_deviation(st, root_done, count, dst=rstd):
                dve.wait_ge(s[root_done], count)
                st.done(dve.reciprocal(dst[:], var[:]))
                st.wait()

            def variance(st, done):
                join_statistics(st)
                dve.tensor_scalar(var[:], variances, EPS, None, ALU.add).then_inc(s[done], 1)

            def normalise(src, dst, done):
                for t in range(T):
                    ins = dve.tensor_scalar(dst[:, t * D:(t + 1) * D], src[:, t * D:(t + 1) * D], means[:, t:t + 1],
                                            rstd[:, t:t + 1], ALU.subtract, ALU.mult)
                    if t % (T // 2) == T // 2 - 1:
                        ins.then_inc(s[done], 1)

            def top2(st, score, experts, rev, scale, eps, steps=range(ROUTES)):
                n = T * experts
                view = lambda k: small[:, k * T * E0:k * T * E0 + n].rearrange("p (t e) -> p t e", e=experts)
                eq, key, hot1, left = view(2), view(3), view(4), view(5)
                col = lambda k: tops[:, k * T:(k + 1) * T]
                wide = lambda c: c.unsqueeze(2).to_broadcast([P, T, experts])
                order = rev.unsqueeze(1).to_broadcast([P, T, experts])

                def best(src, value):
                    st.done(dve.tensor_reduce(value, src, AX_X, ALU.max))
                    st.wait()
                    st.done(dve.tensor_tensor(eq, src, wide(value), ALU.is_equal))
                    st.wait()
                    st.done(dve.tensor_tensor(key, eq, order, ALU.mult))

                def first_of_equals(hot):
                    st.done(dve.tensor_reduce(col(4), key, AX_X, ALU.max))
                    st.wait()
                    st.done(dve.tensor_tensor(hot, key, wide(col(4)), ALU.is_equal))

                for step in steps:
                    st.wait()
                    if step == 0:
                        best(score, col(2))
                    elif step == 1:
                        first_of_equals(hot1)
                        st.wait()
                        st.done(dve.scalar_tensor_tensor(left, hot1, -4.0, score, ALU.mult, ALU.add))
                    elif step == 2:
                        best(left, col(3))
                    elif step == 3:
                        first_of_equals(eq)
                        st.wait()
                        st.done(dve.tensor_tensor(hot1, hot1, eq, ALU.add))
                        st.done(dve.scalar_tensor_tensor(col(5), col(2), eps, col(3), ALU.add, ALU.add))
                        st.wait()
                        st.done(dve.tensor_tensor(key, hot1, score, ALU.mult))
                        st.done(dve.reciprocal(col(6), col(5)))
                    else:
                        st.done(dve.scalar_tensor_tensor(left, key, scale, wide(col(6)), ALU.mult, ALU.mult))
                        st.wait()
                        for part in range(PARTS):
                            dst = rt[:, :, part, 0:experts]
                            ins = dve.tensor_copy(dst, left)
                            if part == PARTS - 1:
                                ins.then_inc(s["route_ready"], 1)
                                break
                            st.done(ins)
                            st.wait()
                            st.done(dve.tensor_tensor(left, left, dst, ALU.subtract))
                            st.wait()

            def mixture(b, base, chunks, hid_rows, beside=None, first_half=None):
                route_steps = steps_of_routes(beside) if beside is not None else None
                for n in range(2 * chunks):
                    k = STEPS * b + base + n
                    m = hid_rows(n % chunks)
                    dve.wait_ge(s["sg_ready"], k + 1)
                    dve.tensor_tensor(gu[n % 2][0:m, :], sg[n % 2][0:m, :], ps[n % 2][0:m, HALF:], ALU.mult).then_inc(s["gu_ready"], 1)
                    if base + n >= 2:
                        dve.wait_ge(s["down_done"], k - 1)
                    dve.wait_ge(s["gu_ready"], k + 1)
                    dve.wait_ge(s["spread_psum"], k + 1)
                    dve.tensor_tensor(hid[n % 2][0:m, :], gu[n % 2][0:m, :], bank(SPREAD_BANK)[0:m, :], ALU.mult).then_inc(s["hid_ready"], 1)
                    if first_half is not None and n == chunks + 2:
                        first_half()
                    for stage in front_stages(n) if beside is not None else ():
                        if stage < FRONT:
                            front(beside, stage)
                        else:
                            front_routes(beside, stage - FRONT, route_steps)

            def front(b, stage):
                t, part = divmod(stage - TILES, 3)
                st = Steps(dve, s["front_steps"], b * FRONT_STEPS + (0 if stage == 0 else LN_STEPS if stage == 1 else LN_STEPS + 1 + max(t, 0)))
                if stage == 0:
                    dve.wait_ge(s["x_in"], 16 * b + 16)
                    half_statistics(st, x_b, 0)
                    half_statistics(st, x_b, 1)
                    variance(st, "var0_ready")
                    assert st.n == LN_STEPS, st.n
                elif stage == 1:
                    inverse_deviation(st, "std0_ready", b + 1)
                    normalise(x_b, xn0, "x_norm_ready")
                elif TILES <= stage < LOGITS and part == 0:
                    dve.wait_ge(s["s0_psum"], b * T + t + 1)
                    dve.tensor_reduce(nmax0[:, t:t + 1], ps[FRONT_PS][:, 0:(t + 1) * P], AX_X, ALU.max, negate=True).then_inc(s["max0_ready"], 1)
                elif TILES <= stage < LOGITS and part == 2:
                    dve.wait_ge(s["p0_ready"], b * T + t + 1)
                    st.done(dve.reciprocal(rsum[:, t:t + 1], sum0[:, t:t + 1]))
                    st.wait()
                    dve.wait_ge(s["o0_psum"], b * T + t + 1)
                    dve.scalar_tensor_tensor(x0[:, t * D:(t + 1) * D], ps[FRONT_PS][:, 0:D], rsum[:, t:t + 1],
                                             x_b[:, t * D:(t + 1) * D], ALU.mult, ALU.add).then_inc(s["o0_used"], 1)

            LN_STEPS = 14

            def front_routes(b, step, st):
                e0, score = small[:, 0:T * E0], small[:, T * E0:2 * T * E0]
                if step == 0:
                    dve.wait_ge(s["e_ready"], 2 * b + 1)
                    st.done(dve.tensor_scalar(e0, e0, 1.0, None, ALU.add))
                    st.wait()
                    st.done(dve.reciprocal(score, e0))
                top2(st, score.rearrange("p (t e) -> p t e", e=E0), E0, rev0, ROUTE_SCALE, ROUTE_EPS, [step])
                if step == ROUTES - 1:
                    assert LN_STEPS + 1 + T + st.n == FRONT_STEPS, LN_STEPS + 1 + T + st.n

            def steps_of_routes(b):
                return Steps(dve, s["front_steps"], b * FRONT_STEPS + LN_STEPS + 1 + T)

            def batch(b, last):
                st = Steps(dve, s["dve_steps"], b * DVE_STEPS)

                def left_of(kind, part):
                    n = 2 * b + kind
                    for u, (src, left, parts) in enumerate(splits(kind)):
                        dve.wait_ge(s["part_done"], 2 * (PARTS * n + part) + u + 1)
                        if part:
                            dve.wait_ge(s["left_done"], 2 * ((PARTS - 1) * n + part - 1) + u + 1)
                        dve.tensor_tensor(left, left if part else src, parts(part), ALU.subtract).then_inc(s["left_done"], 1)

                def piece(kind, g, i):
                    j, t, half, lo, hi = PIECES[kind][i]
                    dve.wait_ge(s["s_psum"], pieces_before(b, kind, g) + i + 1)
                    dve.tensor_reduce(nm[:, half, t, j:j + 1], piece_bank(kind, g, i)[0][:, 0:hi - lo],
                                      AX_X, ALU.max, negate=True).then_inc(s["max_done"], 1)

                nm = nmax[:].rearrange("p (h t j) -> p h t j", h=2, j=GH)

                def maxima(kind, g):
                    G = (2 * b + kind) * GROUPS + g
                    ms = Steps(dve, s["m_steps"], G * M_STEPS)
                    dve.wait_ge(s["max_done"], CREDIT + pieces_before(b, kind, g) + NP[kind])
                    m, r = nm[:, 0], m_rest[:].rearrange("p (t j) -> p t j", j=GH)
                    two = T // 2 if kind == 1 else 0
                    ms.done(dve.tensor_tensor(m[:, two:], m[:, two:], nm[:, 1, two:], ALU.min))
                    ms.wait()
                    ms.done(dve.tensor_copy(mp[:, :, :, 0], m))
                    ms.wait()
                    ms.done(dve.tensor_tensor(r, m, mp[:, :, :, 0], ALU.subtract))
                    ms.wait()
                    ms.done(dve.tensor_copy(mp[:, :, :, 1], r))
                    ms.wait()
                    ms.done(dve.tensor_tensor(r, r, mp[:, :, :, 1], ALU.subtract))
                    ms.wait()
                    assert ms.n == M_STEPS
                    dve.tensor_copy(mp[:, :, :, 2], r).then_inc(s["m_split"], 1)
                    dve.wait_ge(s["mt_psum"], G + 1)
                    dve.tensor_copy(mT[0:MR, :], piece_bank(kind, g, NP[kind])[0][0:MR, :].bitcast(BF16)).then_inc(s["mt_ready"], 1)

                def stack_keys(g, m):
                    dve.wait_ge(s["kc_psum"], (b * GROUPS + g) * TURNS + m + 1)
                    if m == 0:
                        dst, src = k_turn_c, side_bank(g, "k", m)[0:GR, :].bitcast(BF16)
                    else:
                        at = g * GH * S + (m - 1) * HALF
                        dst, src = kT[:, at:at + HALF], side_bank(g, "k", m)
                    dve.tensor_scalar(dst, src, 1.0, None, ALU.mult).then_inc(s["kc_ready"], 1)

                def beside(kind, g, step):
                    G = (2 * b + kind) * GROUPS + g
                    after, later = (kind, g + 1) if step < GROUPS - 1 else (1, 0)
                    for what, *how in sum(plan(kind, step), []):
                        if what == "piece":
                            piece(after, later, how[0])
                        elif what == "maxima":
                            maxima(after, later)
                        elif what == "stack" and how[2] == "k":
                            stack_keys(how[0], how[1])
                        elif what == "outputs" and how[0] == 1:
                            outputs(G - 1, *((g - 1, kind) if step > 0 else (GROUPS - 1, 0)))

                def attentions(following):
                    for i in range(NP[0]):
                        piece(0, 0, i)
                        if i in (8, 28):
                            left_of(1, (8, 28).index(i))
                    maxima(0, 0)
                    beside(0, 0, 0)
                    with dve.Fori(1, GROUPS - 1) as g:
                        beside(0, g, 1)
                    beside(0, GROUPS - 1, GROUPS - 1)
                    for g in range(GROUPS):
                        beside(1, g, g)
                    if following is not None:
                        front(following, 0)
                        front(following, 1)
                    outputs((2 * b + 2) * GROUPS - 1, GROUPS - 1, 1)

                def outputs(G, g, kind):
                    hd, dst = ((HD, heads_out), (HDC, heads_c))[kind]
                    dve.wait_ge(s["ot_psum"], G + 1)
                    o = bank(SIDE_BANK)[:, 0:T * OC].rearrange("p (t j c) -> p t j c", j=GH, c=HF)
                    inv = rsum_g[:].rearrange("p (t j) -> p t j", j=GH)
                    dve.reciprocal(inv, o[:, :, :, HD]).then_inc(s["rsum_done"], 1)
                    dve.wait_ge(s["rsum_done"], G + 1)
                    dst = tiles(dst)[:, :, bass.ds(g * GH * hd, GH * hd)].rearrange("p t (j d) -> p t j d", d=hd)
                    dve.tensor_tensor(dst, o[:, :, :, 0:hd], inv.unsqueeze(3).to_broadcast([P, T, GH, hd]), ALU.mult).then_inc(s["norm_done"], 1)

                def residual0(half):
                    tok = slice(half * HALF, (half + 1) * HALF)
                    dve.wait_ge(s["ytok_psum"], 3 * b + half + 1)
                    dve.wait_ge(s["o0_used"], b * T + T)
                    st.done(dve.tensor_tensor(x1[:, tok], x0[:, tok], ps[FRONT_PS][:, tok], ALU.add))
                    st.wait()
                    half_statistics(st, x1, half)

                mixture(b, 0, C0, lambda c: P if c < C0 - 1 else M0, first_half=lambda: residual0(0))
                residual0(1)
                variance(st, "var_ready")
                inverse_deviation(st, "std_ready", 3 * b + 1)
                normalise(x1, xn, "tok_ready")
                st.done(dve.tensor_tensor(var[:], rstd[:], rstd[:], ALU.mult))
                st.wait()
                st.done(dve.tensor_tensor(var[:], var[:], variances, ALU.mult))
                st.wait()
                dve.tensor_scalar(var[:], var[:], EPS, None, ALU.add).then_inc(s["var_ready"], 1)
                st.done(dve.memset(qp[:, :, :, HD:HF], 0.0))
                for t in range(T):
                    dve.wait_ge(s["qkv_psum"], T * b + t + 1)
                    for n, dst in enumerate((q_tok, k_tok, v_tok)):
                        ins = dve.scalar_tensor_tensor(dst[:, t * D:(t + 1) * D], bank(QKV_BANKS[t % len(QKV_BANKS)])[:, n * D:(n + 1) * D], scale4[:, n:n + 1],
                                                       bias4[:, n * D:(n + 1) * D], ALU.mult, ALU.add)
                    ins.then_inc(s["qkv_used"], 1)
                dve.wait_ge(s["qkv_used"], T * b + T)
                left_of(0, 0)
                left_of(0, 1)

                inverse_deviation(st, "std_ready", 3 * b + 2, rstd_c)
                dve.wait_ge(s["qkv_c_psum"], b + 1)
                st.done(dve.memset(qpc[:, :, :, HDC:HFC], 0.0))
                st.done(dve.memset(q_parts_c[:, PC:PC + GR - GRC], 0.0))
                st.done(dve.memset(k_parts_c[:, PC:PC + GR - GRC], 0.0))
                st.done(dve.memset(kpc[:, :, 0, HDC:HFC], 1.0))
                st.done(dve.memset(kpc[:, :, 1:, HDC:HFC], 0.0))
                for t in range(T):
                    src = bank(QKV_C_BANKS[t // 2])[:, t % 2 * 3 * L:(t % 2 + 1) * 3 * L]
                    st.done(dve.tensor_scalar(qk_c[:, t * 2 * L:(t + 1) * 2 * L], src[:, 0:2 * L], rstd_c[:, t:t + 1], None, ALU.mult))
                    st.done(dve.tensor_scalar(v_c[:, t * L:(t + 1) * L], src[:, 2 * L:3 * L], rstd_c[:, t:t + 1], None, ALU.mult))
                st.wait()
                pairs = qk_c.rearrange("p (t n f two) -> p t n f two", t=T, n=2 * HEADS, two=2)
                turned_pairs = turned.rearrange("p (t n f two) -> p t n f two", t=T, n=2 * HEADS, two=2)
                left4 = spin_a[:, 0:S // 2].rearrange("p (t n f) -> p t n f", t=T, f=2)
                right4 = spin_b[:, 0:S // 2].rearrange("p (t n f) -> p t n f", t=T, f=2)
                over = lambda c: c.unsqueeze(2).to_broadcast([P, T, 2 * HEADS, 2])
                for out_half, (first, second, op) in enumerate(((cos, sin, ALU.subtract), (sin, cos, ALU.add))):
                    st.done(dve.tensor_tensor(left4, pairs[:, :, :, :, 0], over(first), ALU.mult))
                    st.done(dve.tensor_tensor(right4, pairs[:, :, :, :, 1], over(second), ALU.mult))
                    st.wait()
                    ins = dve.tensor_tensor(turned_pairs[:, :, :, :, out_half], left4, right4, op)
                    if out_half == 0:
                        st.done(ins)
                        st.wait()
                ins.then_inc(s["turned_ready"], 1)
                attentions(None if last else b + 1)
                if not last:
                    front(b + 1, 4)
                dve.wait_ge(s["proj_psum"], 2 * b + 2)
                dve.wait_ge(s["out_stored"], 16 * b + 16)
                st.done(dve.tensor_tensor(res[:], xn[:], ps[1][:], ALU.add))
                if not last:
                    front(b + 1, 6)
                st.wait()
                statistics(st, res)
                st.done(dve.tensor_tensor(var[:], means, means, ALU.mult))
                st.wait()
                dve.scalar_tensor_tensor(var[:], var[:], EPS, variances, ALU.add, ALU.add).then_inc(s["var_ready"], 1)
                if not last:
                    front(b + 1, 7)
                inverse_deviation(st, "std_ready", 3 * b + 3)
                for t in range(T):
                    ins = dve.scalar_tensor_tensor(q_tok[:, t * D:(t + 1) * D], res[:, t * D:(t + 1) * D], rstd[:, t:t + 1], g2[:],
                                                   ALU.mult, ALU.mult)
                    if t % (T // 2) == T // 2 - 1:
                        ins.then_inc(s["tok_ready"], 1)
                st.done(dve.scalar_tensor_tensor(x1[:], ps[2][:], scale4[:, 3:4], x1[:], ALU.mult, ALU.add))
                st.wait()
                st.done(dve.tensor_tensor(tiles(x1[:]), tiles(x1[:]), bias4[:, 3 * D:4 * D].unsqueeze(1).to_broadcast([P, T, D]), ALU.add))
                st.wait()
                st.done(dve.tensor_tensor(x1[:], x1[:], res[:], ALU.add))
                z = small[:, 0:T * E1].rearrange("p (t e) -> p t e", e=E1)
                prob = small[:, T * E0:T * E0 + T * E1].rearrange("p (t e) -> p t e", e=E1)
                wide1 = lambda c: c.unsqueeze(2).to_broadcast([P, T, E1])
                logits = bank(LOGIT_BANK)[:, 0:T * E1].rearrange("p (t e) -> p t e", e=E1)
                dve.wait_ge(s["logit_psum"], 2 * b + 2)
                st.done(dve.tensor_reduce(tops[:, 0:T], logits, AX_X, ALU.max))
                st.wait()
                dve.tensor_tensor(z, logits, wide1(tops[:, 0:T]), ALU.subtract).then_inc(s["shift1_ready"], 1)
                dve.wait_ge(s["e_ready"], 2 * b + 2)
                st.done(dve.tensor_reduce(tops[:, T:2 * T], z, AX_X, ALU.add))
                st.wait()
                st.done(dve.reciprocal(tops[:, 0:T], tops[:, T:2 * T]))
                st.wait()
                st.done(dve.tensor_tensor(prob, z, wide1(tops[:, 0:T]), ALU.mult))
                st.wait()
                top2(st, prob, E1, rev1, 1.0, 0.0)
                if not last:
                    front(b + 1, 9)
                mixture(b, 2 * C0, C1, lambda c: P, None if last else b + 1)
                dve.wait_ge(s["ytok_psum"], 3 * b + 3)
                dve.tensor_tensor(res[:], x1[:], ps[1][:], ALU.add).then_inc(s["out_ready"], 1)
                assert st.n == DVE_STEPS, st.n

            for stage in range(LOGITS):
                front(0, stage)
            route_steps = steps_of_routes(0)
            for step in range(ROUTES):
                front_routes(0, step, route_steps)
            dve.wait_ge(s["weights_in"], 16 * N_WEIGHTS)
            dve.tensor_scalar(w_down[:], w_down[:], g1[:, 0:1], None, ALU.mult).then_inc(s["setup_done"], 1)
            with dve.Fori(0, B - 1) as b:
                batch(b, False)
            batch(B - 1, True)

        @block.scalar
        def _(act):
            act.wait_ge(s["first_in"], 16 * N_FIRST)

            def root(b, n):
                act.wait_ge(s["var_ready"], 3 * b + n + 1)
                act.activation(var[:], var[:], ACT.Sqrt).then_inc(s["std_ready"], 1)

            def evacuate(b, n, dst, rows=P):
                for half in range(2):
                    tok = slice(half * HALF, (half + 1) * HALF)
                    act.wait_ge(s["tokT_psum"], 8 * b + 2 * n + half + 1)
                    act.activation(dst[0:rows, tok], ps[0][0:rows, tok], ACT.Copy).then_inc(s["tokT_ready"], 1)

            def front(b, stage):
                t, part = divmod(stage - TILES, 3)
                keys = (t + 1) * P
                if stage == 1:
                    act.wait_ge(s["var0_ready"], b + 1)
                    act.activation(var[:], var[:], ACT.Sqrt).then_inc(s["std0_ready"], 1)
                elif stage == TURN_X:
                    for half in range(2):
                        tok = slice(half * HALF, (half + 1) * HALF)
                        act.wait_ge(s["xT_psum"], 2 * b + half + 1)
                        act.activation(xnT[:, tok], ps[FRONT_PS][:, tok], ACT.Copy).then_inc(s["xT_ready"], 1)
                elif stage == ENCODE:
                    act.wait_ge(s["encr_psum"], b + 1)
                    act.activation(encR, ps[FRONT_PS][:], ACT.Copy).then_inc(s["encr_ready"], 1)
                elif stage == LOGITS:
                    act.wait_ge(s["logit_psum"], 2 * b + 1)
                    act.activation(small[:, 0:T * E0], ps[FRONT_PS][:, 0:T * E0], ACT.Exp, scale=-1.0).then_inc(s["e_ready"], 1)
                elif stage >= TILES and part == 0:
                    act.wait_ge(s["max0_ready"], b * T + t + 1)
                    act.activation(p0[t % 2][:, 0:keys], ps[FRONT_PS][:, 0:keys], ACT.Exp, bias=nmax0[:, t:t + 1],
                                   accum_out=sum0[:, t:t + 1]).then_inc(s["p0_ready"], 1)
                elif stage >= TILES and part == 1:
                    act.wait_ge(s["pt_psum"], b * T + t + 1)
                    act.activation(pT0[:, 0:keys], ps[FRONT_PS][:, 0:keys], ACT.Copy).then_inc(s["pt_ready"], 1)

            def mixture(b, which, base, chunks, hid_rows, beside=None):
                for n in range(2 * chunks):
                    m = hid_rows(n % chunks)
                    act.wait_ge(s["gu_psum"], STEPS * b + base + n + 1)
                    act.activation(sg[n % 2][0:m, :], ps[n % 2][0:m, 0:HALF], ACT.Silu).then_inc(s["sg_ready"], 1)
                    if n == 0:
                        routes_out(b, which)
                    if n == chunks:
                        leave(b, which, 0)
                    for stage in front_stages(n) if beside is not None else ():
                        if stage < FRONT:
                            front(beside, stage)
                leave(b, which, 1)

            def leave(b, which, half):
                act.wait_ge(s["down_done"], STEPS * b + (half + 1) * (C0, C1)[which] + (0, 2 * C0)[which])
                act.activation(yT[:, half * HALF:(half + 1) * HALF], bank(Y_BANK), ACT.Copy).then_inc(s["y_ready"], 1)

            def routes_out(b, n):
                act.wait_ge(s["rt_psum"], 2 * b + n + 1)
                act.activation(routeT[0:PARTS * CW, :], bank(SPREAD_BANK)[0:PARTS * CW, :].bitcast(BF16), ACT.Copy).then_inc(s["rt_ready"], 1)

            def batch(b, last):
                def part_of(kind, part):
                    n = 2 * b + kind
                    if part == 0:
                        act.wait_ge(s[("qkv_used", "turned_ready")[kind]], (b + 1) * (T, 1)[kind])
                    for u, (src, left, parts) in enumerate(splits(kind)):
                        if part:
                            act.wait_ge(s["left_done"], 2 * ((PARTS - 1) * n + part - 1) + u + 1)
                        act.activation(parts(part), left if part else src, ACT.Copy).then_inc(s["part_done"], 1)

                def stacks(g):
                    for n in range(2 + 2 * GH):
                        act.wait_ge(s["stack_psum"], (b * GROUPS + g) * (2 + 2 * GH) + n + 1)
                        src = ps[n % 2 * 2]
                        if n < 2:
                            act.activation((q_turn, k_turn)[n], src[0:GR, 0:HALF].bitcast(BF16), ACT.Copy).then_inc(s["stack_ready"], 1)
                        else:
                            act.activation((qT, kT)[n % 2][:, bass.ds((g * GH + n // 2 - 1) * S, S)], src[:],
                                           ACT.Copy).then_inc(s["stack_ready"], 1)

                def stack_queries(g, m):
                    act.wait_ge(s["qc_psum"], (b * GROUPS + g) * TURNS + m + 1)
                    if m == 0:
                        dst, src = q_turn_c, side_bank(g, "q", m)[0:GR, :].bitcast(BF16)
                    else:
                        at = g * GH * S + (m - 1) * HALF
                        dst, src = qT[:, at:at + HALF], side_bank(g, "q", m)
                    act.activation(dst, src, ACT.Copy).then_inc(s["qc_ready"], 1)

                def outputs(G):
                    act.wait_ge(s["pv_done"], CREDIT + (G + 1) * T)
                    act.activation(o_sb[:], ps[2][:], ACT.Copy).then_inc(s["o_evac"], 1)

                def group(kind, g, step):
                    G = (2 * b + kind) * GROUPS + g
                    first = (b * GROUPS + g) * NU[kind]
                    todo = plan(kind, step)
                    banks = banks_of_units(kind, step == GROUPS - 1)
                    for i, (kc, j, lo, hi) in enumerate(UNITS[kind]):
                        for what, *how in todo[i]:
                            if what == "stack" and how[2] == "q":
                                stack_queries(how[0], how[1])
                            elif what == "outputs" and how[0] == 0:
                                outputs(G - 1)
                        act.wait_ge(s[ST_PSUM[kind]], first + i + 1)
                        if (kind, step, i) == (1, GROUPS - 1, NU[1] // 3) and not last:
                            front(b + 1, 1)
                        if j == 0:
                            act.wait_ge(s["pv_done"], CREDIT + G * T + kc - 1)
                        act.activation(slot(kc % 2 * GH + j)[:, lo:hi], bank(banks[i % len(banks)])[:, 0:hi - lo], ACT.Exp,
                                       scale=SCALES[kind]).then_inc(s[P_READY[kind]], 1)

                SCALES = float(1.0 / np.sqrt(np.float32(HD))), float(1.0 / np.sqrt(np.float32(HDC)))

                def attentions():
                    group(0, 0, 0)
                    with act.Fori(1, GROUPS - 1) as g:
                        group(0, g, 1)
                    group(0, GROUPS - 1, GROUPS - 1)
                    for g in range(GROUPS):
                        group(1, g, g)
                    outputs((2 * b + 2) * GROUPS - 1)

                mixture(b, 0, 0, C0, lambda c: P if c < C0 - 1 else M0)
                root(b, 0)
                root(b, 1)
                evacuate(b, 0, xnT)
                act.wait_ge(s["ct_psum"], b + 1)
                act.activation(cT[0:L, :], ps[2][0:L, :], ACT.Copy).then_inc(s["ct_ready"], 1)
                for part in range(PARTS):
                    part_of(0, part)
                stacks(0)
                for g in range(1, GROUPS):
                    part_of(1, g - 1)
                    stacks(g)
                attentions()
                evacuate(b, 1, heads_outT)
                if not last:
                    front(b + 1, 2)
                    front(b + 1, 3)
                evacuate(b, 2, heads_cT, L)
                if not last:
                    front(b + 1, 4)
                    front(b + 1, 5)
                root(b, 2)
                if not last:
                    front(b + 1, 7)
                evacuate(b, 3, tT)
                if not last:
                    front(b + 1, 8)
                act.wait_ge(s["shift1_ready"], b + 1)
                act.activation(small[:, 0:T * E1], small[:, 0:T * E1], ACT.Exp).then_inc(s["e_ready"], 1)
                mixture(b, 1, 2 * C0, C1, lambda c: P, None if last else b + 1)

            for stage in range(FRONT):
                front(0, stage)
            with act.Fori(0, B - 1) as b:
                batch(b, False)
            batch(B - 1, True)

        @block.tensor
        def _(pe):
            pe.wait_ge(s["first_in"], 16 * N_FIRST)
            pe.wait_ge(s["setup_done"], 2)

            def turn(src, width=D, dst=ps[0], done="tokT_psum", ready=None, count=0):
                for t in range(T):
                    if ready is not None and t % (T // 2) == 0:
                        pe.wait_ge(s[ready], count + t * 2 // T + 1)
                    to, tile = dst[0:width, t * P:(t + 1) * P], src[:, t * width:(t + 1) * width]
                    ins = pe.transpose(to, tile, ident_f) if width == D else pe.matmul(to, tile, ident_f, start=True, stop=True)
                    if t % (T // 2) == T // 2 - 1:
                        ins.then_inc(s[done], 1)

            def front(b, stage):
                t, part = divmod(stage - TILES, 3)
                to, keys = ps[FRONT_PS], (t + 1) * P
                if stage == TURN_X:
                    turn(xn0, D, to, "xT_psum", "x_norm_ready", 2 * b)
                elif stage == ENCODE:
                    for half in range(2):
                        pe.wait_ge(s["xT_ready"], 2 * b + half + 1)
                        ins = pe.matmul(to[:, half * HALF:(half + 1) * HALF], R_w[:], xnT[:, half * HALF:(half + 1) * HALF], start=True, stop=True)
                    ins.then_inc(s["encr_psum"], 1)
                elif stage == LOGITS:
                    pe.wait_ge(s["o0_used"], b * T + T)
                    for tile in range(T):
                        ins = pe.matmul(to[:, tile * E0:(tile + 1) * E0], xnT[:, tile * P:(tile + 1) * P], gate0[:], start=True, stop=True)
                    ins.then_inc(s["logit_psum"], 1)
                elif stage >= TILES and part == 0:
                    if t == 0:
                        pe.wait_ge(s["encr_ready"], b + 1)
                    else:
                        pe.wait_ge(s["o0_used"], b * T + t)
                    for lo in range(0, keys, HALF):
                        hi = min(keys, lo + HALF)
                        pe.matmul(to[:, lo:hi], encR[:, t * P:(t + 1) * P], xnT[:, lo:hi], start=True, stop=True)
                    pe.matmul(to[:, t * P:keys], ident_b, mask_q, start=False, stop=True, skip_group_check=True).then_inc(s["s0_psum"], 1)
                elif stage >= TILES and part == 1:
                    pe.wait_ge(s["p0_ready"], b * T + t + 1)
                    for j in range(t + 1):
                        ins = pe.transpose(to[:, j * P:(j + 1) * P], p0[t % 2][:, j * P:(j + 1) * P], ident_f)
                    ins.then_inc(s["pt_psum"], 1)
                elif stage >= TILES:
                    pe.wait_ge(s["pt_ready"], b * T + t + 1)
                    for j in range(t + 1):
                        ins = pe.matmul(to[:, 0:D], pT0[:, j * P:(j + 1) * P], xn0[:, j * D:(j + 1) * D], start=j == 0, stop=j == t)
                    ins.then_inc(s["o0_psum"], 1)

            def routes_in(b, n):
                pe.wait_ge(s["route_ready"], 2 * b + n + 1)
                dst = bank(SPREAD_BANK).bitcast(BF16)
                for t in range(T):
                    ins = pe.transpose(dst[0:PARTS * CW, t * P:(t + 1) * P], routes[:, t * PARTS * CW:(t + 1) * PARTS * CW], ident_b)
                ins.then_inc(s["rt_psum"], 1)
                pe.wait_ge(s["rt_ready"], 2 * b + n + 1)

            def mixture(b, which, base, chunks, hid_rows, wg, wu, wd, spread, xT, beside=None):
                def down(n):
                    half, c = n // chunks, n % chunks
                    m = hid_rows(c)
                    if c == 0 and half == 1:
                        pe.wait_ge(s["y_ready"], 4 * b + 2 * which + 1)
                    pe.wait_ge(s["hid_ready"], STEPS * b + base + n + 1)
                    pe.matmul(bank(Y_BANK), wd[0:m, c * D:(c + 1) * D], hid[n % 2][0:m, :],
                              start=c == 0, stop=c == chunks - 1).then_inc(s["down_done"], 1)

                def back(first, end):
                    pe.wait_ge(s["y_ready"], 4 * b + 2 * which + end * 2 // T)
                    for t in range(first, end):
                        ins = pe.transpose(ps[(FRONT_PS, 1)[which]][:, t * P:(t + 1) * P], yT[:, t * P:(t + 1) * P], ident_f)
                    ins.then_inc(s["ytok_psum"], 1)

                for n in range(2 * chunks):
                    half, c = n // chunks, n % chunks
                    m = hid_rows(c)
                    tok = slice(half * HALF, (half + 1) * HALF)
                    if n == 1 and which == 0:
                        pe.wait_ge(s["out_ready"], CREDIT + b)
                    pe.matmul(ps[n % 2][0:m, 0:HALF], wg[:, c * P:c * P + m], xT[:, tok], start=True, stop=True)
                    pe.matmul(ps[n % 2][0:m, HALF:], wu[:, c * P:c * P + m], xT[:, tok], start=True, stop=True).then_inc(s["gu_psum"], 1)
                    if n == 0:
                        routes_in(b, which)
                    for stage in front_stages(n) if beside is not None else ():
                        if stage < FRONT:
                            front(beside, stage)
                    if n >= 1:
                        down(n - 1)
                    pe.matmul(bank(SPREAD_BANK)[0:m, :], spread(c, m), routeT[0:PARTS * CW, tok], start=True, stop=True).then_inc(s["spread_psum"], 1)
                    if which == 0 and n == chunks + 1:
                        back(0, T // 2)
                down(2 * chunks - 1)
                back(T // 2 if which == 0 else 0, T)

            def batch(b, last):
                def turn_parts(parts, g, rows, dst):
                    for t in range(T):
                        at = (t * GROUPS + g) * rows
                        ins = pe.transpose(dst[0:GR, t * P:(t + 1) * P], parts[:, at:at + GR], ident_b)
                    return ins

                def stacks(g, n):
                    pe.wait_ge(s["stack_ready"], (b * GROUPS + g) * (2 + 2 * GH) + n - 1 + CREDIT)
                    dst = ps[n % 2 * 2]
                    if n < 2:
                        ins = turn_parts((q_parts, k_parts)[n], g, GR, dst[:, 0:HALF].bitcast(BF16))
                    else:
                        j = n // 2 - 1
                        for half in range(2):
                            ins = pe.matmul(dst[:, half * HALF:(half + 1) * HALF], (pick_q, pick_k)[n % 2][0:GR, j * P:(j + 1) * P],
                                            (q_turn, k_turn)[n % 2][:, half * HALF:(half + 1) * HALF], start=True, stop=True)
                    ins.then_inc(s["stack_psum"], 1)

                def stacks_c(g, m, side):
                    count = (b * GROUPS + g) * TURNS + m
                    late = 1 if g == 0 and m >= 2 else 0
                    if side == "q":
                        if m >= 1 or g >= 1:
                            pe.wait_ge(s["qc_ready"], count - late)
                        if g >= 1:
                            pe.wait_ge(s["kc_ready"], count + CREDIT)
                        parts, pick, turned_parts, done = q_parts_c, pick_qc, q_turn_c, "qc_psum"
                    else:
                        if g >= 1:
                            pe.wait_ge(s["qc_ready"], count + 1)
                        else:
                            pe.wait_ge(s["kc_ready"], count - late + CREDIT)
                        parts, pick, turned_parts, done = k_parts_c, pick_kc, k_turn_c, "kc_psum"
                    if m == 0:
                        ins = turn_parts(parts, g, GRC, side_bank(g, side, m).bitcast(BF16))
                    else:
                        j, half = (m - 1) // 2, (m - 1) % 2
                        ins = pe.matmul(side_bank(g, side, m), pick[0:GR, j * P:(j + 1) * P],
                                        turned_parts[:, half * HALF:(half + 1) * HALF], start=True, stop=True)
                    ins.then_inc(s[done], 1)

                def head(stacked, g, j):
                    return stacked[:, bass.ds((g * GH + j) * S, S)]

                def piece(kind, g, i):
                    j, t, half, lo, hi = PIECES[kind][i]
                    n = hi - lo
                    dst, gone = piece_bank(kind, g, i)
                    if i >= gone and not (kind == 0 and i == EARLY):
                        pe.wait_ge(s["max_done"], CREDIT + pieces_before(b, kind, g) + i - gone + 1)
                    ins = pe.matmul(dst[:, 0:n], head(qT, g, j)[:, t * P:(t + 1) * P], head(kT, g, j)[:, lo:hi], start=True, stop=True)
                    if kind == 1 and hi == (t + 1) * P:
                        ins = pe.matmul(dst[:, n - P:n], ident_b, mask_q, start=False, stop=True, skip_group_check=True)
                    ins.then_inc(s["s_psum"], 1)

                def maxima(kind, g):
                    pe.wait_ge(s["m_split"], (2 * b + kind) * GROUPS + g + 1)
                    dst = piece_bank(kind, g, NP[kind])[0][0:MR, :].bitcast(BF16)
                    for t in range(T):
                        ins = pe.transpose(dst[:, t * P:(t + 1) * P], m_parts[:, t * MR:(t + 1) * MR], ident_b)
                    ins.then_inc(s["mt_psum"], 1)

                def scores(kind, g, i, banks):
                    kc, j, lo, hi = UNITS[kind][i]
                    dst = bank(banks[i % len(banks)])
                    if i >= len(banks):
                        pe.wait_ge(s[P_READY[kind]], (b * GROUPS + g) * NU[kind] + i - len(banks) + 1)
                    ins = pe.matmul(dst[:, 0:hi - lo], head(kT, g, j)[:, kc * P:(kc + 1) * P], head(qT, g, j)[:, lo:hi], start=True, stop=True)
                    if kind == 1 and lo == kc * P:
                        ins = pe.matmul(dst[:, 0:P], ident_b, mask_k, start=False, stop=True, skip_group_check=True)
                    ins.then_inc(s[ST_PSUM[kind]], 1)

                def values(kind, g, kc, half):
                    lo, hi = max(kc * P if kind == 1 else 0, half * HALF), (half + 1) * HALF
                    if lo >= hi:
                        return
                    if kc == 0 and half == 0:
                        pe.wait_ge(s["v_staged"], (2 * b + kind) * GROUPS + g + 1)
                    done = sum(unit[0] <= kc for unit in UNITS[kind])
                    pe.wait_ge(s[P_READY[kind]], (b * GROUPS + g) * NU[kind] + done)
                    for j in range(GH):
                        ins = pe.matmul(ps[2][CW * j:CW * (j + 1), lo:hi], v_st[:, kc, j, :], slot(kc % 2 * GH + j)[:, lo:hi],
                                        start=kc == 0, stop=kc == T - 1, skip_group_check=True)
                    if half == 1:
                        ins.then_inc(s["pv_done"], 1)

                def outputs(G, half):
                    if half == 0:
                        pe.wait_ge(s["norm_done"], CREDIT + G)
                        pe.wait_ge(s["o_evac"], G + 1)
                    for t in range(half * T // 2, (half + 1) * T // 2):
                        ins = pe.matmul(bank(SIDE_BANK)[:, OC * t:OC * (t + 1)], o_sb[:, t * P:(t + 1) * P], pick_o, start=True, stop=True)
                    if half == 1:
                        ins.then_inc(s["ot_psum"], 1)

                def group(kind, g, step):
                    G = (2 * b + kind) * GROUPS + g
                    after, later = (kind, g + 1) if step < GROUPS - 1 else (1, 0)
                    before = (kind, g - 1) if step > 0 else (0, GROUPS - 1)
                    todo = plan(kind, step)
                    banks = banks_of_units(kind, step == GROUPS - 1)
                    for i in range(NU[kind] + 1):
                        if i == 1:
                            pe.wait_ge(s["m_rows"], 16 * GH * (G + 1))
                            if (kind, step) == (0, GROUPS - 1):
                                pe.wait_ge(s["qc_ready"], b * GROUPS * TURNS + TURNS)
                                pe.wait_ge(s["kc_ready"], b * GROUPS * TURNS + TURNS + CREDIT)
                        if i >= 1:
                            kc, j, lo, hi = UNITS[kind][i - 1]
                            scores(kind, g, i - 1, banks)
                            if kc >= 1 and hi == S and j % 2 == 1:
                                values(kind, g, kc - 1, j // 2)
                        for what, *how in todo[i]:
                            if what == "values":
                                values(*before, T - 1, how[0])
                            elif what == "outputs":
                                outputs(G - 1, how[0])
                            elif what == "stack":
                                if how[1:] == [0, "q"] and how[0] > 0:
                                    pe.wait_ge(s["norm_done"], CREDIT + G)
                                if how == [0, 1, "k"]:
                                    pe.wait_ge(s["mt_ready"], G + 1)
                                stacks_c(*how)
                            elif what == "piece":
                                if how[0] == 0:
                                    pe.wait_ge(s["mt_ready"], G + 1)
                                if how[0] == 0 and after == 1:
                                    pe.wait_ge(s["qc_ready"], (b * GROUPS + later + 1) * TURNS)
                                    pe.wait_ge(s["kc_ready"], (b * GROUPS + later + 1) * TURNS + CREDIT)
                                if how[0] == EARLY and after == 0 and step > 0:
                                    pe.wait_ge(s["norm_done"], CREDIT + G)
                                piece(after, later, how[0])
                            else:
                                maxima(after, later)

                def attentions():
                    pe.wait_ge(s["part_done"], 2 * PARTS * (2 * b + 1))
                    each = 2 + 2 * GH
                    out = 8
                    for n in range(out):
                        stacks(0, n)
                    pe.wait_ge(s["turned_ready"], b + 1)
                    for i in range(NP[0]):
                        j = PIECES[0][i][0]
                        if i == 0 or PIECES[0][i - 1][0] < j:
                            pe.wait_ge(s["stack_ready"], CREDIT + b * GROUPS * each + 2 * j + 4)
                        piece(0, 0, i)
                        while out - 8 < (GROUPS * each - 8) * (i + 1) // NP[0]:
                            stacks(out // each, out % each)
                            out += 1
                    maxima(0, 0)
                    pe.wait_ge(s["stack_ready"], CREDIT + (b + 1) * GROUPS * each)
                    pe.wait_ge(s["part_done"], 2 * PARTS * (2 * b + 2))
                    group(0, 0, 0)
                    with pe.Fori(1, GROUPS - 1) as g:
                        group(0, g, 1)
                    group(0, GROUPS - 1, GROUPS - 1)
                    for g in range(GROUPS):
                        group(1, g, g)
                    values(1, GROUPS - 1, T - 1, 0)
                    values(1, GROUPS - 1, T - 1, 1)

                mixture(b, 0, 0, C0, lambda c: P if c < C0 - 1 else M0, wg0, wu0, wd0,
                        lambda c, m: sel0[0:PARTS * CW, c * P:c * P + m], xnT)
                def turned_tile(n, t):
                    if t % (T // 2) == 0:
                        pe.wait_ge(s["tokT_ready"], 8 * b + 2 * n + t * 2 // T + 1)

                turn(xn, ready="tok_ready", count=4 * b)
                for t in range(T):
                    if t < 2:
                        pe.wait_ge(s["tokT_ready"], 8 * b + t + 1)
                    if t >= len(QKV_BANKS):
                        pe.wait_ge(s["qkv_used"], T * b + t - len(QKV_BANKS) + 1)
                    pe.matmul(bank(QKV_BANKS[t % len(QKV_BANKS)])[:, 0:3 * D], xnT[:, t * P:(t + 1) * P], wqkv[:], start=True, stop=True).then_inc(s["qkv_psum"], 1)
                    if t == 1:
                        for half in range(2):
                            ins = pe.matmul(ps[2][0:L, half * HALF:(half + 1) * HALF], w_down[:], xnT[:, half * HALF:(half + 1) * HALF],
                                            start=True, stop=True)
                        ins.then_inc(s["ct_psum"], 1)
                pe.wait_ge(s["ct_ready"], b + 1)
                pe.wait_ge(s["qkv_used"], T * b + T)
                for t in range(T):
                    ins = pe.matmul(bank(QKV_C_BANKS[t // 2])[:, t % 2 * 3 * L:(t % 2 + 1) * 3 * L], cT[0:L, t * P:(t + 1) * P], wqkv1[0:L, :],
                                    start=True, stop=True)
                ins.then_inc(s["qkv_c_psum"], 1)
                attentions()
                turn(heads_out)
                if not last:
                    front(b + 1, 2)
                outputs((2 * b + 2) * GROUPS - 1, 0)
                outputs((2 * b + 2) * GROUPS - 1, 1)
                for t in range(T):
                    turned_tile(1, t)
                    ins = pe.matmul(ps[2][:, t * D:(t + 1) * D], heads_outT[:, t * P:(t + 1) * P], wo[:], start=True, stop=True)
                ins.then_inc(s["proj_psum"], 1)
                if not last:
                    front(b + 1, 3)
                pe.wait_ge(s["norm_done"], CREDIT + (2 * b + 2) * GROUPS)
                turn(heads_c, L)
                if not last:
                    front(b + 1, 4)
                for t in range(T):
                    turned_tile(2, t)
                    ins = pe.matmul(ps[1][:, t * D:(t + 1) * D], heads_cT[:, t * P:(t + 1) * P], w_up[0:L, :], start=True, stop=True)
                ins.then_inc(s["proj_psum"], 1)
                if not last:
                    for stage in (5, 6, 7):
                        front(b + 1, stage)
                turn(q_tok, ready="tok_ready", count=4 * b + 2)
                if not last:
                    front(b + 1, 8)
                for t in range(T):
                    turned_tile(3, t)
                    ins = pe.matmul(bank(LOGIT_BANK)[:, t * E1:(t + 1) * E1], tT[:, t * P:(t + 1) * P], router[:], start=True, stop=True)
                ins.then_inc(s["logit_psum"], 1)
                if not last:
                    front(b + 1, 9)
                mixture(b, 1, 2 * C0, C1, lambda c: P, wg1, wu1, wd1, lambda c, m: sel1[0:PARTS * CW, (c // 2) * P:(c // 2) * P + m], tT,
                        None if last else b + 1)

            for stage in range(FRONT):
                front(0, stage)
            pe.wait_ge(s["weights_in"], 16 * N_WEIGHTS)
            pe.wait_ge(s["setup_done"], 3)
            with pe.Fori(0, B - 1) as b:
                batch(b, False)
            batch(B - 1, True)


def kernel(**inputs):
    import ml_dtypes
    import concourse.bacc as bacc
    from concourse.bass_utils import run_bass_kernel_spmd as run

    i = {k: np.asarray(v) for k, v in inputs.items()}
    cb, cf = constants()
    side = lambda w: w.transpose(1, 0, 2).reshape(w.shape[1], -1)
    rows = lambda w: w.reshape(-1, P, D).transpose(1, 0, 2).reshape(P, -1)
    a = {
        "const_b": cb.astype(ml_dtypes.bfloat16), "const_f": cf,
        "x": i["L0_attn_encoding"], "R": i["L0_attn_R"], "gate0": i["L0_ffn_gate_w"].T,
        "wg0": np.concatenate([side(i["L0_ffn_w_gate"]), i["L0_ffn_ws_gate"]], axis=1),
        "wu0": np.concatenate([side(i["L0_ffn_w_up"]), i["L0_ffn_ws_up"]], axis=1),
        "wd0a": rows(i["L0_ffn_w_down"].reshape(-1, D)), "wd0b": i["L0_ffn_ws_down"],
        "wqkv": np.concatenate([i[f"L1_attn_w_{n}"].T for n in "qkv"], axis=1), "wo": i["L1_attn_w_o"].T,
        "scale4": np.stack([i[f"L1_attn_s_{n}"].reshape(()) for n in "qkvo"]),
        "bias4": np.concatenate([i[f"L1_attn_b_{n}"] for n in "qkvo"]),
        "g1": i["L1_ffn_g1"].reshape(D, 1), "g2": i["L1_ffn_g2"],
        "w_down": i["L1_ffn_w_down"], "wqkv1": np.concatenate([i[f"L1_ffn_w{n}"] for n in "qkv"], axis=1),
        "w_up": i["L1_ffn_w_up"], "router": i["L1_ffn_router_w"],
        "wg1": side(i["L1_ffn_w1"]), "wu1": side(i["L1_ffn_w3"]), "wd1": rows(i["L1_ffn_w2"].reshape(-1, D)),
    }
    nc = bacc.Bacc("TRN2", target_bir_lowering=False, num_devices=1)
    arrays, h = {}, {}
    for name, v in a.items():
        v = np.ascontiguousarray(v)
        arrays[f"in_{name}"] = v
        h[name] = nc.dram_tensor(f"in_{name}", v.shape, mybir.dt.from_np(v.dtype), kind="ExternalInput").ap()
    h["out"] = nc.dram_tensor("out_0", (B, S, D), F32, kind="ExternalOutput").ap()
    build(nc, h)
    r = run(nc, [arrays], core_ids=[0])
    return r.results[0]["out_0"]
```
